# Optimizing a Trainium2 kernel written in Bass

```python
import numpy as np
import jax
import jax.numpy as jnp

def _softmax(x, axis=-1):
    return jax.nn.softmax(x, axis=axis)

def _gelu(x):
    return jax.nn.gelu(x, approximate=True)

def _silu(x):
    return jax.nn.silu(x)

def _sigmoid(x):
    return jax.nn.sigmoid(x)

def _layernorm(x, axis=-1, eps=1e-05):
    m = jnp.mean(x, axis=axis, keepdims=True)
    v = jnp.var(x, axis=axis, keepdims=True)
    return (x - m) / jnp.sqrt(v + eps)

def _scatter_add(tgt, idx, src, axis=0):
    return tgt.at[idx].add(src)

def _segment_sum(src, seg, n):
    return jax.ops.segment_sum(src, seg, n)
kernel_name = 'mk_pixart_seq_d1_seqx_r4_4d4d7d'

def setup_inputs(seed: int=0):
    np.random.seed(seed)
    _w = jnp.asarray

    def _rec_inputs():
        import jax
        import jax.numpy as jnp
        _rk = jax.random.key(seed)
        x = -0.0005207 + 1.001 * jax.random.normal(jax.random.fold_in(_rk, 1), (4, 1024, 256), jnp.float32)
        _lenS = 1024 - jax.random.randint(jax.random.fold_in(_rk, 7), (4,), 0, max(1, 1024 // 4) + 1, jnp.int32)
        _lenS2 = 77 - jax.random.randint(jax.random.fold_in(_rk, 8), (4,), 0, max(1, 77 // 4) + 1, jnp.int32)
        cond_1024 = 0.000887014 + 1.03683 * jax.random.normal(jax.random.fold_in(_rk, 11), (4, 256), jnp.float32)
        _ctx_768P = jax.random.normal(jax.random.fold_in(_rk, 12), (4, 16, 192), jnp.float32)
        _ctx_768c = jax.random.dirichlet(jax.random.fold_in(_rk, 512), 0.3 * jnp.ones((16,), jnp.float32), (4, 77))
        _ctx_768t = jnp.einsum('bsk,bkd->bsd', _ctx_768c, _ctx_768P)
        _ctx_768t = _ctx_768t * jax.lax.rsqrt(jnp.mean(jnp.square(_ctx_768t)) + 1e-12) * 0.953939
        ctx_768 = 0.000599585 + 1.00006 * (_ctx_768t + 0.3 * jax.random.normal(jax.random.fold_in(_rk, 612), (4, 77, 192), jnp.float32))
        return (x, cond_1024, ctx_768)
    x, cond_1024, ctx_768 = _rec_inputs()

    def _L0_xcond_setup():
        import jax, jax.numpy as jnp
        import numpy as np
        B, N, M = (2, 256, 128)
        D, H, DH = (256, 16, 64)
        MID = H * DH
        DC = 192
        MULT = 4
        EPS = 1e-05

        def _ln(x, w, b):
            mu = jnp.mean(x, -1, keepdims=True)
            var = jnp.mean((x - mu) ** 2, -1, keepdims=True)
            return (x - mu) * jax.lax.rsqrt(var + EPS) * w + b

        def _sincos(n, d):
            inv = 1.0 / 10000.0 ** (jnp.arange(0, d, 2, dtype=jnp.float32) / d)
            ang = jnp.arange(n, dtype=jnp.float32)[:, None] * inv[None, :]
            return (jnp.sin(ang), jnp.cos(ang))

        def _rope(x, sin, cos):
            s = sin[None, None]
            c = cos[None, None]
            xe = x[..., ::2]
            xo = x[..., 1::2]
            re = xe * c - xo * s
            ro = xe * s + xo * c
            return jnp.stack((re, ro), axis=-1).reshape(x.shape)

        def _heads(t):
            b, n, _ = t.shape
            return t.reshape(b, n, H, DH).transpose(0, 2, 1, 3)

        def _attn(xq, ctx, wq, wkv, wo, bo):
            q = _heads(xq @ wq)
            k, v = jnp.split(ctx @ wkv, 2, axis=-1)
            k = _heads(k)
            v = _heads(v)
            sq, cq = _sincos(q.shape[2], DH)
            sk, ck = _sincos(k.shape[2], DH)
            q = _rope(q, sq, cq)
            k = _rope(k, sk, ck)
            sim = jnp.einsum('bhnd,bhmd->bhnm', q, k) * DH ** (-0.5)
            a = jax.nn.softmax(sim, axis=-1)
            o = jnp.einsum('bhnm,bhmd->bhnd', a, v)
            o = o.transpose(0, 2, 1, 3).reshape(xq.shape[0], xq.shape[1], MID)
            return o @ wo + bo

        def _adaln(x, c, lw, lb, gw, gb, bw, bb):
            g = (c @ gw + gb)[:, None, :]
            bt = (c @ bw + bb)[:, None, :]
            return _ln(x, lw, lb) * (1.0 + g) + bt
        ks = jax.random.split(jax.random.key(seed), 24)
        s = 0.02
        inp = {'x': jax.random.normal(ks[0], (B, N, D), jnp.float32), 'cond': jax.random.normal(ks[1], (B, D), jnp.float32), 'context': jax.random.normal(ks[2], (B, M, DC), jnp.float32), 'ln1_w': jnp.ones((D,), jnp.float32), 'ln1_b': jnp.zeros((D,), jnp.float32), 'g1_w': jax.random.normal(ks[3], (D, D), jnp.float32) * s, 'g1_b': jnp.zeros((D,), jnp.float32), 'b1_w': jax.random.normal(ks[4], (D, D), jnp.float32) * s, 'b1_b': jnp.zeros((D,), jnp.float32), 'ln2_w': jnp.ones((D,), jnp.float32), 'ln2_b': jnp.zeros((D,), jnp.float32), 'g2_w': jax.random.normal(ks[5], (D, D), jnp.float32) * s, 'g2_b': jnp.zeros((D,), jnp.float32), 'b2_w': jax.random.normal(ks[6], (D, D), jnp.float32) * s, 'b2_b': jnp.zeros((D,), jnp.float32), 'sa_wq': jax.random.normal(ks[7], (D, MID), jnp.float32) * s, 'sa_wkv': jax.random.normal(ks[8], (D, 2 * MID), jnp.float32) * s, 'sa_wo': jax.random.normal(ks[9], (MID, D), jnp.float32) * s, 'sa_bo': jnp.zeros((D,), jnp.float32), 'ca_lnc_w': jnp.ones((DC,), jnp.float32), 'ca_lnc_b': jnp.zeros((DC,), jnp.float32), 'ca_wq': jax.random.normal(ks[10], (D, MID), jnp.float32) * s, 'ca_wkv': jax.random.normal(ks[11], (DC, 2 * MID), jnp.float32) * s, 'ca_wo': jax.random.normal(ks[12], (MID, D), jnp.float32) * s, 'ca_bo': jnp.zeros((D,), jnp.float32), 'ff_w1': jax.random.normal(ks[13], (D, MULT * D), jnp.float32) * s, 'ff_b1': jnp.zeros((MULT * D,), jnp.float32), 'ff_w2': jax.random.normal(ks[14], (MULT * D, D), jnp.float32) * s, 'ff_b2': jnp.zeros((D,), jnp.float32)}
        return inp
    _L0_xcond_all = _L0_xcond_setup()
    _L0_xcond_in = {k: v for k, v in _L0_xcond_all.items() if k in ('ln1_w', 'ln1_b', 'g1_w', 'g1_b', 'b1_w', 'b1_b', 'ln2_w', 'ln2_b', 'g2_w', 'g2_b', 'b2_w', 'b2_b', 'sa_wq', 'sa_wkv', 'sa_wo', 'sa_bo', 'ca_lnc_w', 'ca_lnc_b', 'ca_wq', 'ca_wkv', 'ca_wo', 'ca_bo', 'ff_w1', 'ff_b1', 'ff_w2', 'ff_b2')}
    del _L0_xcond_all
    return {'x': x, 'cond_1024': cond_1024, 'ctx_768': ctx_768, 'L0_xcond_ln1_w': _L0_xcond_in['ln1_w'], 'L0_xcond_ln1_b': _L0_xcond_in['ln1_b'], 'L0_xcond_g1_w': _L0_xcond_in['g1_w'], 'L0_xcond_g1_b': _L0_xcond_in['g1_b'], 'L0_xcond_b1_w': _L0_xcond_in['b1_w'], 'L0_xcond_b1_b': _L0_xcond_in['b1_b'], 'L0_xcond_ln2_w': _L0_xcond_in['ln2_w'], 'L0_xcond_ln2_b': _L0_xcond_in['ln2_b'], 'L0_xcond_g2_w': _L0_xcond_in['g2_w'], 'L0_xcond_g2_b': _L0_xcond_in['g2_b'], 'L0_xcond_b2_w': _L0_xcond_in['b2_w'], 'L0_xcond_b2_b': _L0_xcond_in['b2_b'], 'L0_xcond_sa_wq': _L0_xcond_in['sa_wq'], 'L0_xcond_sa_wkv': _L0_xcond_in['sa_wkv'], 'L0_xcond_sa_wo': _L0_xcond_in['sa_wo'], 'L0_xcond_sa_bo': _L0_xcond_in['sa_bo'], 'L0_xcond_ca_lnc_w': _L0_xcond_in['ca_lnc_w'], 'L0_xcond_ca_lnc_b': _L0_xcond_in['ca_lnc_b'], 'L0_xcond_ca_wq': _L0_xcond_in['ca_wq'], 'L0_xcond_ca_wkv': _L0_xcond_in['ca_wkv'], 'L0_xcond_ca_wo': _L0_xcond_in['ca_wo'], 'L0_xcond_ca_bo': _L0_xcond_in['ca_bo'], 'L0_xcond_ff_w1': _L0_xcond_in['ff_w1'], 'L0_xcond_ff_b1': _L0_xcond_in['ff_b1'], 'L0_xcond_ff_w2': _L0_xcond_in['ff_w2'], 'L0_xcond_ff_b2': _L0_xcond_in['ff_b2']}

def reference(x, cond_1024, ctx_768, L0_xcond_ln1_w, L0_xcond_ln1_b, L0_xcond_g1_w, L0_xcond_g1_b, L0_xcond_b1_w, L0_xcond_b1_b, L0_xcond_ln2_w, L0_xcond_ln2_b, L0_xcond_g2_w, L0_xcond_g2_b, L0_xcond_b2_w, L0_xcond_b2_b, L0_xcond_sa_wq, L0_xcond_sa_wkv, L0_xcond_sa_wo, L0_xcond_sa_bo, L0_xcond_ca_lnc_w, L0_xcond_ca_lnc_b, L0_xcond_ca_wq, L0_xcond_ca_wkv, L0_xcond_ca_wo, L0_xcond_ca_bo, L0_xcond_ff_w1, L0_xcond_ff_b1, L0_xcond_ff_w2, L0_xcond_ff_b2):
    import jax
    import jax.numpy as jnp

    def _L0_xcond_ref(x, cond, context, ln1_w, ln1_b, g1_w, g1_b, b1_w, b1_b, ln2_w, ln2_b, g2_w, g2_b, b2_w, b2_b, sa_wq, sa_wkv, sa_wo, sa_bo, ca_lnc_w, ca_lnc_b, ca_wq, ca_wkv, ca_wo, ca_bo, ff_w1, ff_b1, ff_w2, ff_b2):
        import jax, jax.numpy as jnp
        import numpy as np
        B, N, M = (2, 256, 128)
        D, H, DH = (256, 16, 64)
        MID = H * DH
        DC = 192
        MULT = 4
        EPS = 1e-05

        def _ln(x, w, b):
            mu = jnp.mean(x, -1, keepdims=True)
            var = jnp.mean((x - mu) ** 2, -1, keepdims=True)
            return (x - mu) * jax.lax.rsqrt(var + EPS) * w + b

        def _sincos(n, d):
            inv = 1.0 / 10000.0 ** (jnp.arange(0, d, 2, dtype=jnp.float32) / d)
            ang = jnp.arange(n, dtype=jnp.float32)[:, None] * inv[None, :]
            return (jnp.sin(ang), jnp.cos(ang))

        def _rope(x, sin, cos):
            s = sin[None, None]
            c = cos[None, None]
            xe = x[..., ::2]
            xo = x[..., 1::2]
            re = xe * c - xo * s
            ro = xe * s + xo * c
            return jnp.stack((re, ro), axis=-1).reshape(x.shape)

        def _heads(t):
            b, n, _ = t.shape
            return t.reshape(b, n, H, DH).transpose(0, 2, 1, 3)

        def _attn(xq, ctx, wq, wkv, wo, bo):
            q = _heads(xq @ wq)
            k, v = jnp.split(ctx @ wkv, 2, axis=-1)
            k = _heads(k)
            v = _heads(v)
            sq, cq = _sincos(q.shape[2], DH)
            sk, ck = _sincos(k.shape[2], DH)
            q = _rope(q, sq, cq)
            k = _rope(k, sk, ck)
            sim = jnp.einsum('bhnd,bhmd->bhnm', q, k) * DH ** (-0.5)
            a = jax.nn.softmax(sim, axis=-1)
            o = jnp.einsum('bhnm,bhmd->bhnd', a, v)
            o = o.transpose(0, 2, 1, 3).reshape(xq.shape[0], xq.shape[1], MID)
            return o @ wo + bo

        def _adaln(x, c, lw, lb, gw, gb, bw, bb):
            g = (c @ gw + gb)[:, None, :]
            bt = (c @ bw + bb)[:, None, :]
            return _ln(x, lw, lb) * (1.0 + g) + bt
        attn_in = _adaln(x, cond, ln1_w, ln1_b, g1_w, g1_b, b1_w, b1_b)
        x = _attn(attn_in, attn_in, sa_wq, sa_wkv, sa_wo, sa_bo) + x
        cross_in = _adaln(x, cond, ln1_w, ln1_b, g1_w, g1_b, b1_w, b1_b)
        ctx_n = _ln(context, ca_lnc_w, ca_lnc_b)
        x = _attn(cross_in, ctx_n, ca_wq, ca_wkv, ca_wo, ca_bo) + x
        ffn_in = _adaln(x, cond, ln2_w, ln2_b, g2_w, g2_b, b2_w, b2_b)
        h = jax.nn.gelu(ffn_in @ ff_w1 + ff_b1, approximate=False)
        x = h @ ff_w2 + ff_b2 + x
        return x
    x = _L0_xcond_ref(x, cond_1024, ctx_768, L0_xcond_ln1_w, L0_xcond_ln1_b, L0_xcond_g1_w, L0_xcond_g1_b, L0_xcond_b1_w, L0_xcond_b1_b, L0_xcond_ln2_w, L0_xcond_ln2_b, L0_xcond_g2_w, L0_xcond_g2_b, L0_xcond_b2_w, L0_xcond_b2_b, L0_xcond_sa_wq, L0_xcond_sa_wkv, L0_xcond_sa_wo, L0_xcond_sa_bo, L0_xcond_ca_lnc_w, L0_xcond_ca_lnc_b, L0_xcond_ca_wq, L0_xcond_ca_wkv, L0_xcond_ca_wo, L0_xcond_ca_bo, L0_xcond_ff_w1, L0_xcond_ff_b1, L0_xcond_ff_w2, L0_xcond_ff_b2)
    return x

_drawn_inputs = setup_inputs


def setup_inputs(seed=0):
    import zlib

    import numpy as np

    out = dict(_drawn_inputs(seed))
    spreads = {'L0_xcond_ln1_w': (1.0, 0.6),
     'L0_xcond_ln1_b': (0.0, 0.384),
     'L0_xcond_g1_b': (0.0, 0.8),
     'L0_xcond_b1_b': (0.0, 0.358),
     'L0_xcond_ln2_w': (1.0, 0.6),
     'L0_xcond_ln2_b': (0.0, 0.618),
     'L0_xcond_g2_b': (0.0, 0.694),
     'L0_xcond_b2_b': (0.0, 0.764),
     'L0_xcond_sa_bo': (0.0, 0.1),
     'L0_xcond_ca_lnc_w': (1.0, 0.6),
     'L0_xcond_ca_lnc_b': (0.0, 0.531),
     'L0_xcond_ca_bo': (0.0, 0.1),
     'L0_xcond_ff_b1': (0.0, 0.273),
     'L0_xcond_ff_b2': (0.0, 0.1)}
    factors = {'L0_xcond_g1_w': 7.962, 'L0_xcond_sa_wq': 8.0, 'L0_xcond_ca_wq': 8.0}
    for name, (base, spread) in spreads.items():
        noise = np.random.default_rng([zlib.crc32(name.encode()), seed]).standard_normal(out[name].shape)
        drawn = base * np.exp(spread * noise) if base else spread * noise
        out[name] = jnp.asarray(drawn.astype(out[name].dtype))
    for name, factor in factors.items():
        out[name] = (out[name] * factor).astype(out[name].dtype)
    return out
```

```python
from contextlib import ExitStack

import numpy as np

import concourse.bass as bass
from concourse import mybir

F32 = mybir.dt.float32
F16 = mybir.dt.float16
ALU = mybir.AluOpType
ACT = mybir.ActivationFunctionType
AX_X = mybir.AxisListType.X

P = 128
B, N, D = 4, 1024, 256
M, DC = 77, 192
H, DH = 16, 64
MID = H * DH
HID = 4 * D
PAIRS = H // 2
TT = N // P
KD = D // P
KM = MID // P
HALF = N // 2
DH2 = 2 * DH
EPS = 1e-5
WS = 64.0
MS = 64.0




def clear_semaphores(nc, sems):
    nc.all_engine_barrier()
    nc.clear_and_free_semaphores(sems)
    nc.all_engine_barrier()


def prepare(nc, tag, consts, x_src, cond, norm, weights, xT_hi, xT_lo, context=None):
    lnw, lnb, gw, gb, bw, bb = norm
    with ExitStack() as ctx:
        def sb(name, shape, dt=F32):
            return ctx.enter_context(nc.sbuf_tensor(f"{tag}_{name}", shape, dt))

        sems = []
        ctx.callback(clear_semaphores, nc, sems)

        def sem(name):
            sems.append(nc.alloc_semaphore(f"{tag}_{name}"))
            return sems[-1]

        short = [n for n, w in enumerate(weights) if w[0].shape[0] < P]
        units = weights
        staged = sb("staged", [P, len(units), N])
        xs = sb("xs", [P, B, TT, D])
        xh = sb("xh", [P, 2, TT, D])
        rows = sb("rows", [P, 4, D])
        condT = sb("condT", [P, KD, B])
        cond_wide = sb("cond_wide", [P, KD, B, P])
        gates = sb("gates", [P, 2, KD, D])
        ones = sb("ones", [P, P])
        ident = sb("ident", [P, P])
        gam = sb("gam", [P, B, D])
        bet = sb("bet", [P, B, D])
        tmp = sb("tmp", [P, B, 2, D])
        tiles = B * TT
        cols = tiles + (B if context is not None else 0)
        stats = sb("stats", [P, cols, 6])
        mv = sb("mv", [P, cols, 2])
        var = sb("var", [P, cols])
        root = sb("root", [P, cols])
        rstd = sb("rstd", [P, cols])
        newton = sb("newton", [P, cols])
        ps_gate = [ctx.enter_context(nc.psum_tensor(f"{tag}_gate{i}", [P, 2, D], F32)) for i in range(4)]
        ps_t = [ctx.enter_context(nc.psum_tensor(f"{tag}_t{i}", [P, HALF], F32)) for i in range(4)]

        s_ident = sem("s_ident")
        s_par = sem("s_par")
        s_w = sem("s_w")
        s_x = [sem(f"s_x{b}") for b in range(B)]
        s_ones = sem("s_ones")
        s_zero = sem("s_zero")
        s_wide = sem("s_wide")
        s_gate = sem("s_gate")
        s_tab = sem("s_tab")
        s_whi = sem("s_whi")
        s_wlo = sem("s_wlo")
        s_stat = sem("s_stat")
        s_root = sem("s_root")
        s_xc = sem("s_xc")
        s_xn = sem("s_xn")
        s_xb = sem("s_xb")
        s_tr = sem("s_tr")
        s_hi = sem("s_hi")
        s_lo = sem("s_lo")
        if context is not None:
            c_src, c_w, c_b, cT_hi, cT_lo = context
            cs = sb("cs", [M, B, DC])
            crow = sb("crow", [M, 2, DC])
            s_c = sem("s_c")
            s_cn = sem("s_cn")
            s_ct = sem("s_ct")
            s_chi = sem("s_chi")
            s_clo = sem("s_clo")
            c_parts = [(k, (P, DC - P)[k], ps_gate[k].rearrange("p a d -> p (a d)")[0:(P, DC - P)[k], 0:B * M])
                       for k in range(2)]
        block = ctx.enter_context(nc.Block())

        @block.sync
        def _(sp):
            x_v = x_src.rearrange("b (t p) d -> b p t d", p=P)
            sp.dma_start(ident[:], consts["identity"]).then_inc(s_ident, 16)
            sp.dma_start(xs[:, 0], x_v[0]).then_inc(s_x[0], 16)
            for k in range(KD):
                sp.dma_start(condT[:, k, :], cond[:, k * P:(k + 1) * P].rearrange("b p -> p b"),
                             allow_slow_non_contiguous=True).then_inc(s_par, 16)
            for i, w in enumerate((gw, bw)):
                sp.dma_start(gates[:, i], w.rearrange("(k p) n -> p k n", p=P)).then_inc(s_par, 16)
            for i, v in enumerate((lnw, lnb, gb, bb)):
                sp.dma_start(rows[:, i, :], v.partition_broadcast(P)).then_inc(s_par, 16)
            for b in range(1, B):
                sp.dma_start(xs[:, b], x_v[b]).then_inc(s_x[b], 16)
            if context is not None:
                sp.dma_start(cs[:], c_src.rearrange("b m d -> m b d")).then_inc(s_c, 16)
                sp.dma_start(crow[:, 0, :], c_w.partition_broadcast(M)).then_inc(s_c, 16)
                sp.dma_start(crow[:, 1, :], c_b.partition_broadcast(M)).then_inc(s_c, 16)
            if short:
                sp.wait_ge(s_zero, 1)
            for n, (src, _, _) in enumerate(units):
                dst = staged[0:src.shape[0], n, :]
                if len(src.shape) == 3:
                    dst = dst.rearrange("p (a b) -> p a b", b=src.shape[2])
                sp.dma_start(dst, src).then_inc(s_w, 16)

        @block.gpsimd
        def _(pool):
            if context is not None:
                pool.memset(mv[:, tiles:cols, :], 1.0)
            pool.memset(ones[:], 1.0).then_inc(s_ones, 1)
            for n in short:
                ins = pool.memset(staged[:, n, :], 0.0)
            if short:
                ins.then_inc(s_zero, 1)
            pool.wait_ge(s_tab, 5 * B)
            for b in range(B):
                pool.wait_ge(s_xn, b + 1)
                pool.tensor_tensor(xh[:, b % 2], xh[:, b % 2], bet[:, b:b + 1, :].broadcast_to([P, TT, D]),
                                   ALU.add).then_inc(s_xb, 1)

        @block.scalar
        def _(act):
            act.wait_ge(s_stat, 3)
            act.activation(root[:], var[:], ACT.Sqrt).then_inc(s_root, 1)
            act.wait_ge(s_w, 16 * len(units))
            for n in range(len(units)):
                if context is not None and n == len(units) // 2:
                    for k, rows_k, src in c_parts:
                        act.wait_ge(s_ct, k + 1)
                        act.activation(cT_hi[0:rows_k, :, k, :], src.rearrange("p (b m) -> p b m", m=M),
                                       ACT.Copy).then_inc(s_chi, 1)
                act.activation(units[n][1], staged[:, n, :], ACT.Copy, scale=WS).then_inc(s_whi, 1)
            for b in range(B):
                for n in range(4):
                    k, h = n // 2, n % 2
                    act.wait_ge(s_tr, 4 * b + n + 1)
                    act.activation(xT_hi[:, b, k, h * HALF:(h + 1) * HALF], ps_t[n][:, :],
                                   ACT.Copy).then_inc(s_hi, 1)

        @block.tensor
        def _(pe):
            pe.wait_ge(s_ident, 16)
            if context is not None:
                pe.wait_ge(s_cn, 3)
                for k, rows_k, dst in c_parts:
                    for b in range(B):
                        ins = pe.transpose(dst[:, b * M:(b + 1) * M], cs[:, b, k * P:k * P + rows_k], ident[0:M, 0:M])
                    ins.then_inc(s_ct, 1)
                pe.wait_ge(s_clo, 2)
            pe.wait_ge(s_par, 16 * 8)
            pe.wait_ge(s_wide, 1)
            for b in range(B):
                for i in range(2):
                    for k in range(KD):
                        ins = pe.matmul(ps_gate[b][:, i, :], cond_wide[:, k, b, :], gates[:, i, k, :],
                                        start=(k == 0), stop=(k == KD - 1))
                ins.then_inc(s_gate, 1)
            for b in range(B):
                pe.wait_ge(s_xb, b + 1)
                for n in range(4):
                    k, h = n // 2, n % 2
                    if b >= 1:
                        pe.wait_ge(s_lo, 4 * (b - 1) + n + 1)
                    for q in range(4):
                        ins = pe.transpose(ps_t[n][:, q * P:(q + 1) * P], xh[:, b % 2, 4 * h + q, k * P:(k + 1) * P],
                                           ident[:, :])
                    ins.then_inc(s_tr, 1)

        @block.vector
        def _(dve):
            if context is not None:
                dve.memset(cT_hi[DC - P:P, :, 1, :], 0.0)
                dve.memset(cT_lo[DC - P:P, :, 1, :], 0.0)
            dve.wait_ge(s_par, 16 * 8)
            dve.wait_ge(s_ones, 1)
            for k in range(KD):
                for b in range(B):
                    ins = dve.tensor_scalar(cond_wide[:, k, b, :], ones[:, :], condT[:, k, b:b + 1], None, ALU.mult)
            ins.then_inc(s_wide, 1)
            for b in range(B):
                dve.wait_ge(s_x[b], 16)
                for t in range(TT):
                    ins = dve.bn_stats(stats[:, b * TT + t, :], xs[:, b, t, :])
            if context is not None:
                dve.wait_ge(s_c, 48)
                for b in range(B):
                    ins = dve.bn_stats(stats[0:M, tiles + b, :], cs[:, b, :])
            ins.then_inc(s_stat, 1)
            dve.wait_ge(s_stat, 1)
            for n in range(cols):
                rows_n = P if n < tiles else M
                ins = dve.bn_aggr(mv[0:rows_n, n, :], stats[0:rows_n, n, :])
            ins.then_inc(s_stat, 1)
            dve.wait_ge(s_stat, 2)
            dve.tensor_scalar(var[:], mv[:, :, 1], EPS, None, ALU.add).then_inc(s_stat, 1)
            dve.wait_ge(s_root, 1)
            dve.reciprocal(rstd[:], root[:]).then_inc(s_stat, 1)
            dve.wait_ge(s_stat, 4)
            dve.tensor_tensor(newton[:], rstd[:], rstd[:], ALU.mult).then_inc(s_stat, 1)
            dve.wait_ge(s_stat, 5)
            dve.scalar_tensor_tensor(out=newton[:], in0=newton[:], scalar=-0.5, in1=var[:], op0=ALU.mult,
                                     op1=ALU.mult).then_inc(s_stat, 1)
            dve.wait_ge(s_stat, 6)
            dve.scalar_tensor_tensor(out=rstd[:], in0=newton[:], scalar=1.5, in1=rstd[:], op0=ALU.add,
                                     op1=ALU.mult).then_inc(s_stat, 1)
            dve.wait_ge(s_stat, 7)
            if context is not None:
                for b in range(B):
                    n = tiles + b
                    ins = dve.tensor_scalar(cs[:, b, :], cs[:, b, :], mv[0:M, n, 0:1], rstd[0:M, n:n + 1],
                                            ALU.subtract, ALU.mult)
                ins.then_inc(s_cn, 1)
                dve.wait_ge(s_cn, 1)
                dve.tensor_tensor(cs[:], cs[:], crow[:, 0:1, :].broadcast_to([M, B, DC]), ALU.mult).then_inc(s_cn, 1)
                dve.wait_ge(s_cn, 2)
                dve.tensor_tensor(cs[:], cs[:], crow[:, 1:2, :].broadcast_to([M, B, DC]), ALU.add).then_inc(s_cn, 1)

            def tokens(b):
                if b >= 2:
                    dve.wait_ge(s_tr, 4 * (b - 1))
                for t in range(TT):
                    n = b * TT + t
                    ins = dve.tensor_scalar(xh[:, b % 2, t, :], xs[:, b, t, :], mv[:, n, 0:1], rstd[:, n:n + 1],
                                            ALU.subtract, ALU.mult)
                ins.then_inc(s_xc, 1)
                dve.wait_ge(s_xc, b + 1)
                if b == 0:
                    dve.wait_ge(s_tab, 5 * B)
                dve.tensor_tensor(xh[:, b % 2], xh[:, b % 2], gam[:, b:b + 1, :].broadcast_to([P, TT, D]),
                                  ALU.mult).then_inc(s_xn, 1)

            def tokens_lo(b):
                for n in range(4):
                    k, h = n // 2, n % 2
                    dve.wait_ge(s_hi, 4 * b + n + 1)
                    dve.tensor_tensor(xT_lo[:, b, k, h * HALF:(h + 1) * HALF], ps_t[n][:, :],
                                      xT_hi[:, b, k, h * HALF:(h + 1) * HALF], ALU.subtract).then_inc(s_lo, 1)

            if context is not None:
                for k, rows_k, src in c_parts:
                    dve.wait_ge(s_chi, k + 1)
                    dve.tensor_tensor(cT_lo[0:rows_k, :, k, :], src.rearrange("p (b m) -> p b m", m=M),
                                      cT_hi[0:rows_k, :, k, :], ALU.subtract).then_inc(s_clo, 1)
            for b in range(B):
                dve.wait_ge(s_gate, b + 1)
                for i in range(2):
                    dve.tensor_tensor(tmp[:, b, i, :], ps_gate[b][:, i, :], rows[:, 2 + i, :], ALU.add).then_inc(s_tab, 1)
            for b in range(B):
                dve.wait_ge(s_tab, 2 * b + 2)
                for i, dst in enumerate((gam, bet)):
                    dve.scalar_tensor_tensor(out=dst[:, b, :], in0=tmp[:, b, 0, :], scalar=1.0, in1=rows[:, i, :],
                                             op0=ALU.add, op1=ALU.mult).then_inc(s_tab, 1)
            for b in range(B):
                dve.wait_ge(s_tab, 2 * B + 2 * b + 2)
                dve.tensor_tensor(bet[:, b, :], bet[:, b, :], tmp[:, b, 1, :], ALU.add).then_inc(s_tab, 1)
            for b in range(B):
                tokens(b)
                for n in range(b * len(units) // B, (b + 1) * len(units) // B):
                    dve.wait_ge(s_whi, n + 1)
                    _, w_hi, w_lo = units[n]
                    dve.scalar_tensor_tensor(out=w_lo, in0=staged[:, n, :], scalar=WS, in1=w_hi, op0=ALU.mult,
                                             op1=ALU.subtract).then_inc(s_wlo, 1)
                if b >= 1:
                    tokens_lo(b - 1)
            tokens_lo(B - 1)


def pair_at(j):
    if isinstance(j, int):
        return j // PAIRS % B, bass.ds(j % PAIRS * P, P)
    return (j >> 3) & (B - 1), bass.ds((j & (PAIRS - 1)) * P, P)


def split_product(pe, out, k_tiles, lhs, rhs, lhs_at, rhs_at, start=True, stop=True):
    terms = [(k, a, b) for k in k_tiles for a, b in ((0, 0), (1, 0), (0, 1))]
    for i, (k, a, b) in enumerate(terms):
        ins = pe.matmul(out, lhs[a][lhs_at(k)], rhs[b][rhs_at(k)], start=(start and i == 0),
                        stop=(stop and i == len(terms) - 1))
    return ins


def output_projection(pe, o_hi, o_lo, wo, ps_y, s_y, s_yr, b, s_ot, parts):
    o, last = (o_hi, o_lo), KM - 1

    def product(t, ks, start, stop):
        ts = slice(t * P, (t + 1) * P)
        return split_product(pe, ps_y[t % 4], ks, o, wo, lambda k: (slice(None), k, ts),
                             lambda k: (slice(None), k, slice(None)), start, stop)

    pe.wait_ge(s_ot, 1 + parts * (KM * b + last))
    for t in range(4):
        product(t, range(last), True, False)
    for t in range(4):
        if t == 0:
            pe.wait_ge(s_ot, 1 + parts * (KM * b + last) + 1)
        product(t, (last,), False, True).then_inc(s_y, 1)
    pe.wait_ge(s_ot, 1 + parts * KM * (b + 1))
    for t in range(4, TT):
        pe.wait_ge(s_yr, 1 + TT * b + t - 3)
        product(t, range(KM), True, True).then_inc(s_y, 1)


def self_attention(nc, consts, x_src, x_dst, bo, xT, wq, wk, wv, wo):
    NK = N // P
    MAXB = 4 * TT
    STEP_MAX = {1: range(0, 6), 2: range(6, 11), 3: range(11, 16), 4: range(16, 22), 5: range(22, 27),
                6: range(27, 32)}
    ident16, ropeC, ropeS, ones32 = consts["ident16"], consts["ropeC"], consts["ropeS"], consts["ones32"]
    with ExitStack() as ctx:
        def sb(name, shape, dt=F32):
            return ctx.enter_context(nc.sbuf_tensor(f"sa_{name}", shape, dt))

        def ps(name, shape):
            return ctx.enter_context(nc.psum_tensor(f"sa_{name}", shape, F32))

        def sem(name):
            return ctx.enter_context(nc.semaphore(f"sa_{name}"))

        q_hh = sb("q_hh", [P, 2, 2, N], F16)
        q_lm = sb("q_lm", [P, 2, 2, N], F16)
        k_hl = sb("k_hl", [P, 2, 2, N], F16)
        k_h1 = sb("k_h1", [P, 2, 2, N], F16)
        raw = sb("raw", [P, 2, N])
        swp = sb("swp", [P, 2, N])
        hi = sb("hi", [P, 2, N], F16)
        lo = sb("lo", [P, 2, N], F16)
        v_pair = sb("v_pair", [P, 2, NK, P])
        probs = sb("probs", [P, 2, 2, N])
        acc = sb("acc", [P, 2, N])
        inv = acc[:, 1, :]
        o_pair = sb("o_pair", [P, N])
        o_hi = sb("o_hi", [P, PAIRS, N], F16)
        o_lo = sb("o_lo", [P, PAIRS, N], F16)
        xr = sb("xr", [P, TT, D])
        bo_row = sb("bo_row", [P, 1, D])
        mx = sb("mx", [P, 2, 2, TT])
        mc = sb("mc", [P, 2, TT])
        zcol = sb("zcol", [P, 2, TT, DH + 1], F16)
        ps_s = [ps(f"ps_s{i}", [P, N]) for i in range(2)]
        ps_o = ps("ps_o", [P, N])
        ps_turn = [ps(f"ps_turn{i}", [P, HALF]) for i in range(2)]
        ps_y = [ps_s[i // 2][:, i % 2 * HALF:i % 2 * HALF + D] for i in range(4)]

        s_init = sem("s_init")
        s_bo = sem("s_bo")
        s_x = sem("s_x")
        s_xb = sem("s_xb")
        s_swap = [sem("s_swapk"), sem("s_swapq")]
        s_stack = [sem("s_stackk"), sem("s_stackq")]
        s_cos = sem("s_cos")
        s_sin = sem("s_sin")
        s_rot = sem("s_rot")
        s_hi = sem("s_hi")
        s_lo = sem("s_lo")
        s_kq_w = sem("s_kq_w")
        s_kq_r = sem("s_kq_r")
        s_v_w = sem("s_v_w")
        s_v_r = sem("s_v_r")
        s_max_w = sem("s_max_w")
        s_max_r = sem("s_max_r")
        s_mc = sem("s_mc")
        s_z = sem("s_z")
        s_row_w = sem("s_row_w")
        s_row_r = sem("s_row_r")
        s_sum_w = sem("s_sum_w")
        s_sum_r = sem("s_sum_r")
        s_st = sem("s_st")
        s_p = sem("s_p")
        s_acc0 = sem("s_acc0")
        s_acc1 = sem("s_acc1")
        s_pv = sem("s_pv")
        s_oev = sem("s_oev")
        s_inv = sem("s_inv")
        s_div = sem("s_div")
        s_ohi = sem("s_ohi")
        s_ot = sem("s_ot")
        s_y = sem("s_y")
        s_yr = sem("s_yr")
        s_out = sem("s_out")
        block = ctx.enter_context(nc.Block())
        x_v = x_src.rearrange("b (t p) d -> b p t d", p=P)
        y_v = x_dst.rearrange("b (t p) d -> b p t d", p=P)

        @block.sync
        def _(sp):
            def swap(j):
                for i in range(2):
                    sp.wait_ge(s_kq_r, 4 * j + 2 * i + 2)
                    sp.dma_start(swp[0:P:2, i, :], raw[1:P:2, i, :]).then_inc(s_swap[i], 16)
                    sp.dma_start(swp[1:P:2, i, :], raw[0:P:2, i, :]).then_inc(s_swap[i], 16)

            def stack(j, par):
                for i in range(2):
                    sp.wait_ge(s_hi, 2 * j + i + 1)
                    for x in range(2):
                        mine = hi[DH * x:DH * x + DH, i, :]
                        first, second = ((k_hl[0:DH], k_h1[0:DH]), (q_hh[0:DH], q_hh[DH:P]))[i]
                        sp.dma_start(first[:, par, x, :], mine).then_inc(s_stack[i], 16)
                        sp.dma_start(second[:, par, x, :], mine).then_inc(s_stack[i], 16)
                    sp.wait_ge(s_lo, 2 * j + i + 1)
                    for x in range(2):
                        dst = (k_hl[DH:P], q_lm[0:DH])[i]
                        sp.dma_start(dst[:, par, x, :], lo[DH * x:DH * x + DH, i, :]).then_inc(s_stack[i], 16)

            sp.dma_start(bo_row[:, 0, :], bo.partition_broadcast(P)).then_inc(s_bo, 16)
            swap(0)
            sp.wait_ge(s_init, 4)
            stack(0, 0)
            swap(1)
            for b in range(B):
                if b >= 1:
                    sp.wait_ge(s_out, 16 * b)
                sp.dma_start(xr[:], x_v[b]).then_inc(s_x, 16)
                with sp.Fori(0, PAIRS // 2) as pp:
                    for par in range(2):
                        g = b * PAIRS + pp * 2 + par
                        sp.wait_ge(s_st, 1 + 2 * NK * g)
                        stack(g + 1, 1 - par)
                        swap(g + 2)
                sp.wait_ge(s_yr, 1 + TT * b + TT)
                sp.dma_start(y_v[b], xr[:]).then_inc(s_out, 16)
            sp.wait_ge(s_out, 16 * B)
            for i in range(2):
                sp.wait_ge(s_swap[i], 32 * (B * PAIRS + 2))
                sp.wait_ge(s_stack[i], 96 * (B * PAIRS + 1))

        @block.gpsimd
        def _(pool):
            def rotate(j, i, table):
                pool.wait_ge(s_swap[i], 32 * j + 32)
                if table == 0:
                    pool.tensor_tensor(raw[:, i, :], raw[:, i, :], ropeC[:, :], ALU.mult).then_inc(s_cos, 1)
                else:
                    pool.tensor_tensor(swp[:, i, :], swp[:, i, :], ropeS[:, :], ALU.mult).then_inc(s_sin, 1)

            def low(j, i):
                pool.wait_ge(s_hi, 2 * j + i + 1)
                pool.wait_ge(s_stack[i], 96 * j)
                pool.tensor_tensor(lo[:, i, :], raw[:, i, :], hi[:, i, :], ALU.subtract).then_inc(s_lo, 1)

            def add_probs(g, kt):
                pool.wait_ge(s_p, 1 + 2 * NK * g + 2 * kt + 1)
                if kt == 1:
                    before = probs[:, 0, 0, :]
                else:
                    before = acc[:, 0, :]
                    pool.wait_ge(s_acc0, (NK - 1) * g + kt - 1)
                pool.tensor_tensor(acc[:, 0, :], before, probs[:, kt % 2, 0, :], ALU.add).then_inc(s_acc0, 1)

            for i in range(2):
                rotate(0, i, 0)
                rotate(0, i, 1)
            for i in range(2):
                pool.wait_ge(s_hi, i + 1)
                pool.tensor_tensor(lo[:, i, :], raw[:, i, :], hi[:, i, :], ALU.subtract).then_inc(s_lo, 1)
            for i in range(2):
                rotate(1, i, 0)
                rotate(1, i, 1)
            for i in range(2):
                low(1, i)
            with pool.Fori(0, B * PAIRS) as g:
                for kt in range(1, NK):
                    add_probs(g, kt)
                    if kt <= 4:
                        rotate(g + 2, (kt - 1) // 2, (kt - 1) % 2)
                    elif kt <= 6:
                        low(g + 2, kt - 5)

        @block.tensor
        def _(pe):
            def project(j, first):
                b, cols = pair_at(j)
                for i, w in enumerate((wk, wq)):
                    for c in range(2):
                        if i == 0:
                            for s, v in first(c):
                                pe.wait_ge(s, v)
                        else:
                            pe.wait_ge(s_kq_r, 4 * j + c + 1)
                        split_product(pe, ps_turn[c][:, :], range(KD), w, xT, lambda k: (slice(None), k, cols),
                                      lambda k, c=c: (slice(None), b, k, slice(c * HALF, (c + 1) * HALF)))\
                            .then_inc(s_kq_w, 1)

            def project_v(j):
                b, cols = pair_at(j)
                for c in range(2):
                    for q in range(4):
                        ks = slice((4 * c + q) * P, (4 * c + q + 1) * P)
                        ins = split_product(pe, ps_turn[c][:, q * P:(q + 1) * P], range(KD), xT, wv,
                                            lambda k, ks=ks: (slice(None), b, k, ks),
                                            lambda k: (slice(None), k, cols))
                    ins.then_inc(s_v_w, 1)

            def max_block(j, par, n):
                if n >= 2:
                    pe.wait_ge(s_max_r, MAXB * j + n - 1)
                x, t, c = n // (2 * TT), n // 2 % TT, n % 2
                pe.matmul(ps_turn[c][:, :], q_hh[:, par, x, t * P:(t + 1) * P],
                          k_hl[:, par, x, c * HALF:(c + 1) * HALF], start=True, stop=True).then_inc(s_max_w, 1)

            def max_rows(j, x):
                pe.wait_ge(s_z, 2 * j + x + 1)
                for c in range(2):
                    if x == 0:
                        pe.wait_ge(s_max_r, MAXB * (j + 1) - 1 + c)
                    else:
                        pe.wait_ge(s_row_r, 4 * j + c + 1)
                    for q in range(4):
                        ins = pe.matmul(ps_turn[c][0:DH + 1, q * P:(q + 1) * P], zcol[:, x, 4 * c + q, :],
                                        ident16[:, :], start=True, stop=True)
                    ins.then_inc(s_row_w, 1)

            def scores(par, x, kt, c):
                cs, ks = slice(c * HALF, (c + 1) * HALF), slice(kt * P, (kt + 1) * P)
                pe.matmul(ps_s[x][:, cs], k_hl[:, par, x, ks], q_hh[:, par, x, cs], start=True, stop=False)
                return pe.matmul(ps_s[x][:, cs], k_h1[:, par, x, ks], q_lm[:, par, x, cs], start=False, stop=True)

            def values(par, kt, c):
                cs = slice(c * HALF, (c + 1) * HALF)
                for x in range(2):
                    ins = pe.matmul(ps_o[DH * x:DH * x + DH, cs], v_pair[:, par, kt, DH * x:DH * x + DH],
                                    probs[:, kt % 2, x, cs], start=(kt == 0), stop=(kt == NK - 1))
                return ins

            project(0, lambda c: ())
            for c in range(2):
                pe.wait_ge(s_kq_r, 3 + c)
            project_v(0)
            project(1, lambda c: ((s_v_r, c + 1),))
            for i in range(2):
                pe.wait_ge(s_stack[i], 96)
            pe.wait_ge(s_kq_r, 8)
            for n in range(MAXB):
                max_block(0, 0, n)
            max_rows(0, 0)
            max_rows(0, 1)
            pe.sem_inc(s_st, 1)
            with pe.Fori(0, B) as b:
                with pe.Fori(0, PAIRS // 2) as pp:
                    for par in range(2):
                        g = b * PAIRS + pp * 2 + par
                        pe.wait_ge(s_yr, 1 + TT * b)
                        pe.wait_ge(s_row_r, 4 * (g + 1))
                        for kt in range(NK):
                            blocks = STEP_MAX.get(kt, ())
                            if kt == 1:
                                for i in range(2):
                                    pe.wait_ge(s_stack[i], 96 * (g + 2))
                                pe.wait_ge(s_kq_r, 4 * (g + 3))
                            for x in range(2):
                                if kt == 0:
                                    pe.wait_ge(s_p, 1 + 2 * NK * g)
                                else:
                                    pe.wait_ge(s_p, 1 + 2 * NK * g + 2 * (kt - 1) + x + 1)
                                for c in range(2):
                                    ins = scores(par, x, kt, c)
                                    if c == 1:
                                        ins.then_inc(s_st, 1)
                                    if 2 * x + c < len(blocks):
                                        max_block(g + 1, 1 - par, blocks[2 * x + c])
                            if kt == 0:
                                pe.wait_ge(s_sum_r, 1 + 2 * g)
                                project_v(g + 1)
                                project(g + 2, lambda c: ((s_v_r, 2 * (g + 1) + c + 1),))
                            else:
                                pe.wait_ge(s_p, 1 + 2 * NK * g + 2 * kt)
                                if kt == 1:
                                    pe.wait_ge(s_oev, 1 + g)
                                    pe.wait_ge(s_v_r, 2 * (g + 1))
                                for c in range(2):
                                    ins = values(par, kt - 1, c)
                                    if c == 1:
                                        ins.then_inc(s_pv, 1)
                                    if 4 + c < len(blocks):
                                        max_block(g + 1, 1 - par, blocks[4 + c])
                            if kt == 6:
                                max_rows(g + 1, 0)
                        max_rows(g + 1, 1)
                        pe.wait_ge(s_p, 1 + 2 * NK * (g + 1))
                        for c in range(2):
                            ins = values(par, NK - 1, c)
                        ins.then_inc(s_pv, 1)
                        pe.wait_ge(s_acc0, (NK - 1) * (g + 1))
                        pe.wait_ge(s_acc1, (NK - 1) * (g + 1))
                        for c in range(2):
                            pe.wait_ge(s_row_r, 4 * (g + 1) + 3 + c)
                            for x in range(2):
                                ins = pe.matmul(ps_turn[c][DH * x:DH * x + DH, :], ones32[:, :],
                                                acc[:, x, c * HALF:(c + 1) * HALF], start=True, stop=True)
                            ins.then_inc(s_sum_w, 1)
                output_projection(pe, o_hi, o_lo, wo, ps_y, s_y, s_yr, b, s_ot, 2)

        @block.scalar
        def _(act):
            def evacuate_kq(j, i, c):
                act.wait_ge(s_kq_w, 4 * j + 2 * i + c + 1)
                act.activation(raw[:, i, c * HALF:(c + 1) * HALF], ps_turn[c][:, :], ACT.Copy,
                               scale=1.0 / WS).then_inc(s_kq_r, 1)

            def evacuate_v(j, par):
                for c in range(2):
                    act.wait_ge(s_v_w, 2 * j + c + 1)
                    act.activation(v_pair[:, par, 4 * c:4 * c + 4, :],
                                   ps_turn[c].rearrange("p (a b) -> p a b", b=P), ACT.Copy,
                                   scale=1.0 / WS).then_inc(s_v_r, 1)

            def high(j, i):
                act.wait_ge(s_rot, 2 * j + i + 1)
                act.activation(hi[:, i, :], raw[:, i, :], ACT.Copy).then_inc(s_hi, 1)

            def row(j, par, x):
                for c in range(2):
                    act.wait_ge(s_row_w, 4 * j + 2 * x + c + 1)
                    act.activation(q_lm[DH:DH + 1, par, x, c * HALF:(c + 1) * HALF], ps_turn[c][DH:DH + 1, :],
                                   ACT.Copy).then_inc(s_row_r, 1)

            def exponentials(g, kt, x):
                act.wait_ge(s_st, 1 + 2 * NK * g + 2 * kt + x + 1)
                if kt >= 2:
                    act.wait_ge(s_pv, NK * g + kt - 1)
                    act.wait_ge((s_acc0, s_acc1)[x], (NK - 1) * g + max(1, kt - 2))
                act.activation(probs[:, kt % 2, x, :], ps_s[x][:, :], ACT.Exp, scale=float(DH) ** -0.5).then_inc(s_p, 1)

            act.sem_inc(s_p, 1)
            act.sem_inc(s_oev, 1)
            act.sem_inc(s_sum_r, 1)
            act.wait_ge(s_init, 4)
            for i in range(2):
                for c in range(2):
                    evacuate_kq(0, i, c)
            evacuate_v(0, 0)
            high(0, 0)
            high(0, 1)
            for i in range(2):
                act.wait_ge(s_lo, i + 1)
                for c in range(2):
                    evacuate_kq(1, i, c)
            row(0, 0, 0)
            row(0, 0, 1)
            for i in range(2):
                act.wait_ge(s_stack[i], 96)
                high(1, i)
            with act.Fori(0, B) as b:
                with act.Fori(0, PAIRS // 2) as pp:
                    for par in range(2):
                        g = b * PAIRS + pp * 2 + par
                        p = pp * 2 + par
                        for kt in range(NK):
                            exponentials(g, kt, 0)
                            exponentials(g, kt, 1)
                            if kt == 0:
                                evacuate_v(g + 1, 1 - par)
                                for i in range(2):
                                    act.wait_ge(s_lo, 2 * (g + 1) + i + 1)
                                    for c in range(2):
                                        evacuate_kq(g + 2, i, c)
                            if kt in (3, 5):
                                i = (kt - 3) // 2
                                act.wait_ge(s_stack[i], 96 * (g + 2))
                                high(g + 2, i)
                            if kt == 6:
                                row(g + 1, 1 - par, 0)
                        row(g + 1, 1 - par, 1)
                        act.wait_ge(s_pv, NK * (g + 1))
                        act.wait_ge(s_ot, 1 + 2 * g)
                        act.activation(o_pair[:], ps_o[:], ACT.Copy).then_inc(s_oev, 1)
                        for c in range(2):
                            act.wait_ge(s_sum_w, 2 * g + c + 1)
                            act.activation(inv[:, c * HALF:(c + 1) * HALF], ps_turn[c][:, :], ACT.Copy).then_inc(s_sum_r, 1)

        @block.vector
        def _(dve):
            def rotated(j, i):
                dve.wait_ge(s_sin, 2 * j + i + 1)
                dve.wait_ge(s_cos, 2 * j + i + 1)
                dve.tensor_tensor(raw[:, i, :], raw[:, i, :], swp[:, i, :], ALU.add).then_inc(s_rot, 1)

            def maximum(j, n):
                x, t, c = n // (2 * TT), n // 2 % TT, n % 2
                dve.wait_ge(s_max_w, MAXB * j + n + 1)
                dve.reduce_max(mx[:, x, c, t:t + 1], ps_turn[c][:, :], AX_X).then_inc(s_max_r, 1)
                if n % (2 * TT) == 2 * TT - 1:
                    dve.wait_ge(s_max_r, MAXB * j + n + 1)
                    dve.tensor_tensor(mc[:, x, :], mx[:, x, 0, :], mx[:, x, 1, :], ALU.max).then_inc(s_mc, 1)
                    dve.wait_ge(s_mc, 2 * j + x + 1)
                    dve.tensor_scalar(zcol[:, x, :, DH], mc[:, x, :], -1.0 / MS, None, ALU.mult).then_inc(s_z, 1)

            def add_probs(g, kt):
                dve.wait_ge(s_p, 1 + 2 * NK * g + 2 * kt + 2)
                if kt == 1:
                    before = probs[:, 0, 1, :]
                else:
                    before = acc[:, 1, :]
                    dve.wait_ge(s_acc1, (NK - 1) * g + kt - 1)
                dve.tensor_tensor(acc[:, 1, :], before, probs[:, kt % 2, 1, :], ALU.add).then_inc(s_acc1, 1)

            dve.sem_inc(s_ot, 1)
            dve.sem_inc(s_yr, 1)
            dve.memset(zcol[:], 0.0).then_inc(s_init, 1)
            dve.memset(q_lm[DH:P], 0.0).then_inc(s_init, 1)
            dve.memset(k_h1[DH:P], 0.0).then_inc(s_init, 1)
            dve.wait_ge(s_init, 3)
            dve.memset(k_h1[DH:DH + 1], MS).then_inc(s_init, 1)
            rotated(0, 0)
            rotated(0, 1)
            rotated(1, 0)
            rotated(1, 1)
            for n in range(MAXB):
                maximum(0, n)
            dve.wait_ge(s_bo, 16)
            with dve.Fori(0, B) as b:
                dve.wait_ge(s_x, 16 * b + 16)
                dve.tensor_tensor(xr[:], xr[:], bo_row[:].broadcast_to([P, TT, D]), ALU.add).then_inc(s_xb, 1)
                with dve.Fori(0, PAIRS) as p:
                    g = b * PAIRS + p
                    for kt in range(1, NK):
                        blocks = STEP_MAX.get(kt, ())
                        for n in blocks[:2]:
                            maximum(g + 1, n)
                        if kt >= 2:
                            add_probs(g, kt - 1)
                        for n in blocks[2:]:
                            maximum(g + 1, n)
                        if kt in (3, 5):
                            rotated(g + 2, (kt - 3) // 2)
                    add_probs(g, NK - 1)
                    for c in range(2):
                        n, cs = 2 * g + c + 1, slice(c * HALF, (c + 1) * HALF)
                        dve.wait_ge(s_sum_r, 1 + n)
                        dve.reciprocal(inv[:, cs], inv[:, cs]).then_inc(s_inv, 1)
                        dve.wait_ge(s_inv, n)
                        dve.wait_ge(s_oev, 1 + g + 1)
                        dve.tensor_tensor(o_pair[:, cs], o_pair[:, cs], inv[:, cs], ALU.mult).then_inc(s_div, 1)
                        dve.wait_ge(s_div, n)
                        dve.tensor_copy(o_hi[:, p, cs], o_pair[:, cs]).then_inc(s_ohi, 1)
                        dve.wait_ge(s_ohi, n)
                        dve.tensor_tensor(o_lo[:, p, cs], o_pair[:, cs], o_hi[:, p, cs], ALU.subtract).then_inc(s_ot, 1)
                dve.wait_ge(s_xb, b + 1)
                for t in range(TT):
                    dve.wait_ge(s_y, TT * b + t + 1)
                    dve.scalar_tensor_tensor(out=xr[:, t, :], in0=ps_y[t % 4], scalar=1.0 / WS, in1=xr[:, t, :],
                                             op0=ALU.mult, op1=ALU.add).then_inc(s_yr, 1)


def cross_attention(nc, consts, x_src, x_dst, bo, xT, cT, wq, wk, wv, wo):
    ropeC, ropeS = consts["ropeC"], consts["ropeS"]
    width = (M, N)
    with ExitStack() as ctx:
        def sb(name, shape, dt=F32):
            return ctx.enter_context(nc.sbuf_tensor(f"ca_{name}", shape, dt))

        def ps(name, shape):
            return ctx.enter_context(nc.psum_tensor(f"ca_{name}", shape, F32))

        def sem(name):
            return ctx.enter_context(nc.semaphore(f"ca_{name}"))

        q_hl = sb("q_hl", [P, 2, 2, N], F16)
        k_hh = sb("k_hh", [P, 2, 2, M], F16)
        k_lo = sb("k_lo", [DH, 2, 2, M], F16)
        raw = [sb(f"raw{i}", [P, 2, width[i]]) for i in range(2)]
        swp = [sb(f"swp{i}", [P, 2, width[i]]) for i in range(2)]
        rot = [sb(f"rot{i}", [P, 2, width[i]]) for i in range(2)]
        hi = [sb(f"hi{i}", [P, 2, width[i]], F16) for i in range(2)]
        lo = [sb(f"lo{i}", [P, 2, width[i]], F16) for i in range(2)]
        v_pair = sb("v_pair", [M, 2, P])
        ident = sb("ident", [P, P])
        e = sb("e", [P, 2, 2, TT, M])
        mx = sb("mx", [P, 2, TT])
        total = sb("total", [P, 2, TT])
        inv = sb("inv", [P, 2, 2, TT])
        pT = sb("pT", [M, 2, N])
        o_hi = sb("o_hi", [P, PAIRS, N], F16)
        o_lo = sb("o_lo", [P, PAIRS, N], F16)
        xr = sb("xr", [P, TT, D])
        bo_row = sb("bo_row", [P, 1, D])
        ps_sc = ps("ps_sc", [P, TT, P])
        ps_pt = ps("ps_pt", [P, N])
        ps_o = ps("ps_o", [P, N])
        ps_turn = [ps(f"ps_turn{i}", [P, HALF]) for i in range(2)]
        ps_y = [ps_pt[:, i * HALF:i * HALF + D] for i in range(2)] + [t[:, 0:D] for t in ps_turn]

        s_ident = sem("s_ident")
        s_bo = sem("s_bo")
        s_x = sem("s_x")
        s_xb = sem("s_xb")
        s_swap = [[sem(f"s_swap{n}{par}") for n in "kq"] for par in range(2)]
        s_stack = [[sem(f"s_stack{n}{par}") for n in "kq"] for par in range(2)]
        s_cos = sem("s_cos")
        s_sin = sem("s_sin")
        s_rot = sem("s_rot")
        s_hi = sem("s_hi")
        s_lo = sem("s_lo")
        s_kq_w = sem("s_kq_w")
        s_kq_r = sem("s_kq_r")
        s_v_w = sem("s_v_w")
        s_v_r = sem("s_v_r")
        s_sc_w = sem("s_sc_w")
        s_sc_r = sem("s_sc_r")
        s_mx = sem("s_mx")
        s_e = sem("s_e")
        s_total = sem("s_total")
        s_inv = sem("s_inv")
        s_prob0 = sem("s_prob0")
        s_prob1 = sem("s_prob1")
        s_pt_w = sem("s_pt_w")
        s_pt_r = sem("s_pt_r")
        s_pv = sem("s_pv")
        s_ohi = sem("s_ohi")
        s_ot = sem("s_ot")
        s_y = sem("s_y")
        s_yr = sem("s_yr")
        s_out = sem("s_out")
        block = ctx.enter_context(nc.Block())
        x_v = x_src.rearrange("b (t p) d -> b p t d", p=P)
        y_v = x_dst.rearrange("b (t p) d -> b p t d", p=P)

        @block.sync
        def _(sp):
            def swap(j, par):
                for i in range(2):
                    sp.wait_ge(s_kq_r, 3 * j + 2 * i + 1)
                    sp.dma_start(swp[i][0:P:2, par, :], raw[i][1:P:2, par, :]).then_inc(s_swap[par][i], 16)
                    sp.dma_start(swp[i][1:P:2, par, :], raw[i][0:P:2, par, :]).then_inc(s_swap[par][i], 16)

            def stack(j, par):
                for i in range(2):
                    sp.wait_ge(s_hi, 2 * j + i + 1)
                    for x in range(2):
                        for dst in ((k_hh[0:DH], k_hh[DH:P]), (q_hl[0:DH],))[i]:
                            sp.dma_start(dst[:, par, x, :], hi[i][DH * x:DH * x + DH, par, :]).then_inc(s_stack[par][i], 16)
                    sp.wait_ge(s_lo, 2 * j + i + 1)
                    for x in range(2):
                        dst = (k_lo, q_hl[DH:P])[i]
                        sp.dma_start(dst[:, par, x, :], lo[i][DH * x:DH * x + DH, par, :]).then_inc(s_stack[par][i], 16)

            sp.dma_start(bo_row[:, 0, :], bo.partition_broadcast(P)).then_inc(s_bo, 16)
            sp.dma_start(ident[:], consts["identity"]).then_inc(s_ident, 16)
            swap(0, 0)
            swap(1, 1)
            stack(0, 0)
            stack(1, 1)
            swap(2, 0)
            for b in range(B):
                if b >= 1:
                    sp.wait_ge(s_out, 16 * b)
                sp.dma_start(xr[:], x_v[b]).then_inc(s_x, 16)
                with sp.Fori(0, PAIRS // 2) as pp:
                    for par in range(2):
                        g = b * PAIRS + pp * 2 + par
                        sp.wait_ge(s_sc_w, 2 * (g + 1))
                        stack(g + 2, par)
                        swap(g + 3, 1 - par)
                sp.wait_ge(s_yr, 1 + TT * b + TT)
                sp.dma_start(y_v[b], xr[:]).then_inc(s_out, 16)
            sp.wait_ge(s_out, 16 * B)
            for par in range(2):
                for i in range(2):
                    sp.wait_ge(s_swap[par][i], 32 * (B * PAIRS // 2 + 2 - par))
                    sp.wait_ge(s_stack[par][i], (96, 64)[i] * (B * PAIRS // 2 + 1))

        @block.gpsimd
        def _(pool):
            def rotate(j, par, used=None):
                if used is not None:
                    pool.wait_ge(s_lo, used)
                for i in range(2):
                    pool.wait_ge(s_kq_r, 3 * j + 2 * i + 1)
                    pool.tensor_tensor(rot[i][:, par, :], raw[i][:, par, :], ropeC[:, 0:width[i]],
                                       ALU.mult).then_inc(s_cos, 1)
                for i in range(2):
                    pool.wait_ge(s_swap[par][i], 32 * (j >> 1) + 32)
                    pool.tensor_tensor(swp[i][:, par, :], swp[i][:, par, :], ropeS[:, 0:width[i]],
                                       ALU.mult).then_inc(s_sin, 1)

            def normalise(j, par):
                pool.wait_ge(s_inv, 2 * j + 2)
                pool.tensor_tensor(e[:, par, 1], e[:, par, 1],
                                   inv[:, par, 1, :].rearrange("p (t a) -> p t a", a=1).broadcast_to([P, TT, M]),
                                   ALU.mult).then_inc(s_prob1, 1)

            rotate(0, 0)
            rotate(1, 1)
            rotate(2, 0, 4)
            normalise(0, 0)
            with pool.Fori(0, B * PAIRS // 2) as gg:
                for par in range(2):
                    g = gg * 2 + par
                    rotate(g + 3, 1 - par, 2 * (g + 2))
                    normalise(g + 1, 1 - par)

        @block.tensor
        def _(pe):
            def project_v(j):
                b, cols = pair_at(j)
                split_product(pe, ps_turn[0][0:M, 0:P], range(KD), cT, wv, lambda k: (slice(None), b, k, slice(0, M)),
                              lambda k: (slice(None), k, cols)).then_inc(s_v_w, 1)

            def project_k(j):
                b, cols = pair_at(j)
                split_product(pe, ps_turn[1][:, 0:M], range(KD), wk, cT, lambda k: (slice(None), k, cols),
                              lambda k: (slice(None), b, k, slice(0, M))).then_inc(s_kq_w, 1)

            def project_q(j, c):
                b, cols = pair_at(j)
                split_product(pe, ps_turn[c][:, :], range(KD), wq, xT, lambda k: (slice(None), k, cols),
                              lambda k: (slice(None), b, k, slice(c * HALF, (c + 1) * HALF))).then_inc(s_kq_w, 1)

            def scores(par, x):
                for t in range(TT):
                    ts = slice(t * P, (t + 1) * P)
                    pe.matmul(ps_sc[:, t, 0:M], q_hl[:, par, x, ts], k_hh[:, par, x, :], start=True, stop=False)
                    ins = pe.matmul(ps_sc[:, t, 0:M], q_hl[0:DH, par, x, ts], k_lo[:, par, x, :], start=False, stop=True)
                ins.then_inc(s_sc_w, 1)

            def transposes(par, x):
                for t in range(TT):
                    ins = pe.transpose(ps_pt[0:M, t * P:(t + 1) * P], e[:, par, x, t, :], ident[:, :])
                ins.then_inc(s_pt_w, 1)

            project_k(0)
            project_q(0, 0)
            pe.wait_ge(s_kq_r, 1)
            project_q(0, 1)
            for j in (1, 2):
                pe.wait_ge(s_kq_r, 3 * j)
                project_k(j)
                project_q(j, 0)
                pe.wait_ge(s_kq_r, 3 * j + 1)
                project_q(j, 1)
            pe.wait_ge(s_kq_r, 8)
            project_v(0)
            for i in range(2):
                pe.wait_ge(s_stack[0][i], (96, 64)[i])
            scores(0, 0)
            pe.wait_ge(s_sc_r, 1)
            scores(0, 1)
            pe.wait_ge(s_ident, 16)
            pe.sem_inc(s_pv, 1)

            def values(g, par):
                pe.wait_ge(s_ot, 1 + g)
                pe.wait_ge(s_pt_r, 1 + 2 * g + 2)
                for c in range(2):
                    for x in range(2):
                        cs = slice(c * HALF, (c + 1) * HALF)
                        ins = pe.matmul(ps_o[DH * x:DH * x + DH, cs], v_pair[:, par, DH * x:DH * x + DH],
                                        pT[:, x, cs], start=True, stop=True)
                ins.then_inc(s_pv, 1)

            def iteration(b, g, par, first=False):
                for i in range(2):
                    pe.wait_ge(s_stack[1 - par][i], (96, 64)[i] * (((g + 1) >> 1) + 1))
                pe.wait_ge(s_sc_r, 2 * (g + 1))
                scores(1 - par, 0)
                if not first:
                    values(g - 1, 1 - par)
                pe.wait_ge(s_yr, 1 + TT * b)
                pe.wait_ge(s_pt_r, 1 + 2 * g)
                pe.wait_ge(s_prob0, g + 1)
                transposes(par, 0)
                pe.wait_ge(s_kq_r, 3 * (g + 3) - 1)
                project_v(g + 1)
                pe.wait_ge(s_kq_r, 3 * (g + 3))
                project_k(g + 3)
                pe.wait_ge(s_sc_r, 2 * (g + 1) + 1)
                scores(1 - par, 1)
                pe.wait_ge(s_v_r, g + 2)
                project_q(g + 3, 0)
                pe.wait_ge(s_kq_r, 3 * (g + 3) + 1)
                project_q(g + 3, 1)
                pe.wait_ge(s_pt_r, 1 + 2 * g + 1)
                pe.wait_ge(s_prob1, g + 1)
                transposes(par, 1)

            with pe.Fori(0, B) as b:
                iteration(b, b * PAIRS, 0, first=True)
                with pe.Fori(0, PAIRS // 2 - 1) as pp:
                    iteration(b, b * PAIRS + pp * 2 + 1, 1)
                    iteration(b, b * PAIRS + pp * 2 + 2, 0)
                iteration(b, b * PAIRS + PAIRS - 1, 1)
                values(b * PAIRS + PAIRS - 1, 1)
                pe.wait_ge(s_kq_r, 3 * (b * PAIRS + PAIRS + 3))
                output_projection(pe, o_hi, o_lo, wo, ps_y, s_y, s_yr, b, s_ot, 1)

        @block.scalar
        def _(act):
            def evacuate_kq(j, par, n):
                act.wait_ge(s_kq_w, 3 * j + n + 1)
                if n == 0:
                    dst, src = raw[0][:, par, :], ps_turn[1][:, 0:M]
                else:
                    dst, src = raw[1][:, par, (n - 1) * HALF:n * HALF], ps_turn[n - 1][:, :]
                act.activation(dst, src, ACT.Copy, scale=1.0 / WS).then_inc(s_kq_r, 1)

            def evacuate_v(j, par):
                act.wait_ge(s_v_w, j + 1)
                act.activation(v_pair[:, par, :], ps_turn[0][0:M, 0:P], ACT.Copy, scale=1.0 / WS).then_inc(s_v_r, 1)

            def high(j, par, i):
                act.wait_ge(s_rot, 2 * j + i + 1)
                act.activation(hi[i][:, par, :], rot[i][:, par, :], ACT.Copy).then_inc(s_hi, 1)

            def exponentials(j, par, x):
                act.wait_ge(s_sc_r, 2 * j + x + 1)
                act.activation(e[:, par, x], e[:, par, x], ACT.Exp, scale=float(DH) ** -0.5).then_inc(s_e, 1)

            def untranspose(g, x):
                act.wait_ge(s_pt_w, 2 * g + x + 1)
                act.activation(pT[:, x, :], ps_pt[0:M, :], ACT.Copy).then_inc(s_pt_r, 1)

            act.sem_inc(s_pt_r, 1)
            for n in range(3):
                evacuate_kq(0, 0, n)
            for n in range(3):
                evacuate_kq(1, 1, n)
            high(0, 0, 0)
            high(0, 0, 1)
            act.wait_ge(s_lo, 2)
            for n in range(3):
                evacuate_kq(2, 0, n)
            evacuate_v(0, 0)
            high(1, 1, 0)
            high(1, 1, 1)
            exponentials(0, 0, 0)
            exponentials(0, 0, 1)

            def split_output(g, p):
                act.wait_ge(s_pv, 1 + g + 1)
                act.activation(o_hi[:, p, :], ps_o[:], ACT.Copy).then_inc(s_ohi, 1)

            def iteration(g, p, par, first=False):
                if not first:
                    split_output(g - 1, p - 1)
                act.wait_ge(s_pv, 1 + g)
                untranspose(g, 0)
                evacuate_v(g + 1, 1 - par)
                act.wait_ge(s_lo, 2 * (g + 2))
                evacuate_kq(g + 3, 1 - par, 0)
                exponentials(g + 1, 1 - par, 0)
                for i in range(2):
                    act.wait_ge(s_stack[par][i], (96, 64)[i] * ((g >> 1) + 1))
                    high(g + 2, par, i)
                evacuate_kq(g + 3, 1 - par, 1)
                exponentials(g + 1, 1 - par, 1)
                evacuate_kq(g + 3, 1 - par, 2)
                untranspose(g, 1)

            with act.Fori(0, B) as b:
                iteration(b * PAIRS, 0, 0, first=True)
                with act.Fori(0, PAIRS // 2 - 1) as pp:
                    iteration(b * PAIRS + pp * 2 + 1, pp * 2 + 1, 1)
                    iteration(b * PAIRS + pp * 2 + 2, pp * 2 + 2, 0)
                iteration(b * PAIRS + PAIRS - 1, PAIRS - 1, 1)
                split_output(b * PAIRS + PAIRS - 1, PAIRS - 1)

        @block.vector
        def _(dve):
            def rotated(j, par, i):
                dve.wait_ge(s_sin, 2 * j + i + 1)
                dve.wait_ge(s_cos, 2 * j + i + 1)
                dve.tensor_tensor(rot[i][:, par, :], rot[i][:, par, :], swp[i][:, par, :], ALU.add).then_inc(s_rot, 1)

            def low(j, par, i):
                dve.wait_ge(s_hi, 2 * j + i + 1)
                dve.tensor_tensor(lo[i][:, par, :], rot[i][:, par, :], hi[i][:, par, :], ALU.subtract).then_inc(s_lo, 1)

            def shift(j, par, x):
                dve.wait_ge(s_sc_w, 2 * j + x + 1)
                dve.reduce_max(mx[:, x, :], ps_sc[:, :, 0:M], AX_X).then_inc(s_mx, 1)
                dve.wait_ge(s_mx, 2 * j + x + 1)
                dve.tensor_tensor(e[:, par, x], ps_sc[:, :, 0:M],
                                  mx[:, x, :].rearrange("p (t a) -> p t a", a=1).broadcast_to([P, TT, M]),
                                  ALU.subtract).then_inc(s_sc_r, 1)

            def totals(j, par, x):
                dve.wait_ge(s_e, 2 * j + x + 1)
                dve.reduce_sum(total[:, x, :], e[:, par, x], AX_X).then_inc(s_total, 1)
                dve.wait_ge(s_total, 2 * j + x + 1)
                dve.reciprocal(inv[:, par, x, :], total[:, x, :]).then_inc(s_inv, 1)
                if x == 0:
                    dve.wait_ge(s_inv, 2 * j + 1)
                    dve.tensor_tensor(e[:, par, 0], e[:, par, 0],
                                      inv[:, par, 0, :].rearrange("p (t a) -> p t a", a=1).broadcast_to([P, TT, M]),
                                      ALU.mult).then_inc(s_prob0, 1)

            dve.sem_inc(s_ot, 1)
            dve.sem_inc(s_yr, 1)
            for j in range(2):
                for i in range(2):
                    rotated(j, j, i)
                for i in range(2):
                    low(j, j, i)
            shift(0, 0, 0)
            shift(0, 0, 1)
            totals(0, 0, 0)
            totals(0, 0, 1)
            dve.wait_ge(s_bo, 16)

            def split_output(g, p):
                dve.wait_ge(s_ohi, g + 1)
                dve.tensor_tensor(o_lo[:, p, :], ps_o[:], o_hi[:, p, :], ALU.subtract).then_inc(s_ot, 1)

            def iteration(g, p, par, first=False):
                shift(g + 1, 1 - par, 0)
                if not first:
                    split_output(g - 1, p - 1)
                rotated(g + 2, par, 0)
                rotated(g + 2, par, 1)
                shift(g + 1, 1 - par, 1)
                for i in range(2):
                    dve.wait_ge(s_stack[par][i], (96, 64)[i] * ((g >> 1) + 1))
                    low(g + 2, par, i)
                totals(g + 1, 1 - par, 0)
                totals(g + 1, 1 - par, 1)

            with dve.Fori(0, B) as b:
                dve.wait_ge(s_x, 16 * b + 16)
                dve.tensor_tensor(xr[:], xr[:], bo_row[:].broadcast_to([P, TT, D]), ALU.add).then_inc(s_xb, 1)
                iteration(b * PAIRS, 0, 0, first=True)
                with dve.Fori(0, PAIRS // 2 - 1) as pp:
                    iteration(b * PAIRS + pp * 2 + 1, pp * 2 + 1, 1)
                    iteration(b * PAIRS + pp * 2 + 2, pp * 2 + 2, 0)
                iteration(b * PAIRS + PAIRS - 1, PAIRS - 1, 1)
                split_output(b * PAIRS + PAIRS - 1, PAIRS - 1)
                dve.wait_ge(s_xb, b + 1)
                for t in range(TT):
                    dve.wait_ge(s_y, TT * b + t + 1)
                    dve.scalar_tensor_tensor(out=xr[:, t, :], in0=ps_y[t % 4], scalar=1.0 / WS, in1=xr[:, t, :],
                                             op0=ALU.mult, op1=ALU.add).then_inc(s_yr, 1)


def feed_forward(nc, tag, x_src, x_dst, b1, b2, xT, w1, w2):
    with ExitStack() as ctx:
        def sb(name, shape, dt=F32):
            return ctx.enter_context(nc.sbuf_tensor(f"{tag}_{name}", shape, dt))

        def sem(name):
            return ctx.enter_context(nc.semaphore(f"{tag}_{name}"))

        hid = sb("hid", [P, 2, N])
        h_hi = sb("h_hi", [P, KM, N], F16)
        h_lo = sb("h_lo", [P, KM, N], F16)
        xr = sb("xr", [P, 2, TT, D])
        b1_col = sb("b1_col", [P, KM])
        b2_row = sb("b2_row", [P, 1, D])
        ps_h = [ctx.enter_context(nc.psum_tensor(f"{tag}_ps_h{i}", [P, N], F32)) for i in range(2)]
        ps_y = [ctx.enter_context(nc.psum_tensor(f"{tag}_ps_y{i}", [P, HALF], F32)) for i in range(4)]
        s_b = sem("s_b")
        s_x = [sem("s_x0"), sem("s_x1")]
        s_xb = sem("s_xb")
        s_h = sem("s_h")
        s_g = sem("s_g")
        s_hi = sem("s_hi")
        s_lo = sem("s_lo")
        s_y = sem("s_y")
        s_yr = sem("s_yr")
        s_out = sem("s_out")
        block = ctx.enter_context(nc.Block())
        x_v = x_src.rearrange("b (t p) d -> b p t d", p=P)
        y_v = x_dst.rearrange("b (t p) d -> b p t d", p=P)

        @block.sync
        def _(sp):
            sp.dma_start(b1_col[:], b1.rearrange("(k p) -> p k", p=P),
                         allow_slow_non_contiguous=True).then_inc(s_b, 16)
            sp.dma_start(b2_row[:, 0, :], b2.partition_broadcast(P)).then_inc(s_b, 16)
            sp.dma_start(xr[:, 0], x_v[0]).then_inc(s_x[0], 16)
            for b in range(B):
                if b + 1 < B:
                    if b >= 1:
                        sp.wait_ge(s_out, 16 * b)
                    sp.dma_start(xr[:, 1 - b % 2], x_v[b + 1]).then_inc(s_x[1 - b % 2], 16)
                sp.wait_ge(s_yr, 1 + TT * b + TT)
                sp.dma_start(y_v[b], xr[:, b % 2]).then_inc(s_out, 16)
            sp.wait_ge(s_out, 16 * B)

        @block.tensor
        def _(pe):
            with pe.Fori(0, B) as b:
                for m in range(KM):
                    n = KM * b + m
                    if m >= 2:
                        pe.wait_ge(s_g, 1 + n - 1)
                    else:
                        pe.wait_ge(s_g, 1 + KM * b)
                    for c in range(2):
                        cs, ms = slice(c * HALF, (c + 1) * HALF), slice(m * P, (m + 1) * P)
                        ins = split_product(pe, ps_h[m % 2][:, cs], range(KD), w1, xT, lambda k, ms=ms: (slice(None), k, ms),
                                            lambda k, cs=cs: (slice(None), b, k, cs))
                    ins.then_inc(s_h, 1)
                pe.wait_ge(s_yr, 1 + TT * b)
                output_projection(pe, h_hi, h_lo, w2, [t[:, 0:D] for t in ps_y], s_y, s_yr, b, s_lo, 1)

        @block.scalar
        def _(act):
            act.sem_inc(s_g, 1)
            act.wait_ge(s_b, 32)
            with act.Fori(0, B) as b:
                for m in range(KM):
                    act.wait_ge(s_h, KM * b + m + 1)
                    if m >= 2:
                        act.wait_ge(s_lo, 1 + KM * b + m - 1)
                    act.activation(hid[:, m % 2, :], ps_h[m % 2][:, :], ACT.Gelu, bias=b1_col[:, m:m + 1],
                                   scale=1.0 / WS).then_inc(s_g, 1)

        @block.vector
        def _(dve):
            dve.sem_inc(s_yr, 1)
            dve.sem_inc(s_lo, 1)
            dve.wait_ge(s_b, 32)
            with dve.Fori(0, B // 2) as bb:
                for par in range(2):
                    b = bb * 2 + par
                    dve.wait_ge(s_x[par], 16 * bb + 16)
                    dve.tensor_tensor(xr[:, par], xr[:, par], b2_row[:].broadcast_to([P, TT, D]),
                                      ALU.add).then_inc(s_xb, 1)
                    for m in range(KM):
                        n = KM * b + m + 1
                        dve.wait_ge(s_g, 1 + n)
                        dve.tensor_copy(h_hi[:, m, :], hid[:, m % 2, :]).then_inc(s_hi, 1)
                        dve.wait_ge(s_hi, n)
                        dve.tensor_tensor(h_lo[:, m, :], hid[:, m % 2, :], h_hi[:, m, :],
                                          ALU.subtract).then_inc(s_lo, 1)
                    dve.wait_ge(s_xb, b + 1)
                    for t in range(TT):
                        dve.wait_ge(s_y, TT * b + t + 1)
                        dve.scalar_tensor_tensor(out=xr[:, par, t, :], in0=ps_y[t % 4][:, 0:D], scalar=1.0 / WS,
                                                 in1=xr[:, par, t, :], op0=ALU.mult, op1=ALU.add).then_inc(s_yr, 1)


def load_constants(nc, consts, cosines, sines):
    with ExitStack() as ctx:
        ident = ctx.enter_context(nc.sbuf_tensor("const_ident", [P, P], F32))
        s_load = ctx.enter_context(nc.semaphore("const_load"))
        s_made = ctx.enter_context(nc.semaphore("const_made"))
        block = ctx.enter_context(nc.Block())

        @block.sync
        def _(sp):
            sp.dma_start(ident[:], consts["identity"]).then_inc(s_load, 16)
            sp.dma_start(consts["ropeC"][:], cosines).then_inc(s_load, 16)
            sp.dma_start(consts["ropeS"][:], sines).then_inc(s_load, 16)
            sp.wait_ge(s_load, 48)

        @block.vector
        def _(dve):
            dve.memset(consts["ones32"][:], 1.0).then_inc(s_made, 1)
            dve.wait_ge(s_load, 48)
            dve.tensor_copy(consts["ident16"][:], ident[:]).then_inc(s_made, 1)


def program(nc, a, identity, cosines, sines, out):
    with ExitStack() as top:
        def keep(name, shape, dt=F32):
            return top.enter_context(nc.sbuf_tensor(name, shape, dt))

        consts = {"identity": identity, "ident16": keep("ident16", [P, P], F16),
                  "ropeC": keep("ropeC", [P, N]), "ropeS": keep("ropeS", [P, N]), "ones32": keep("ones32", [P, DH])}
        x1 = nc.dram_tensor("x_after_self", (B, N, D), F32, kind="Internal").ap()
        x2 = nc.dram_tensor("x_after_cross", (B, N, D), F32, kind="Internal").ap()
        xT = (keep("xT_hi", [P, B, KD, N], F16), keep("xT_lo", [P, B, KD, N], F16))
        load_constants(nc, consts, cosines, sines)

        def units(src, pair, width):
            hi, lo = pair
            rows = src.shape[0]
            if width == N:
                return [(src[k * P:min(rows, (k + 1) * P), :], hi[:, k, :], lo[:, k, :]) for k in range(-(-rows // P))]
            n = N // width
            return [(src[k * P:(k + n) * P, :].rearrange("(k p) n -> p k n", p=P),
                     hi[:, k:k + n, :].rearrange("p k n -> p (k n)"), lo[:, k:k + n, :].rearrange("p k n -> p (k n)"))
                    for k in range(0, rows // P, n)]

        def split_pair(ctx, name, k, width):
            return tuple(ctx.enter_context(nc.sbuf_tensor(f"{name}_{part}", [P, k, width], F16)) for part in ("hi", "lo"))

        norm1 = [a[n] for n in ("ln1_w", "ln1_b", "g1_w", "g1_b", "b1_w", "b1_b")]
        norm2 = [a[n] for n in ("ln2_w", "ln2_b", "g2_w", "g2_b", "b2_w", "b2_b")]
        for tag, src in (("sa", a["x"]), ("ca", x1)):
            with ExitStack() as ctx:
                wq, wk, wv = (split_pair(ctx, f"{tag}_{n}", KD, MID) for n in ("wq", "wk", "wv"))
                wo = split_pair(ctx, f"{tag}_wo", KM, D)
                wkv = a[f"{tag}_wkv"]
                pieces = units(a[f"{tag}_wq"], wq, MID) + units(wkv[:, 0:MID], wk, MID)
                pieces += units(wkv[:, MID:2 * MID], wv, MID) + units(a[f"{tag}_wo"], wo, D)
                if tag == "sa":
                    prepare(nc, "sap", consts, src, a["cond_1024"], norm1, pieces, *xT)
                    self_attention(nc, consts, src, x1, a["sa_bo"], xT, wq, wk, wv, wo)
                else:
                    cT = tuple(ctx.enter_context(nc.sbuf_tensor(f"cT_{part}", [P, B, KD, M], F16))
                               for part in ("hi", "lo"))
                    prepare(nc, "cap", consts, src, a["cond_1024"], norm1, pieces, *xT,
                            context=(a["ctx_768"], a["ca_lnc_w"], a["ca_lnc_b"], *cT))
                    cross_attention(nc, consts, src, x2, a["ca_bo"], xT, cT, wq, wk, wv, wo)
        with ExitStack() as ctx:
            w1 = split_pair(ctx, "w1", KD, HID)
            w2 = split_pair(ctx, "w2", KM, D)
            pieces = units(a["ff_w1"], w1, HID) + units(a["ff_w2"], w2, D)
            prepare(nc, "ffp", consts, x2, a["cond_1024"], norm2, pieces, *xT)
            feed_forward(nc, "ff", x2, out, a["ff_b1"], a["ff_b2"], xT, w1, w2)


def rope_tables():
    inv = (np.float32(1.0) / np.float32(10000.0) ** (np.arange(0, DH, 2, dtype=np.float32) / np.float32(DH)))
    ang = inv.astype(np.float32)[:, None] * np.arange(N, dtype=np.float32)[None, :]
    rows = np.arange(P) % DH // 2
    sign = np.where(np.arange(P) % 2 == 0, -1.0, 1.0).astype(np.float32)[:, None]
    return np.cos(ang)[rows].astype(np.float32), (np.sin(ang)[rows] * sign).astype(np.float32)


def kernel(**inputs):
    from concourse import bacc
    from concourse.bass_utils import run_bass_kernel_spmd

    nc = bacc.Bacc("TRN2", target_bir_lowering=False, num_devices=1)
    cosines, sines = rope_tables()
    arrays = {name: np.ascontiguousarray(v) for name, v in inputs.items()}
    arrays |= {"identity": np.eye(P, dtype=np.float32), "rope_cos": cosines, "rope_sin": sines}
    aps = {name: nc.dram_tensor(f"in_{name}", v.shape, mybir.dt.from_np(v.dtype), kind="ExternalInput").ap()
           for name, v in arrays.items()}
    out = nc.dram_tensor("out_x", (B, N, D), F32, kind="ExternalOutput").ap()
    a = {name.removeprefix("L0_xcond_"): ap for name, ap in aps.items()}
    program(nc, a, aps["identity"], aps["rope_cos"], aps["rope_sin"], out)
    r = run_bass_kernel_spmd(nc, [{f"in_{name}": v for name, v in arrays.items()}], core_ids=[0])
    return r.results[0]["out_x"]
```

```python
from contextlib import ExitStack

import numpy as np

import concourse.bass as bass
from concourse import mybir

F32 = mybir.dt.float32
F16 = mybir.dt.float16
ALU = mybir.AluOpType
ACT = mybir.ActivationFunctionType
AX_X = mybir.AxisListType.X

P = 128
B, N, D = 4, 1024, 256
M, DC = 77, 192
H, DH = 16, 64
MID = H * DH
HID = 4 * D
PAIRS = H // 2
TT = N // P
KD = D // P
KM = MID // P
HALF = N // 2
DH2 = 2 * DH
EPS = 1e-5
WS = 64.0
MS = 64.0




def clear_semaphores(nc, sems):
    nc.all_engine_barrier()
    nc.clear_and_free_semaphores(sems)
    nc.all_engine_barrier()


def prepare(nc, tag, consts, x_src, cond, norm, weights, xT_hi, xT_lo, context=None):
    lnw, lnb, gw, gb, bw, bb = norm
    with ExitStack() as ctx:
        def sb(name, shape, dt=F32):
            return ctx.enter_context(nc.sbuf_tensor(f"{tag}_{name}", shape, dt))

        sems = []
        ctx.callback(clear_semaphores, nc, sems)

        def sem(name):
            sems.append(nc.alloc_semaphore(f"{tag}_{name}"))
            return sems[-1]

        short = [n for n, w in enumerate(weights) if w[0].shape[0] < P]
        units = weights
        staged = sb("staged", [P, len(units), N])
        xs = sb("xs", [P, B, TT, D])
        xh = sb("xh", [P, 2, TT, D])
        rows = sb("rows", [P, 4, D])
        condT = sb("condT", [P, KD, B])
        cond_wide = sb("cond_wide", [P, KD, B, P])
        gates = sb("gates", [P, 2, KD, D])
        ones = sb("ones", [P, P])
        ident = sb("ident", [P, P])
        gam = sb("gam", [P, B, D])
        bet = sb("bet", [P, B, D])
        tmp = sb("tmp", [P, B, 2, D])
        tiles = B * TT
        cols = tiles + (B if context is not None else 0)
        stats = sb("stats", [P, cols, 6])
        mv = sb("mv", [P, cols, 2])
        var = sb("var", [P, cols])
        root = sb("root", [P, cols])
        rstd = sb("rstd", [P, cols])
        newton = sb("newton", [P, cols])
        ps_gate = [ctx.enter_context(nc.psum_tensor(f"{tag}_gate{i}", [P, 2, D], F32)) for i in range(4)]
        ps_t = [ctx.enter_context(nc.psum_tensor(f"{tag}_t{i}", [P, HALF], F32)) for i in range(4)]

        s_ident = sem("s_ident")
        s_par = sem("s_par")
        s_w = sem("s_w")
        s_x = [sem(f"s_x{b}") for b in range(B)]
        s_ones = sem("s_ones")
        s_zero = sem("s_zero")
        s_wide = sem("s_wide")
        s_gate = sem("s_gate")
        s_tab = sem("s_tab")
        s_whi = sem("s_whi")
        s_wlo = sem("s_wlo")
        s_stat = sem("s_stat")
        s_root = sem("s_root")
        s_xc = sem("s_xc")
        s_xn = sem("s_xn")
        s_xb = sem("s_xb")
        s_tr = sem("s_tr")
        s_hi = sem("s_hi")
        s_lo = sem("s_lo")
        if context is not None:
            c_src, c_w, c_b, cT_hi, cT_lo = context
            cs = sb("cs", [M, B, DC])
            crow = sb("crow", [M, 2, DC])
            s_c = sem("s_c")
            s_cn = sem("s_cn")
            s_ct = sem("s_ct")
            s_chi = sem("s_chi")
            s_clo = sem("s_clo")
            c_parts = [(k, (P, DC - P)[k], ps_gate[k].rearrange("p a d -> p (a d)")[0:(P, DC - P)[k], 0:B * M])
                       for k in range(2)]
        block = ctx.enter_context(nc.Block())

        @block.sync
        def _(sp):
            x_v = x_src.rearrange("b (t p) d -> b p t d", p=P)
            sp.dma_start(ident[:], consts["identity"]).then_inc(s_ident, 16)
            sp.dma_start(xs[:, 0], x_v[0]).then_inc(s_x[0], 16)
            for k in range(KD):
                sp.dma_start(condT[:, k, :], cond[:, k * P:(k + 1) * P].rearrange("b p -> p b"),
                             allow_slow_non_contiguous=True).then_inc(s_par, 16)
            for i, w in enumerate((gw, bw)):
                sp.dma_start(gates[:, i], w.rearrange("(k p) n -> p k n", p=P)).then_inc(s_par, 16)
            for i, v in enumerate((lnw, lnb, gb, bb)):
                sp.dma_start(rows[:, i, :], v.partition_broadcast(P)).then_inc(s_par, 16)
            for b in range(1, B):
                sp.dma_start(xs[:, b], x_v[b]).then_inc(s_x[b], 16)
            if context is not None:
                sp.dma_start(cs[:], c_src.rearrange("b m d -> m b d")).then_inc(s_c, 16)
                sp.dma_start(crow[:, 0, :], c_w.partition_broadcast(M)).then_inc(s_c, 16)
                sp.dma_start(crow[:, 1, :], c_b.partition_broadcast(M)).then_inc(s_c, 16)
            if short:
                sp.wait_ge(s_zero, 1)
            for n, (src, _, _) in enumerate(units):
                dst = staged[0:src.shape[0], n, :]
                if len(src.shape) == 3:
                    dst = dst.rearrange("p (a b) -> p a b", b=src.shape[2])
                sp.dma_start(dst, src).then_inc(s_w, 16)

        @block.gpsimd
        def _(pool):
            if context is not None:
                pool.memset(mv[:, tiles:cols, :], 1.0)
            pool.memset(ones[:], 1.0).then_inc(s_ones, 1)
            for n in short:
                ins = pool.memset(staged[:, n, :], 0.0)
            if short:
                ins.then_inc(s_zero, 1)
            pool.wait_ge(s_tab, 5 * B)
            for b in range(B):
                pool.wait_ge(s_xn, b + 1)
                pool.tensor_tensor(xh[:, b % 2], xh[:, b % 2], bet[:, b:b + 1, :].broadcast_to([P, TT, D]),
                                   ALU.add).then_inc(s_xb, 1)

        @block.scalar
        def _(act):
            act.wait_ge(s_stat, 3)
            act.activation(root[:], var[:], ACT.Sqrt).then_inc(s_root, 1)
            act.wait_ge(s_w, 16 * len(units))
            for n in range(len(units)):
                if context is not None and n == len(units) // 2:
                    for k, rows_k, src in c_parts:
                        act.wait_ge(s_ct, k + 1)
                        act.activation(cT_hi[0:rows_k, :, k, :], src.rearrange("p (b m) -> p b m", m=M),
                                       ACT.Copy).then_inc(s_chi, 1)
                act.activation(units[n][1], staged[:, n, :], ACT.Copy, scale=WS).then_inc(s_whi, 1)
            for b in range(B):
                for n in range(4):
                    k, h = n // 2, n % 2
                    act.wait_ge(s_tr, 4 * b + n + 1)
                    act.activation(xT_hi[:, b, k, h * HALF:(h + 1) * HALF], ps_t[n][:, :],
                                   ACT.Copy).then_inc(s_hi, 1)

        @block.tensor
        def _(pe):
            pe.wait_ge(s_ident, 16)
            if context is not None:
                pe.wait_ge(s_cn, 3)
                for k, rows_k, dst in c_parts:
                    for b in range(B):
                        ins = pe.transpose(dst[:, b * M:(b + 1) * M], cs[:, b, k * P:k * P + rows_k], ident[0:M, 0:M])
                    ins.then_inc(s_ct, 1)
                pe.wait_ge(s_clo, 2)
            pe.wait_ge(s_par, 16 * 8)
            pe.wait_ge(s_wide, 1)
            for b in range(B):
                for i in range(2):
                    for k in range(KD):
                        ins = pe.matmul(ps_gate[b][:, i, :], cond_wide[:, k, b, :], gates[:, i, k, :],
                                        start=(k == 0), stop=(k == KD - 1))
                ins.then_inc(s_gate, 1)
            for b in range(B):
                pe.wait_ge(s_xb, b + 1)
                for n in range(4):
                    k, h = n // 2, n % 2
                    if b >= 1:
                        pe.wait_ge(s_lo, 4 * (b - 1) + n + 1)
                    for q in range(4):
                        ins = pe.transpose(ps_t[n][:, q * P:(q + 1) * P], xh[:, b % 2, 4 * h + q, k * P:(k + 1) * P],
                                           ident[:, :])
                    ins.then_inc(s_tr, 1)

        @block.vector
        def _(dve):
            if context is not None:
                dve.memset(cT_hi[DC - P:P, :, 1, :], 0.0)
                dve.memset(cT_lo[DC - P:P, :, 1, :], 0.0)
            dve.wait_ge(s_par, 16 * 8)
            dve.wait_ge(s_ones, 1)
            for k in range(KD):
                for b in range(B):
                    ins = dve.tensor_scalar(cond_wide[:, k, b, :], ones[:, :], condT[:, k, b:b + 1], None, ALU.mult)
            ins.then_inc(s_wide, 1)
            for b in range(B):
                dve.wait_ge(s_x[b], 16)
                for t in range(TT):
                    ins = dve.bn_stats(stats[:, b * TT + t, :], xs[:, b, t, :])
            if context is not None:
                dve.wait_ge(s_c, 48)
                for b in range(B):
                    ins = dve.bn_stats(stats[0:M, tiles + b, :], cs[:, b, :])
            ins.then_inc(s_stat, 1)
            dve.wait_ge(s_stat, 1)
            for n in range(cols):
                rows_n = P if n < tiles else M
                ins = dve.bn_aggr(mv[0:rows_n, n, :], stats[0:rows_n, n, :])
            ins.then_inc(s_stat, 1)
            dve.wait_ge(s_stat, 2)
            dve.tensor_scalar(var[:], mv[:, :, 1], EPS, None, ALU.add).then_inc(s_stat, 1)
            dve.wait_ge(s_root, 1)
            dve.reciprocal(rstd[:], root[:]).then_inc(s_stat, 1)
            dve.wait_ge(s_stat, 4)
            dve.tensor_tensor(newton[:], rstd[:], rstd[:], ALU.mult).then_inc(s_stat, 1)
            dve.wait_ge(s_stat, 5)
            dve.scalar_tensor_tensor(out=newton[:], in0=newton[:], scalar=-0.5, in1=var[:], op0=ALU.mult,
                                     op1=ALU.mult).then_inc(s_stat, 1)
            dve.wait_ge(s_stat, 6)
            dve.scalar_tensor_tensor(out=rstd[:], in0=newton[:], scalar=1.5, in1=rstd[:], op0=ALU.add,
                                     op1=ALU.mult).then_inc(s_stat, 1)
            dve.wait_ge(s_stat, 7)
            if context is not None:
                for b in range(B):
                    n = tiles + b
                    ins = dve.tensor_scalar(cs[:, b, :], cs[:, b, :], mv[0:M, n, 0:1], rstd[0:M, n:n + 1],
                                            ALU.subtract, ALU.mult)
                ins.then_inc(s_cn, 1)
                dve.wait_ge(s_cn, 1)
                dve.tensor_tensor(cs[:], cs[:], crow[:, 0:1, :].broadcast_to([M, B, DC]), ALU.mult).then_inc(s_cn, 1)
                dve.wait_ge(s_cn, 2)
                dve.tensor_tensor(cs[:], cs[:], crow[:, 1:2, :].broadcast_to([M, B, DC]), ALU.add).then_inc(s_cn, 1)

            def tokens(b):
                if b >= 2:
                    dve.wait_ge(s_tr, 4 * (b - 1))
                for t in range(TT):
                    n = b * TT + t
                    ins = dve.tensor_scalar(xh[:, b % 2, t, :], xs[:, b, t, :], mv[:, n, 0:1], rstd[:, n:n + 1],
                                            ALU.subtract, ALU.mult)
                ins.then_inc(s_xc, 1)
                dve.wait_ge(s_xc, b + 1)
                if b == 0:
                    dve.wait_ge(s_tab, 5 * B)
                dve.tensor_tensor(xh[:, b % 2], xh[:, b % 2], gam[:, b:b + 1, :].broadcast_to([P, TT, D]),
                                  ALU.mult).then_inc(s_xn, 1)

            def tokens_lo(b):
                for n in range(4):
                    k, h = n // 2, n % 2
                    dve.wait_ge(s_hi, 4 * b + n + 1)
                    dve.tensor_tensor(xT_lo[:, b, k, h * HALF:(h + 1) * HALF], ps_t[n][:, :],
                                      xT_hi[:, b, k, h * HALF:(h + 1) * HALF], ALU.subtract).then_inc(s_lo, 1)

            if context is not None:
                for k, rows_k, src in c_parts:
                    dve.wait_ge(s_chi, k + 1)
                    dve.tensor_tensor(cT_lo[0:rows_k, :, k, :], src.rearrange("p (b m) -> p b m", m=M),
                                      cT_hi[0:rows_k, :, k, :], ALU.subtract).then_inc(s_clo, 1)
            for b in range(B):
                dve.wait_ge(s_gate, b + 1)
                for i in range(2):
                    dve.tensor_tensor(tmp[:, b, i, :], ps_gate[b][:, i, :], rows[:, 2 + i, :], ALU.add).then_inc(s_tab, 1)
            for b in range(B):
                dve.wait_ge(s_tab, 2 * b + 2)
                for i, dst in enumerate((gam, bet)):
                    dve.scalar_tensor_tensor(out=dst[:, b, :], in0=tmp[:, b, 0, :], scalar=1.0, in1=rows[:, i, :],
                                             op0=ALU.add, op1=ALU.mult).then_inc(s_tab, 1)
            for b in range(B):
                dve.wait_ge(s_tab, 2 * B + 2 * b + 2)
                dve.tensor_tensor(bet[:, b, :], bet[:, b, :], tmp[:, b, 1, :], ALU.add).then_inc(s_tab, 1)
            for b in range(B):
                tokens(b)
                for n in range(b * len(units) // B, (b + 1) * len(units) // B):
                    dve.wait_ge(s_whi, n + 1)
                    _, w_hi, w_lo = units[n]
                    dve.scalar_tensor_tensor(out=w_lo, in0=staged[:, n, :], scalar=WS, in1=w_hi, op0=ALU.mult,
                                             op1=ALU.subtract).then_inc(s_wlo, 1)
                if b >= 1:
                    tokens_lo(b - 1)
            tokens_lo(B - 1)


def pair_at(j):
    if isinstance(j, int):
        return j // PAIRS % B, bass.ds(j % PAIRS * P, P)
    return (j >> 3) & (B - 1), bass.ds((j & (PAIRS - 1)) * P, P)


def split_product(pe, out, k_tiles, lhs, rhs, lhs_at, rhs_at, start=True, stop=True):
    terms = [(k, a, b) for k in k_tiles for a, b in ((0, 0), (1, 0), (0, 1))]
    for i, (k, a, b) in enumerate(terms):
        ins = pe.matmul(out, lhs[a][lhs_at(k)], rhs[b][rhs_at(k)], start=(start and i == 0),
                        stop=(stop and i == len(terms) - 1))
    return ins


def output_projection(pe, o_hi, o_lo, wo, ps_y, s_y, s_yr, b, s_ot, parts):
    o, last = (o_hi, o_lo), KM - 1

    def product(t, ks, start, stop):
        ts = slice(t * P, (t + 1) * P)
        return split_product(pe, ps_y[t % 4], ks, o, wo, lambda k: (slice(None), k, ts),
                             lambda k: (slice(None), k, slice(None)), start, stop)

    pe.wait_ge(s_ot, 1 + parts * (KM * b + last))
    for t in range(4):
        product(t, range(last), True, False)
    for t in range(4):
        if t == 0:
            pe.wait_ge(s_ot, 1 + parts * (KM * b + last) + 1)
        product(t, (last,), False, True).then_inc(s_y, 1)
    pe.wait_ge(s_ot, 1 + parts * KM * (b + 1))
    for t in range(4, TT):
        pe.wait_ge(s_yr, 1 + TT * b + t - 3)
        product(t, range(KM), True, True).then_inc(s_y, 1)


def self_attention(nc, consts, x_src, x_dst, bo, xT, wq, wk, wv, wo):
    NK = N // P
    MAXB = 4 * TT
    STEP_MAX = {1: range(0, 6), 2: range(6, 11), 3: range(11, 16), 4: range(16, 22), 5: range(22, 27),
                6: range(27, 32)}
    ident16, ropeC, ropeS, ones32 = consts["ident16"], consts["ropeC"], consts["ropeS"], consts["ones32"]
    with ExitStack() as ctx:
        def sb(name, shape, dt=F32):
            return ctx.enter_context(nc.sbuf_tensor(f"sa_{name}", shape, dt))

        def ps(name, shape):
            return ctx.enter_context(nc.psum_tensor(f"sa_{name}", shape, F32))

        def sem(name):
            return ctx.enter_context(nc.semaphore(f"sa_{name}"))

        q_hh = sb("q_hh", [P, 2, 2, N], F16)
        q_lm = sb("q_lm", [P, 2, 2, N], F16)
        k_hl = sb("k_hl", [P, 2, 2, N], F16)
        k_h1 = sb("k_h1", [P, 2, 2, N], F16)
        raw = sb("raw", [P, 2, N])
        swp = sb("swp", [P, 2, N])
        hi = sb("hi", [P, 2, N], F16)
        lo = sb("lo", [P, 2, N], F16)
        v_pair = sb("v_pair", [P, 2, NK, P])
        probs = sb("probs", [P, 2, 2, N])
        acc = sb("acc", [P, 2, N])
        inv = acc[:, 1, :]
        o_pair = sb("o_pair", [P, N])
        o_hi = sb("o_hi", [P, PAIRS, N], F16)
        o_lo = sb("o_lo", [P, PAIRS, N], F16)
        xr = sb("xr", [P, TT, D])
        bo_row = sb("bo_row", [P, 1, D])
        mx = sb("mx", [P, 2, 2, TT])
        mc = sb("mc", [P, 2, TT])
        zcol = sb("zcol", [P, 2, TT, DH + 1], F16)
        ps_s = [ps(f"ps_s{i}", [P, N]) for i in range(2)]
        ps_o = ps("ps_o", [P, N])
        ps_turn = [ps(f"ps_turn{i}", [P, HALF]) for i in range(2)]
        ps_y = [ps_s[i // 2][:, i % 2 * HALF:i % 2 * HALF + D] for i in range(4)]

        s_init = sem("s_init")
        s_bo = sem("s_bo")
        s_x = sem("s_x")
        s_xb = sem("s_xb")
        s_swap = [sem("s_swapk"), sem("s_swapq")]
        s_stack = [sem("s_stackk"), sem("s_stackq")]
        s_cos = sem("s_cos")
        s_sin = sem("s_sin")
        s_rot = sem("s_rot")
        s_hi = sem("s_hi")
        s_lo = sem("s_lo")
        s_kq_w = sem("s_kq_w")
        s_kq_r = sem("s_kq_r")
        s_v_w = sem("s_v_w")
        s_v_r = sem("s_v_r")
        s_max_w = sem("s_max_w")
        s_max_r = sem("s_max_r")
        s_mc = sem("s_mc")
        s_z = sem("s_z")
        s_row_w = sem("s_row_w")
        s_row_r = sem("s_row_r")
        s_sum_w = sem("s_sum_w")
        s_sum_r = sem("s_sum_r")
        s_st = sem("s_st")
        s_p = sem("s_p")
        s_acc0 = sem("s_acc0")
        s_acc1 = sem("s_acc1")
        s_pv = sem("s_pv")
        s_oev = sem("s_oev")
        s_inv = sem("s_inv")
        s_div = sem("s_div")
        s_ohi = sem("s_ohi")
        s_ot = sem("s_ot")
        s_y = sem("s_y")
        s_yr = sem("s_yr")
        s_out = sem("s_out")
        block = ctx.enter_context(nc.Block())
        x_v = x_src.rearrange("b (t p) d -> b p t d", p=P)
        y_v = x_dst.rearrange("b (t p) d -> b p t d", p=P)

        @block.sync
        def _(sp):
            def swap(j):
                for i in range(2):
                    sp.wait_ge(s_kq_r, 4 * j + 2 * i + 2)
                    sp.dma_start(swp[0:P:2, i, :], raw[1:P:2, i, :]).then_inc(s_swap[i], 16)
                    sp.dma_start(swp[1:P:2, i, :], raw[0:P:2, i, :]).then_inc(s_swap[i], 16)

            def stack(j, par):
                for i in range(2):
                    sp.wait_ge(s_hi, 2 * j + i + 1)
                    for x in range(2):
                        mine = hi[DH * x:DH * x + DH, i, :]
                        first, second = ((k_hl[0:DH], k_h1[0:DH]), (q_hh[0:DH], q_hh[DH:P]))[i]
                        sp.dma_start(first[:, par, x, :], mine).then_inc(s_stack[i], 16)
                        sp.dma_start(second[:, par, x, :], mine).then_inc(s_stack[i], 16)
                    sp.wait_ge(s_lo, 2 * j + i + 1)
                    for x in range(2):
                        dst = (k_hl[DH:P], q_lm[0:DH])[i]
                        sp.dma_start(dst[:, par, x, :], lo[DH * x:DH * x + DH, i, :]).then_inc(s_stack[i], 16)

            sp.dma_start(bo_row[:, 0, :], bo.partition_broadcast(P)).then_inc(s_bo, 16)
            swap(0)
            sp.wait_ge(s_init, 4)
            stack(0, 0)
            swap(1)
            for b in range(B):
                if b >= 1:
                    sp.wait_ge(s_out, 16 * b)
                sp.dma_start(xr[:], x_v[b]).then_inc(s_x, 16)
                with sp.Fori(0, PAIRS // 2) as pp:
                    for par in range(2):
                        g = b * PAIRS + pp * 2 + par
                        sp.wait_ge(s_st, 1 + 2 * NK * g)
                        stack(g + 1, 1 - par)
                        swap(g + 2)
                sp.wait_ge(s_yr, 1 + TT * b + TT)
                sp.dma_start(y_v[b], xr[:]).then_inc(s_out, 16)
            sp.wait_ge(s_out, 16 * B)
            for i in range(2):
                sp.wait_ge(s_swap[i], 32 * (B * PAIRS + 2))
                sp.wait_ge(s_stack[i], 96 * (B * PAIRS + 1))

        @block.gpsimd
        def _(pool):
            def rotate(j, i, table):
                pool.wait_ge(s_swap[i], 32 * j + 32)
                if table == 0:
                    pool.tensor_tensor(raw[:, i, :], raw[:, i, :], ropeC[:, :], ALU.mult).then_inc(s_cos, 1)
                else:
                    pool.tensor_tensor(swp[:, i, :], swp[:, i, :], ropeS[:, :], ALU.mult).then_inc(s_sin, 1)

            def low(j, i):
                pool.wait_ge(s_hi, 2 * j + i + 1)
                pool.wait_ge(s_stack[i], 96 * j)
                pool.tensor_tensor(lo[:, i, :], raw[:, i, :], hi[:, i, :], ALU.subtract).then_inc(s_lo, 1)

            def add_probs(g, kt):
                pool.wait_ge(s_p, 1 + 2 * NK * g + 2 * kt + 1)
                if kt == 1:
                    before = probs[:, 0, 0, :]
                else:
                    before = acc[:, 0, :]
                    pool.wait_ge(s_acc0, (NK - 1) * g + kt - 1)
                pool.tensor_tensor(acc[:, 0, :], before, probs[:, kt % 2, 0, :], ALU.add).then_inc(s_acc0, 1)

            for i in range(2):
                rotate(1, i, 0)
                rotate(1, i, 1)
            for i in range(2):
                low(1, i)
            with pool.Fori(0, B * PAIRS) as g:
                for kt in range(1, NK):
                    add_probs(g, kt)
                    if kt <= 4:
                        rotate(g + 2, (kt - 1) // 2, (kt - 1) % 2)
                    elif kt <= 6:
                        low(g + 2, kt - 5)

        @block.tensor
        def _(pe):
            def project(j, first):
                b, cols = pair_at(j)
                for i, w in enumerate((wk, wq)):
                    for c in range(2):
                        if i == 0:
                            for s, v in first(c):
                                pe.wait_ge(s, v)
                        else:
                            pe.wait_ge(s_kq_r, 4 * j + c + 1)
                        split_product(pe, ps_turn[c][:, :], range(KD), w, xT, lambda k: (slice(None), k, cols),
                                      lambda k, c=c: (slice(None), b, k, slice(c * HALF, (c + 1) * HALF)))\
                            .then_inc(s_kq_w, 1)

            def project_v(j):
                b, cols = pair_at(j)
                for c in range(2):
                    for q in range(4):
                        ks = slice((4 * c + q) * P, (4 * c + q + 1) * P)
                        ins = split_product(pe, ps_turn[c][:, q * P:(q + 1) * P], range(KD), xT, wv,
                                            lambda k, ks=ks: (slice(None), b, k, ks),
                                            lambda k: (slice(None), k, cols))
                    ins.then_inc(s_v_w, 1)

            def max_block(j, par, n):
                if n >= 2:
                    pe.wait_ge(s_max_r, MAXB * j + n - 1)
                x, t, c = n // (2 * TT), n // 2 % TT, n % 2
                pe.matmul(ps_turn[c][:, :], q_hh[:, par, x, t * P:(t + 1) * P],
                          k_hl[:, par, x, c * HALF:(c + 1) * HALF], start=True, stop=True).then_inc(s_max_w, 1)

            def max_rows(j, x):
                pe.wait_ge(s_z, 2 * j + x + 1)
                for c in range(2):
                    if x == 0:
                        pe.wait_ge(s_max_r, MAXB * (j + 1) - 1 + c)
                    else:
                        pe.wait_ge(s_row_r, 4 * j + c + 1)
                    for q in range(4):
                        ins = pe.matmul(ps_turn[c][0:DH + 1, q * P:(q + 1) * P], zcol[:, x, 4 * c + q, :],
                                        ident16[:, :], start=True, stop=True)
                    ins.then_inc(s_row_w, 1)

            def scores(par, x, kt, c):
                cs, ks = slice(c * HALF, (c + 1) * HALF), slice(kt * P, (kt + 1) * P)
                pe.matmul(ps_s[x][:, cs], k_hl[:, par, x, ks], q_hh[:, par, x, cs], start=True, stop=False)
                return pe.matmul(ps_s[x][:, cs], k_h1[:, par, x, ks], q_lm[:, par, x, cs], start=False, stop=True)

            def values(par, kt, c):
                cs = slice(c * HALF, (c + 1) * HALF)
                for x in range(2):
                    ins = pe.matmul(ps_o[DH * x:DH * x + DH, cs], v_pair[:, par, kt, DH * x:DH * x + DH],
                                    probs[:, kt % 2, x, cs], start=(kt == 0), stop=(kt == NK - 1))
                return ins

            project(0, lambda c: ())
            for c in range(2):
                pe.wait_ge(s_kq_r, 3 + c)
            project_v(0)
            project(1, lambda c: ((s_v_r, c + 1),))
            for i in range(2):
                pe.wait_ge(s_stack[i], 96)
            pe.wait_ge(s_kq_r, 8)
            for n in range(MAXB):
                max_block(0, 0, n)
            max_rows(0, 0)
            max_rows(0, 1)
            pe.sem_inc(s_st, 1)
            with pe.Fori(0, B) as b:
                with pe.Fori(0, PAIRS // 2) as pp:
                    for par in range(2):
                        g = b * PAIRS + pp * 2 + par
                        pe.wait_ge(s_yr, 1 + TT * b)
                        pe.wait_ge(s_row_r, 4 * (g + 1))
                        for kt in range(NK):
                            blocks = STEP_MAX.get(kt, ())
                            if kt == 1:
                                for i in range(2):
                                    pe.wait_ge(s_stack[i], 96 * (g + 2))
                                pe.wait_ge(s_kq_r, 4 * (g + 3))
                            for x in range(2):
                                if kt == 0:
                                    pe.wait_ge(s_p, 1 + 2 * NK * g)
                                else:
                                    pe.wait_ge(s_p, 1 + 2 * NK * g + 2 * (kt - 1) + x + 1)
                                for c in range(2):
                                    ins = scores(par, x, kt, c)
                                    if c == 1:
                                        ins.then_inc(s_st, 1)
                                    if 2 * x + c < len(blocks):
                                        max_block(g + 1, 1 - par, blocks[2 * x + c])
                            if kt == 0:
                                pe.wait_ge(s_sum_r, 1 + 2 * g)
                                project_v(g + 1)
                                project(g + 2, lambda c: ((s_v_r, 2 * (g + 1) + c + 1),))
                            else:
                                pe.wait_ge(s_p, 1 + 2 * NK * g + 2 * kt)
                                if kt == 1:
                                    pe.wait_ge(s_oev, 1 + g)
                                    pe.wait_ge(s_v_r, 2 * (g + 1))
                                for c in range(2):
                                    ins = values(par, kt - 1, c)
                                    if c == 1:
                                        ins.then_inc(s_pv, 1)
                                    if 4 + c < len(blocks):
                                        max_block(g + 1, 1 - par, blocks[4 + c])
                            if kt == 6:
                                max_rows(g + 1, 0)
                        max_rows(g + 1, 1)
                        pe.wait_ge(s_p, 1 + 2 * NK * (g + 1))
                        for c in range(2):
                            ins = values(par, NK - 1, c)
                        ins.then_inc(s_pv, 1)
                        pe.wait_ge(s_acc0, (NK - 1) * (g + 1))
                        pe.wait_ge(s_acc1, (NK - 1) * (g + 1))
                        for c in range(2):
                            pe.wait_ge(s_row_r, 4 * (g + 1) + 3 + c)
                            for x in range(2):
                                ins = pe.matmul(ps_turn[c][DH * x:DH * x + DH, :], ones32[:, :],
                                                acc[:, x, c * HALF:(c + 1) * HALF], start=True, stop=True)
                            ins.then_inc(s_sum_w, 1)
                output_projection(pe, o_hi, o_lo, wo, ps_y, s_y, s_yr, b, s_ot, 2)

        @block.scalar
        def _(act):
            def evacuate_kq(j, i, c):
                act.wait_ge(s_kq_w, 4 * j + 2 * i + c + 1)
                act.activation(raw[:, i, c * HALF:(c + 1) * HALF], ps_turn[c][:, :], ACT.Copy,
                               scale=1.0 / WS).then_inc(s_kq_r, 1)

            def evacuate_v(j, par):
                for c in range(2):
                    act.wait_ge(s_v_w, 2 * j + c + 1)
                    act.activation(v_pair[:, par, 4 * c:4 * c + 4, :],
                                   ps_turn[c].rearrange("p (a b) -> p a b", b=P), ACT.Copy,
                                   scale=1.0 / WS).then_inc(s_v_r, 1)

            def high(j, i):
                act.wait_ge(s_rot, 2 * j + i + 1)
                act.activation(hi[:, i, :], raw[:, i, :], ACT.Copy).then_inc(s_hi, 1)

            def row(j, par, x):
                for c in range(2):
                    act.wait_ge(s_row_w, 4 * j + 2 * x + c + 1)
                    act.activation(q_lm[DH:DH + 1, par, x, c * HALF:(c + 1) * HALF], ps_turn[c][DH:DH + 1, :],
                                   ACT.Copy).then_inc(s_row_r, 1)

            def exponentials(g, kt, x):
                act.wait_ge(s_st, 1 + 2 * NK * g + 2 * kt + x + 1)
                if kt >= 2:
                    act.wait_ge(s_pv, NK * g + kt - 1)
                    act.wait_ge((s_acc0, s_acc1)[x], (NK - 1) * g + max(1, kt - 2))
                act.activation(probs[:, kt % 2, x, :], ps_s[x][:, :], ACT.Exp, scale=float(DH) ** -0.5).then_inc(s_p, 1)

            act.sem_inc(s_p, 1)
            act.sem_inc(s_oev, 1)
            act.sem_inc(s_sum_r, 1)
            for i in range(2):
                for c in range(2):
                    evacuate_kq(0, i, c)
            evacuate_v(0, 0)
            high(0, 0)
            high(0, 1)
            for i in range(2):
                act.wait_ge(s_lo, i + 1)
                for c in range(2):
                    evacuate_kq(1, i, c)
            act.wait_ge(s_init, 4)
            row(0, 0, 0)
            for i in range(2):
                act.wait_ge(s_stack[i], 96)
                high(1, i)
            row(0, 0, 1)
            with act.Fori(0, B) as b:
                with act.Fori(0, PAIRS // 2) as pp:
                    for par in range(2):
                        g = b * PAIRS + pp * 2 + par
                        p = pp * 2 + par
                        for kt in range(NK):
                            exponentials(g, kt, 0)
                            exponentials(g, kt, 1)
                            if kt == 0:
                                evacuate_v(g + 1, 1 - par)
                                for i in range(2):
                                    act.wait_ge(s_lo, 2 * (g + 1) + i + 1)
                                    for c in range(2):
                                        evacuate_kq(g + 2, i, c)
                            if kt in (3, 5):
                                i = (kt - 3) // 2
                                act.wait_ge(s_stack[i], 96 * (g + 2))
                                high(g + 2, i)
                            if kt == 6:
                                row(g + 1, 1 - par, 0)
                        row(g + 1, 1 - par, 1)
                        act.wait_ge(s_pv, NK * (g + 1))
                        act.wait_ge(s_ot, 1 + 2 * g)
                        act.activation(o_pair[:], ps_o[:], ACT.Copy).then_inc(s_oev, 1)
                        for c in range(2):
                            act.wait_ge(s_sum_w, 2 * g + c + 1)
                            act.activation(inv[:, c * HALF:(c + 1) * HALF], ps_turn[c][:, :], ACT.Copy).then_inc(s_sum_r, 1)

        @block.vector
        def _(dve):
            def rotated(j, i):
                dve.wait_ge(s_sin, 2 * j + i + 1)
                dve.wait_ge(s_cos, 2 * j + i + 1)
                dve.tensor_tensor(raw[:, i, :], raw[:, i, :], swp[:, i, :], ALU.add).then_inc(s_rot, 1)

            def maximum(j, n):
                x, t, c = n // (2 * TT), n // 2 % TT, n % 2
                dve.wait_ge(s_max_w, MAXB * j + n + 1)
                dve.reduce_max(mx[:, x, c, t:t + 1], ps_turn[c][:, :], AX_X).then_inc(s_max_r, 1)
                if n % (2 * TT) == 2 * TT - 1:
                    dve.wait_ge(s_max_r, MAXB * j + n + 1)
                    dve.tensor_tensor(mc[:, x, :], mx[:, x, 0, :], mx[:, x, 1, :], ALU.max).then_inc(s_mc, 1)
                    dve.wait_ge(s_mc, 2 * j + x + 1)
                    dve.tensor_scalar(zcol[:, x, :, DH], mc[:, x, :], -1.0 / MS, None, ALU.mult).then_inc(s_z, 1)

            def add_probs(g, kt):
                dve.wait_ge(s_p, 1 + 2 * NK * g + 2 * kt + 2)
                if kt == 1:
                    before = probs[:, 0, 1, :]
                else:
                    before = acc[:, 1, :]
                    dve.wait_ge(s_acc1, (NK - 1) * g + kt - 1)
                dve.tensor_tensor(acc[:, 1, :], before, probs[:, kt % 2, 1, :], ALU.add).then_inc(s_acc1, 1)

            dve.sem_inc(s_ot, 1)
            dve.sem_inc(s_yr, 1)
            dve.memset(zcol[:], 0.0).then_inc(s_init, 1)
            dve.memset(q_lm[DH:P], 0.0).then_inc(s_init, 1)
            dve.memset(k_h1[DH:P], 0.0).then_inc(s_init, 1)
            dve.wait_ge(s_init, 3)
            dve.memset(k_h1[DH:DH + 1], MS).then_inc(s_init, 1)
            for i in range(2):
                dve.wait_ge(s_swap[i], 32)
                dve.tensor_tensor(raw[:, i, :], raw[:, i, :], ropeC[:, :], ALU.mult).then_inc(s_cos, 1)
                dve.tensor_tensor(swp[:, i, :], swp[:, i, :], ropeS[:, :], ALU.mult).then_inc(s_sin, 1)
                rotated(0, i)
            for i in range(2):
                dve.wait_ge(s_hi, i + 1)
                dve.tensor_tensor(lo[:, i, :], raw[:, i, :], hi[:, i, :], ALU.subtract).then_inc(s_lo, 1)
            for n in range(MAXB // 2):
                maximum(0, n)
            rotated(1, 0)
            rotated(1, 1)
            for n in range(MAXB // 2, MAXB):
                maximum(0, n)
            dve.wait_ge(s_bo, 16)
            with dve.Fori(0, B) as b:
                dve.wait_ge(s_x, 16 * b + 16)
                dve.tensor_tensor(xr[:], xr[:], bo_row[:].broadcast_to([P, TT, D]), ALU.add).then_inc(s_xb, 1)
                with dve.Fori(0, PAIRS) as p:
                    g = b * PAIRS + p
                    for kt in range(1, NK):
                        blocks = STEP_MAX.get(kt, ())
                        for n in blocks[:2]:
                            maximum(g + 1, n)
                        if kt >= 2:
                            add_probs(g, kt - 1)
                        for n in blocks[2:]:
                            maximum(g + 1, n)
                        if kt in (3, 5):
                            rotated(g + 2, (kt - 3) // 2)
                    add_probs(g, NK - 1)
                    for c in range(2):
                        n, cs = 2 * g + c + 1, slice(c * HALF, (c + 1) * HALF)
                        dve.wait_ge(s_sum_r, 1 + n)
                        dve.reciprocal(inv[:, cs], inv[:, cs]).then_inc(s_inv, 1)
                        dve.wait_ge(s_inv, n)
                        dve.wait_ge(s_oev, 1 + g + 1)
                        dve.tensor_tensor(o_pair[:, cs], o_pair[:, cs], inv[:, cs], ALU.mult).then_inc(s_div, 1)
                        dve.wait_ge(s_div, n)
                        dve.tensor_copy(o_hi[:, p, cs], o_pair[:, cs]).then_inc(s_ohi, 1)
                        dve.wait_ge(s_ohi, n)
                        dve.tensor_tensor(o_lo[:, p, cs], o_pair[:, cs], o_hi[:, p, cs], ALU.subtract).then_inc(s_ot, 1)
                dve.wait_ge(s_xb, b + 1)
                for t in range(TT):
                    dve.wait_ge(s_y, TT * b + t + 1)
                    dve.scalar_tensor_tensor(out=xr[:, t, :], in0=ps_y[t % 4], scalar=1.0 / WS, in1=xr[:, t, :],
                                             op0=ALU.mult, op1=ALU.add).then_inc(s_yr, 1)


def project_context(nc, consts, cT, wk, wv, k_hh, k_lo, v_all):
    ropeC, ropeS = consts["ropeC"], consts["ropeS"]
    PH = PAIRS // 2
    with ExitStack() as ctx:
        def sb(name, shape, dt=F32):
            return ctx.enter_context(nc.sbuf_tensor(f"cv_{name}", shape, dt))

        sems = []
        ctx.callback(clear_semaphores, nc, sems)

        def sem(name):
            sems.append(nc.alloc_semaphore(f"cv_{name}"))
            return sems[-1]

        raw = sb("raw", [P, PAIRS, B, M])
        swp = sb("swp", [P, PAIRS, B, M])
        rot = sb("rot", [P, PAIRS, B, M])
        hi = sb("hi", [P, PAIRS, B, M], F16)
        lo = sb("lo", [P, PAIRS, B, M], F16)
        banks = [ctx.enter_context(nc.psum_tensor(f"cv_bank{i}", [P, HALF], F32)) for i in range(8)]
        s_k_w = sem("s_k_w")
        s_k_r = sem("s_k_r")
        s_v_w = sem("s_v_w")
        s_v_r = sem("s_v_r")
        s_swap = [sem(f"s_swap{n}") for n in range(2)]
        s_cos = sem("s_cos")
        s_sin = sem("s_sin")
        s_rot = sem("s_rot")
        s_hi = sem("s_hi")
        s_lo = sem("s_lo")
        s_stack = sem("s_stack")
        block = ctx.enter_context(nc.Block())

        def half(n):
            return slice(n * PH, (n + 1) * PH)

        @block.sync
        def _(sp):
            for n in range(2):
                sp.wait_ge(s_k_r, PH * (n + 1))
                sp.dma_start(swp[0:P:2, half(n)], raw[1:P:2, half(n)]).then_inc(s_swap[n], 16)
                sp.dma_start(swp[1:P:2, half(n)], raw[0:P:2, half(n)]).then_inc(s_swap[n], 16)
            for n in range(2):
                sp.wait_ge(s_hi, n + 1)
                for x in range(2):
                    for dst in (k_hh[0:DH], k_hh[DH:P]):
                        sp.dma_start(dst[:, half(n), x], hi[DH * x:DH * x + DH, half(n)]).then_inc(s_stack, 16)
                sp.wait_ge(s_lo, n + 1)
                for x in range(2):
                    sp.dma_start(k_lo[:, half(n), x], lo[DH * x:DH * x + DH, half(n)]).then_inc(s_stack, 16)
            sp.wait_ge(s_stack, 16 * 12)

        @block.tensor
        def _(pe):
            for pair in range(PAIRS):
                split_product(pe, banks[pair][:, 0:B * M].rearrange("p (b m) -> p b m", m=M), range(KD), wk, cT,
                              lambda k: (slice(None), k, slice(pair * P, (pair + 1) * P)),
                              lambda k: (slice(None), slice(None), k, slice(0, M))).then_inc(s_k_w, 1)
            for n in range(2 * B):
                b, cs = n // 2, slice(n % 2 * HALF, (n % 2 + 1) * HALF)
                pe.wait_ge(s_k_r, n + 1)
                split_product(pe, banks[n][0:M, :], range(KD), cT, wv, lambda k: (slice(None), b, k, slice(0, M)),
                              lambda k: (slice(None), k, cs)).then_inc(s_v_w, 1)

        @block.scalar
        def _(act):
            for pair in range(PAIRS):
                act.wait_ge(s_k_w, pair + 1)
                act.activation(raw[:, pair], banks[pair][:, 0:B * M].rearrange("p (b m) -> p b m", m=M), ACT.Copy,
                               scale=1.0 / WS).then_inc(s_k_r, 1)
            for n in range(2 * B):
                act.wait_ge(s_v_w, n + 1)
                act.activation(v_all[:, n // 2, n % 2 * HALF:(n % 2 + 1) * HALF], banks[n][0:M, :], ACT.Copy,
                               scale=1.0 / WS).then_inc(s_v_r, 1)
                if n in (1, 5):
                    i = n // 4
                    act.wait_ge(s_rot, i + 1)
                    act.activation(hi[:, half(i)], rot[:, half(i)], ACT.Copy).then_inc(s_hi, 1)

        @block.vector
        def _(dve):
            def rows(buffer, n):
                return buffer[:, half(n)].rearrange("p a b m -> p (a b) m")

            def table(rope):
                return rope[:, 0:M].rearrange("p (a m) -> p a m", a=1).broadcast_to([P, PH * B, M])

            for n in range(2):
                dve.wait_ge(s_k_r, PH * (n + 1))
                dve.tensor_tensor(rows(rot, n), rows(raw, n), table(ropeC), ALU.mult).then_inc(s_cos, 1)
            for n in range(2):
                dve.wait_ge(s_swap[n], 32)
                dve.tensor_tensor(rows(swp, n), rows(swp, n), table(ropeS), ALU.mult).then_inc(s_sin, 1)
                dve.wait_ge(s_cos, n + 1)
                dve.wait_ge(s_sin, n + 1)
                dve.tensor_tensor(rows(rot, n), rows(rot, n), rows(swp, n), ALU.add).then_inc(s_rot, 1)
            for n in range(2):
                dve.wait_ge(s_hi, n + 1)
                dve.tensor_tensor(rows(lo, n), rows(rot, n), rows(hi, n), ALU.subtract).then_inc(s_lo, 1)


def cross_attention(nc, consts, x_src, x_dst, bo, xT, k_hh, k_lo, v_all, wq, wo):
    ropeC, ropeS = consts["ropeC"], consts["ropeS"]
    with ExitStack() as ctx:
        def sb(name, shape, dt=F32):
            return ctx.enter_context(nc.sbuf_tensor(f"ca_{name}", shape, dt))

        def ps(name, shape):
            return ctx.enter_context(nc.psum_tensor(f"ca_{name}", shape, F32))

        def sem(name):
            return ctx.enter_context(nc.semaphore(f"ca_{name}"))

        q_hl = sb("q_hl", [P, 2, 2, N], F16)
        raw = sb("raw", [P, 2, N])
        swp = sb("swp", [P, 2, N])
        rot = sb("rot", [P, 2, N])
        hi = sb("hi", [P, N], F16)
        lo = sb("lo", [P, N], F16)
        v_pair = sb("v_pair", [M, 2, P])
        ident = sb("ident", [P, P])
        e = sb("e", [P, 2, 2, TT, M])
        mx = sb("mx", [P, 2, TT])
        total = sb("total", [P, 2, TT])
        inv = sb("inv", [P, 2, 2, TT])
        pT = sb("pT", [M, 2, N])
        o_hi = sb("o_hi", [P, PAIRS, N], F16)
        o_lo = sb("o_lo", [P, PAIRS, N], F16)
        xr = sb("xr", [P, TT, D])
        bo_row = sb("bo_row", [P, 1, D])
        ps_sc = ps("ps_sc", [P, TT, P])
        ps_pt = ps("ps_pt", [P, N])
        ps_o = ps("ps_o", [P, N])
        ps_turn = [ps(f"ps_turn{i}", [P, HALF]) for i in range(2)]
        ps_y = [ps_pt[:, i * HALF:i * HALF + D] for i in range(2)] + [t[:, 0:D] for t in ps_turn]

        s_ident = sem("s_ident")
        s_bo = sem("s_bo")
        s_x = sem("s_x")
        s_xb = sem("s_xb")
        s_swap = [sem(f"s_swap{par}") for par in range(2)]
        s_stack = [sem(f"s_stack{par}") for par in range(2)]
        s_cos = sem("s_cos")
        s_sin = sem("s_sin")
        s_rot = sem("s_rot")
        s_hi = sem("s_hi")
        s_lo = sem("s_lo")
        s_q_w = sem("s_q_w")
        s_q_r = sem("s_q_r")
        s_sc_w = sem("s_sc_w")
        s_sc_r = sem("s_sc_r")
        s_mx = sem("s_mx")
        s_e = sem("s_e")
        s_v = sem("s_v")
        s_total = sem("s_total")
        s_inv = sem("s_inv")
        s_prob0 = sem("s_prob0")
        s_prob1 = sem("s_prob1")
        s_pt_w = sem("s_pt_w")
        s_pt_r = sem("s_pt_r")
        s_pv = sem("s_pv")
        s_ohi = sem("s_ohi")
        s_ot = sem("s_ot")
        s_y = sem("s_y")
        s_yr = sem("s_yr")
        s_out = sem("s_out")
        block = ctx.enter_context(nc.Block())
        x_v = x_src.rearrange("b (t p) d -> b p t d", p=P)
        y_v = x_dst.rearrange("b (t p) d -> b p t d", p=P)

        @block.sync
        def _(sp):
            def swap(j, par):
                sp.wait_ge(s_q_r, 2 * j + 2)
                sp.dma_start(swp[0:P:2, par, :], raw[1:P:2, par, :]).then_inc(s_swap[par], 16)
                sp.dma_start(swp[1:P:2, par, :], raw[0:P:2, par, :]).then_inc(s_swap[par], 16)

            def stack(j, par):
                sp.wait_ge(s_hi, j + 1)
                for x in range(2):
                    sp.dma_start(q_hl[0:DH, par, x, :], hi[DH * x:DH * x + DH, :]).then_inc(s_stack[par], 16)
                sp.wait_ge(s_lo, j + 1)
                for x in range(2):
                    sp.dma_start(q_hl[DH:P, par, x, :], lo[DH * x:DH * x + DH, :]).then_inc(s_stack[par], 16)

            sp.dma_start(bo_row[:, 0, :], bo.partition_broadcast(P)).then_inc(s_bo, 16)
            sp.dma_start(ident[:], consts["identity"]).then_inc(s_ident, 16)
            swap(0, 0)
            swap(1, 1)
            stack(0, 0)
            stack(1, 1)
            swap(2, 0)
            for b in range(B):
                if b >= 1:
                    sp.wait_ge(s_out, 16 * b)
                sp.dma_start(xr[:], x_v[b]).then_inc(s_x, 16)
                with sp.Fori(0, PAIRS // 2) as pp:
                    for par in range(2):
                        g = b * PAIRS + pp * 2 + par
                        stack(g + 2, par)
                        swap(g + 3, 1 - par)
                sp.wait_ge(s_yr, 1 + TT * b + TT)
                sp.dma_start(y_v[b], xr[:]).then_inc(s_out, 16)
            sp.wait_ge(s_out, 16 * B)
            for par in range(2):
                sp.wait_ge(s_swap[par], 32 * (B * PAIRS // 2 + 2 - par))
                sp.wait_ge(s_stack[par], 64 * (B * PAIRS // 2 + 1))

        @block.gpsimd
        def _(pool):
            def rotate(j, par, used=None):
                if used is not None:
                    pool.wait_ge(s_lo, used)
                pool.wait_ge(s_q_r, 2 * j + 2)
                pool.tensor_tensor(rot[:, par, :], raw[:, par, :], ropeC[:, :], ALU.mult).then_inc(s_cos, 1)
                pool.wait_ge(s_swap[par], 32 * (j >> 1) + 32)
                pool.tensor_tensor(swp[:, par, :], swp[:, par, :], ropeS[:, :], ALU.mult).then_inc(s_sin, 1)

            def normalise(j, par):
                pool.wait_ge(s_inv, 2 * j + 2)
                pool.tensor_tensor(e[:, par, 1], e[:, par, 1],
                                   inv[:, par, 1, :].rearrange("p (t a) -> p t a", a=1).broadcast_to([P, TT, M]),
                                   ALU.mult).then_inc(s_prob1, 1)

            def pick_values(j, par):
                b, cols = pair_at(j)
                pool.tensor_copy(v_pair[:, par, :], v_all[:, b, cols]).then_inc(s_v, 1)

            rotate(0, 0)
            rotate(1, 1)
            rotate(2, 0, 1)
            pick_values(0, 0)
            with pool.Fori(0, B * PAIRS // 2) as gg:
                for par in range(2):
                    g = gg * 2 + par
                    normalise(g, par)
                    pool.wait_ge(s_pv, 1 + g)
                    pick_values(g + 1, 1 - par)
                    rotate(g + 3, 1 - par, g + 2)

        @block.tensor
        def _(pe):
            def project(j, c):
                b, cols = pair_at(j)
                split_product(pe, ps_turn[c][:, :], range(KD), wq, xT, lambda k: (slice(None), k, cols),
                              lambda k: (slice(None), b, k, slice(c * HALF, (c + 1) * HALF))).then_inc(s_q_w, 1)

            def scores(j, par, x):
                b, pair = (j >> 3) & (B - 1), j & (PAIRS - 1)
                for t in range(TT):
                    ts = slice(t * P, (t + 1) * P)
                    pe.matmul(ps_sc[:, t, 0:M], q_hl[:, par, x, ts], k_hh[:, pair, x, b, :], start=True, stop=False)
                    ins = pe.matmul(ps_sc[:, t, 0:M], q_hl[0:DH, par, x, ts], k_lo[:, pair, x, b, :],
                                    start=False, stop=True)
                ins.then_inc(s_sc_w, 1)

            def transposes(par, x):
                for t in range(TT):
                    ins = pe.transpose(ps_pt[0:M, t * P:(t + 1) * P], e[:, par, x, t, :], ident[:, :])
                ins.then_inc(s_pt_w, 1)

            for j in range(3):
                for c in range(2):
                    if j >= 1:
                        pe.wait_ge(s_q_r, 2 * (j - 1) + c + 1)
                    project(j, c)
            pe.wait_ge(s_stack[0], 64)
            scores(0, 0, 0)
            pe.wait_ge(s_sc_r, 1)
            scores(0, 0, 1)
            pe.wait_ge(s_ident, 16)
            pe.sem_inc(s_pv, 1)

            def values(g, par):
                pe.wait_ge(s_v, g + 1)
                pe.wait_ge(s_ot, 1 + g)
                pe.wait_ge(s_pt_r, 1 + 2 * g + 2)
                for c in range(2):
                    for x in range(2):
                        cs = slice(c * HALF, (c + 1) * HALF)
                        ins = pe.matmul(ps_o[DH * x:DH * x + DH, cs], v_pair[:, par, DH * x:DH * x + DH],
                                        pT[:, x, cs], start=True, stop=True)
                ins.then_inc(s_pv, 1)

            def iteration(b, p, par, first=False):
                g = b * PAIRS + p
                pe.wait_ge(s_stack[1 - par], 64 * (((g + 1) >> 1) + 1))
                pe.wait_ge(s_sc_r, 2 * (g + 1))
                scores(g + 1, 1 - par, 0)
                if not first:
                    values(g - 1, 1 - par)
                pe.wait_ge(s_yr, 1 + TT * b)
                pe.wait_ge(s_pt_r, 1 + 2 * g)
                pe.wait_ge(s_prob0, g + 1)
                transposes(par, 0)
                for c in range(2):
                    pe.wait_ge(s_q_r, 2 * (g + 2) + c + 1)
                    project(g + 3, c)
                pe.wait_ge(s_sc_r, 2 * (g + 1) + 1)
                scores(g + 1, 1 - par, 1)
                pe.wait_ge(s_pt_r, 1 + 2 * g + 1)
                pe.wait_ge(s_prob1, g + 1)
                transposes(par, 1)

            with pe.Fori(0, B) as b:
                iteration(b, 0, 0, first=True)
                with pe.Fori(0, PAIRS // 2 - 1) as pp:
                    iteration(b, pp * 2 + 1, 1)
                    iteration(b, pp * 2 + 2, 0)
                iteration(b, PAIRS - 1, 1)
                values(b * PAIRS + PAIRS - 1, 1)
                pe.wait_ge(s_q_r, 2 * (b * PAIRS + PAIRS + 2) + 2)
                output_projection(pe, o_hi, o_lo, wo, ps_y, s_y, s_yr, b, s_ot, 1)

        @block.scalar
        def _(act):
            def evacuate(j, par, c):
                act.wait_ge(s_q_w, 2 * j + c + 1)
                act.activation(raw[:, par, c * HALF:(c + 1) * HALF], ps_turn[c][:, :], ACT.Copy,
                               scale=1.0 / WS).then_inc(s_q_r, 1)

            def high(j, par):
                act.wait_ge(s_rot, j + 1)
                act.activation(hi[:], rot[:, par, :], ACT.Copy).then_inc(s_hi, 1)

            def exponentials(j, par, x):
                act.wait_ge(s_sc_r, 2 * j + x + 1)
                act.activation(e[:, par, x], e[:, par, x], ACT.Exp, scale=float(DH) ** -0.5).then_inc(s_e, 1)

            def untranspose(g, x):
                act.wait_ge(s_pt_w, 2 * g + x + 1)
                act.activation(pT[:, x, :], ps_pt[0:M, :], ACT.Copy).then_inc(s_pt_r, 1)

            act.sem_inc(s_pt_r, 1)
            for j in range(2):
                for c in range(2):
                    evacuate(j, j, c)
            high(0, 0)
            act.wait_ge(s_lo, 1)
            for c in range(2):
                evacuate(2, 0, c)
            act.wait_ge(s_stack[0], 64)
            high(1, 1)
            exponentials(0, 0, 0)
            exponentials(0, 0, 1)

            def split_output(g, p):
                act.wait_ge(s_pv, 1 + g + 1)
                act.activation(o_hi[:, p, :], ps_o[:], ACT.Copy).then_inc(s_ohi, 1)

            def iteration(g, p, par, first=False):
                if not first:
                    split_output(g - 1, p - 1)
                act.wait_ge(s_stack[1 - par], 64 * (((g + 1) >> 1) + 1))
                high(g + 2, par)
                act.wait_ge(s_pv, 1 + g)
                untranspose(g, 0)
                act.wait_ge(s_lo, g + 2)
                evacuate(g + 3, 1 - par, 0)
                exponentials(g + 1, 1 - par, 0)
                evacuate(g + 3, 1 - par, 1)
                untranspose(g, 1)
                exponentials(g + 1, 1 - par, 1)

            with act.Fori(0, B) as b:
                iteration(b * PAIRS, 0, 0, first=True)
                with act.Fori(0, PAIRS // 2 - 1) as pp:
                    iteration(b * PAIRS + pp * 2 + 1, pp * 2 + 1, 1)
                    iteration(b * PAIRS + pp * 2 + 2, pp * 2 + 2, 0)
                iteration(b * PAIRS + PAIRS - 1, PAIRS - 1, 1)
                split_output(b * PAIRS + PAIRS - 1, PAIRS - 1)

        @block.vector
        def _(dve):
            def rotated(j, par):
                dve.wait_ge(s_sin, j + 1)
                dve.wait_ge(s_cos, j + 1)
                dve.tensor_tensor(rot[:, par, :], rot[:, par, :], swp[:, par, :], ALU.add).then_inc(s_rot, 1)

            def low(j, par):
                dve.wait_ge(s_hi, j + 1)
                dve.tensor_tensor(lo[:], rot[:, par, :], hi[:], ALU.subtract).then_inc(s_lo, 1)

            def shift(j, par, x):
                dve.wait_ge(s_sc_w, 2 * j + x + 1)
                dve.reduce_max(mx[:, x, :], ps_sc[:, :, 0:M], AX_X).then_inc(s_mx, 1)
                dve.wait_ge(s_mx, 2 * j + x + 1)
                dve.tensor_tensor(e[:, par, x], ps_sc[:, :, 0:M],
                                  mx[:, x, :].rearrange("p (t a) -> p t a", a=1).broadcast_to([P, TT, M]),
                                  ALU.subtract).then_inc(s_sc_r, 1)

            def totals(j, par, x):
                dve.wait_ge(s_e, 2 * j + x + 1)
                dve.reduce_sum(total[:, x, :], e[:, par, x], AX_X).then_inc(s_total, 1)
                dve.wait_ge(s_total, 2 * j + x + 1)
                dve.reciprocal(inv[:, par, x, :], total[:, x, :]).then_inc(s_inv, 1)
                if x == 0:
                    dve.wait_ge(s_inv, 2 * j + 1)
                    dve.tensor_tensor(e[:, par, 0], e[:, par, 0],
                                      inv[:, par, 0, :].rearrange("p (t a) -> p t a", a=1).broadcast_to([P, TT, M]),
                                      ALU.mult).then_inc(s_prob0, 1)

            dve.sem_inc(s_ot, 1)
            dve.sem_inc(s_yr, 1)
            for j in range(2):
                rotated(j, j)
                if j == 1:
                    dve.wait_ge(s_stack[0], 64)
                low(j, j)
            shift(0, 0, 0)
            shift(0, 0, 1)
            totals(0, 0, 0)
            dve.wait_ge(s_bo, 16)

            def split_output(g, p):
                dve.wait_ge(s_ohi, g + 1)
                dve.tensor_tensor(o_lo[:, p, :], ps_o[:], o_hi[:, p, :], ALU.subtract).then_inc(s_ot, 1)

            def iteration(g, p, par, first=False):
                shift(g + 1, 1 - par, 0)
                rotated(g + 2, par)
                totals(g, par, 1)
                if not first:
                    split_output(g - 1, p - 1)
                dve.wait_ge(s_stack[1 - par], 64 * (((g + 1) >> 1) + 1))
                low(g + 2, par)
                totals(g + 1, 1 - par, 0)
                shift(g + 1, 1 - par, 1)

            with dve.Fori(0, B) as b:
                dve.wait_ge(s_x, 16 * b + 16)
                dve.tensor_tensor(xr[:], xr[:], bo_row[:].broadcast_to([P, TT, D]), ALU.add).then_inc(s_xb, 1)
                iteration(b * PAIRS, 0, 0, first=True)
                with dve.Fori(0, PAIRS // 2 - 1) as pp:
                    iteration(b * PAIRS + pp * 2 + 1, pp * 2 + 1, 1)
                    iteration(b * PAIRS + pp * 2 + 2, pp * 2 + 2, 0)
                iteration(b * PAIRS + PAIRS - 1, PAIRS - 1, 1)
                split_output(b * PAIRS + PAIRS - 1, PAIRS - 1)
                dve.wait_ge(s_xb, b + 1)
                for t in range(TT):
                    dve.wait_ge(s_y, TT * b + t + 1)
                    dve.scalar_tensor_tensor(out=xr[:, t, :], in0=ps_y[t % 4], scalar=1.0 / WS, in1=xr[:, t, :],
                                             op0=ALU.mult, op1=ALU.add).then_inc(s_yr, 1)


def feed_forward(nc, tag, x_src, x_dst, b1, b2, xT, w1, w2):
    with ExitStack() as ctx:
        def sb(name, shape, dt=F32):
            return ctx.enter_context(nc.sbuf_tensor(f"{tag}_{name}", shape, dt))

        def sem(name):
            return ctx.enter_context(nc.semaphore(f"{tag}_{name}"))

        hid = sb("hid", [P, 2, N])
        h_hi = sb("h_hi", [P, KM, N], F16)
        h_lo = sb("h_lo", [P, KM, N], F16)
        xr = sb("xr", [P, 2, TT, D])
        b1_col = sb("b1_col", [P, KM])
        b2_row = sb("b2_row", [P, 1, D])
        ps_h = [ctx.enter_context(nc.psum_tensor(f"{tag}_ps_h{i}", [P, N], F32)) for i in range(2)]
        ps_y = [ctx.enter_context(nc.psum_tensor(f"{tag}_ps_y{i}", [P, HALF], F32)) for i in range(4)]
        s_b = sem("s_b")
        s_x = [sem("s_x0"), sem("s_x1")]
        s_xb = sem("s_xb")
        s_h = sem("s_h")
        s_g = sem("s_g")
        s_hi = sem("s_hi")
        s_lo = sem("s_lo")
        s_y = sem("s_y")
        s_yr = sem("s_yr")
        s_out = sem("s_out")
        block = ctx.enter_context(nc.Block())
        x_v = x_src.rearrange("b (t p) d -> b p t d", p=P)
        y_v = x_dst.rearrange("b (t p) d -> b p t d", p=P)

        @block.sync
        def _(sp):
            sp.dma_start(b1_col[:], b1.rearrange("(k p) -> p k", p=P),
                         allow_slow_non_contiguous=True).then_inc(s_b, 16)
            sp.dma_start(b2_row[:, 0, :], b2.partition_broadcast(P)).then_inc(s_b, 16)
            sp.dma_start(xr[:, 0], x_v[0]).then_inc(s_x[0], 16)
            for b in range(B):
                if b + 1 < B:
                    if b >= 1:
                        sp.wait_ge(s_out, 16 * b)
                    sp.dma_start(xr[:, 1 - b % 2], x_v[b + 1]).then_inc(s_x[1 - b % 2], 16)
                sp.wait_ge(s_yr, 1 + TT * b + TT)
                sp.dma_start(y_v[b], xr[:, b % 2]).then_inc(s_out, 16)
            sp.wait_ge(s_out, 16 * B)

        @block.tensor
        def _(pe):
            with pe.Fori(0, B) as b:
                for m in range(KM):
                    n = KM * b + m
                    if m >= 2:
                        pe.wait_ge(s_g, 1 + n - 1)
                    else:
                        pe.wait_ge(s_g, 1 + KM * b)
                    for c in range(2):
                        cs, ms = slice(c * HALF, (c + 1) * HALF), slice(m * P, (m + 1) * P)
                        ins = split_product(pe, ps_h[m % 2][:, cs], range(KD), w1, xT, lambda k, ms=ms: (slice(None), k, ms),
                                            lambda k, cs=cs: (slice(None), b, k, cs))
                    ins.then_inc(s_h, 1)
                pe.wait_ge(s_yr, 1 + TT * b)
                output_projection(pe, h_hi, h_lo, w2, [t[:, 0:D] for t in ps_y], s_y, s_yr, b, s_lo, 1)

        @block.scalar
        def _(act):
            act.sem_inc(s_g, 1)
            act.wait_ge(s_b, 32)
            with act.Fori(0, B) as b:
                for m in range(KM):
                    act.wait_ge(s_h, KM * b + m + 1)
                    if m >= 2:
                        act.wait_ge(s_lo, 1 + KM * b + m - 1)
                    act.activation(hid[:, m % 2, :], ps_h[m % 2][:, :], ACT.Gelu, bias=b1_col[:, m:m + 1],
                                   scale=1.0 / WS).then_inc(s_g, 1)

        @block.vector
        def _(dve):
            dve.sem_inc(s_yr, 1)
            dve.sem_inc(s_lo, 1)
            dve.wait_ge(s_b, 32)
            with dve.Fori(0, B // 2) as bb:
                for par in range(2):
                    b = bb * 2 + par
                    dve.wait_ge(s_x[par], 16 * bb + 16)
                    dve.tensor_tensor(xr[:, par], xr[:, par], b2_row[:].broadcast_to([P, TT, D]),
                                      ALU.add).then_inc(s_xb, 1)
                    for m in range(KM):
                        n = KM * b + m + 1
                        dve.wait_ge(s_g, 1 + n)
                        dve.tensor_copy(h_hi[:, m, :], hid[:, m % 2, :]).then_inc(s_hi, 1)
                        dve.wait_ge(s_hi, n)
                        dve.tensor_tensor(h_lo[:, m, :], hid[:, m % 2, :], h_hi[:, m, :],
                                          ALU.subtract).then_inc(s_lo, 1)
                    dve.wait_ge(s_xb, b + 1)
                    for t in range(TT):
                        dve.wait_ge(s_y, TT * b + t + 1)
                        dve.scalar_tensor_tensor(out=xr[:, par, t, :], in0=ps_y[t % 4][:, 0:D], scalar=1.0 / WS,
                                                 in1=xr[:, par, t, :], op0=ALU.mult, op1=ALU.add).then_inc(s_yr, 1)


def load_constants(nc, consts, cosines, sines):
    with ExitStack() as ctx:
        ident = ctx.enter_context(nc.sbuf_tensor("const_ident", [P, P], F32))
        s_load = ctx.enter_context(nc.semaphore("const_load"))
        s_made = ctx.enter_context(nc.semaphore("const_made"))
        block = ctx.enter_context(nc.Block())

        @block.sync
        def _(sp):
            sp.dma_start(ident[:], consts["identity"]).then_inc(s_load, 16)
            sp.dma_start(consts["ropeC"][:], cosines).then_inc(s_load, 16)
            sp.dma_start(consts["ropeS"][:], sines).then_inc(s_load, 16)
            sp.wait_ge(s_load, 48)

        @block.vector
        def _(dve):
            dve.memset(consts["ones32"][:], 1.0).then_inc(s_made, 1)
            dve.wait_ge(s_load, 48)
            dve.tensor_copy(consts["ident16"][:], ident[:]).then_inc(s_made, 1)


def program(nc, a, identity, cosines, sines, out):
    with ExitStack() as top:
        def keep(name, shape, dt=F32):
            return top.enter_context(nc.sbuf_tensor(name, shape, dt))

        consts = {"identity": identity, "ident16": keep("ident16", [P, P], F16),
                  "ropeC": keep("ropeC", [P, N]), "ropeS": keep("ropeS", [P, N]), "ones32": keep("ones32", [P, DH])}
        x1 = nc.dram_tensor("x_after_self", (B, N, D), F32, kind="Internal").ap()
        x2 = nc.dram_tensor("x_after_cross", (B, N, D), F32, kind="Internal").ap()
        xT = (keep("xT_hi", [P, B, KD, N], F16), keep("xT_lo", [P, B, KD, N], F16))
        load_constants(nc, consts, cosines, sines)

        def units(src, pair, width):
            hi, lo = pair
            rows = src.shape[0]
            if width == N:
                return [(src[k * P:min(rows, (k + 1) * P), :], hi[:, k, :], lo[:, k, :]) for k in range(-(-rows // P))]
            n = N // width
            return [(src[k * P:(k + n) * P, :].rearrange("(k p) n -> p k n", p=P),
                     hi[:, k:k + n, :].rearrange("p k n -> p (k n)"), lo[:, k:k + n, :].rearrange("p k n -> p (k n)"))
                    for k in range(0, rows // P, n)]

        def split_pair(ctx, name, k, width):
            return tuple(ctx.enter_context(nc.sbuf_tensor(f"{name}_{part}", [P, k, width], F16)) for part in ("hi", "lo"))

        norm1 = [a[n] for n in ("ln1_w", "ln1_b", "g1_w", "g1_b", "b1_w", "b1_b")]
        norm2 = [a[n] for n in ("ln2_w", "ln2_b", "g2_w", "g2_b", "b2_w", "b2_b")]
        for tag, src in (("sa", a["x"]), ("ca", x1)):
            with ExitStack() as ctx:
                wq, wo = split_pair(ctx, f"{tag}_wq", KD, MID), split_pair(ctx, f"{tag}_wo", KM, D)
                wk, wv = (split_pair(ctx, f"{tag}_{n}", KD, MID) for n in ("wk", "wv"))
                wkv = a[f"{tag}_wkv"]
                pieces = units(a[f"{tag}_wq"], wq, MID) + units(wkv[:, 0:MID], wk, MID)
                pieces += units(wkv[:, MID:2 * MID], wv, MID) + units(a[f"{tag}_wo"], wo, D)
                if tag == "sa":
                    prepare(nc, "sap", consts, src, a["cond_1024"], norm1, pieces, *xT)
                    self_attention(nc, consts, src, x1, a["sa_bo"], xT, wq, wk, wv, wo)
                else:
                    cT = tuple(ctx.enter_context(nc.sbuf_tensor(f"cT_{part}", [P, B, KD, M], F16))
                               for part in ("hi", "lo"))
                    prepare(nc, "cap", consts, src, a["cond_1024"], norm1, pieces, *xT,
                            context=(a["ctx_768"], a["ca_lnc_w"], a["ca_lnc_b"], *cT))
                    k_hh, k_lo = (ctx.enter_context(nc.sbuf_tensor(n, [rows, PAIRS, 2, B, M], F16))
                                  for n, rows in (("k_hh", P), ("k_lo", DH)))
                    v_all = ctx.enter_context(nc.sbuf_tensor("v_all", [M, B, MID], F32))
                    project_context(nc, consts, cT, wk, wv, k_hh, k_lo, v_all)
                    cross_attention(nc, consts, src, x2, a["ca_bo"], xT, k_hh, k_lo, v_all, wq, wo)
        with ExitStack() as ctx:
            w1 = split_pair(ctx, "w1", KD, HID)
            w2 = split_pair(ctx, "w2", KM, D)
            pieces = units(a["ff_w1"], w1, HID) + units(a["ff_w2"], w2, D)
            prepare(nc, "ffp", consts, x2, a["cond_1024"], norm2, pieces, *xT)
            feed_forward(nc, "ff", x2, out, a["ff_b1"], a["ff_b2"], xT, w1, w2)


def rope_tables():
    inv = (np.float32(1.0) / np.float32(10000.0) ** (np.arange(0, DH, 2, dtype=np.float32) / np.float32(DH)))
    ang = inv.astype(np.float32)[:, None] * np.arange(N, dtype=np.float32)[None, :]
    rows = np.arange(P) % DH // 2
    sign = np.where(np.arange(P) % 2 == 0, -1.0, 1.0).astype(np.float32)[:, None]
    return np.cos(ang)[rows].astype(np.float32), (np.sin(ang)[rows] * sign).astype(np.float32)


def kernel(**inputs):
    from concourse import bacc
    from concourse.bass_utils import run_bass_kernel_spmd

    nc = bacc.Bacc("TRN2", target_bir_lowering=False, num_devices=1)
    cosines, sines = rope_tables()
    arrays = {name: np.ascontiguousarray(v) for name, v in inputs.items()}
    arrays |= {"identity": np.eye(P, dtype=np.float32), "rope_cos": cosines, "rope_sin": sines}
    aps = {name: nc.dram_tensor(f"in_{name}", v.shape, mybir.dt.from_np(v.dtype), kind="ExternalInput").ap()
           for name, v in arrays.items()}
    out = nc.dram_tensor("out_x", (B, N, D), F32, kind="ExternalOutput").ap()
    a = {name.removeprefix("L0_xcond_"): ap for name, ap in aps.items()}
    program(nc, a, aps["identity"], aps["rope_cos"], aps["rope_sin"], out)
    r = run_bass_kernel_spmd(nc, [{f"in_{name}": v for name, v in arrays.items()}], core_ids=[0])
    return r.results[0]["out_x"]
```

```python
from contextlib import ExitStack

import numpy as np

import concourse.bass as bass
from concourse import mybir

F32 = mybir.dt.float32
F16 = mybir.dt.float16
ALU = mybir.AluOpType
ACT = mybir.ActivationFunctionType
AX_X = mybir.AxisListType.X

P = 128
B, N, D = 4, 1024, 256
M, DC = 77, 192
H, DH = 16, 64
MID = H * DH
HID = 4 * D
PAIRS = H // 2
TT = N // P
KD = D // P
KM = MID // P
HALF = N // 2
EPS = 1e-5
WS = 64.0
MS = 64.0




def clear_semaphores(nc, sems):
    nc.all_engine_barrier()
    nc.clear_and_free_semaphores(sems)
    nc.all_engine_barrier()


def prepare(nc, tag, consts, x_src, cond, norm, weights, xT_hi, xT_lo, context=None):
    lnw, lnb, gw, gb, bw, bb = norm
    with ExitStack() as ctx:
        def sb(name, shape, dt=F32):
            return ctx.enter_context(nc.sbuf_tensor(f"{tag}_{name}", shape, dt))

        sems = []
        ctx.callback(clear_semaphores, nc, sems)

        def sem(name):
            sems.append(nc.alloc_semaphore(f"{tag}_{name}"))
            return sems[-1]

        staged = sb("staged", [P, len(weights), N])
        xs = sb("xs", [P, B, TT, D])
        xn = sb("xn", [P, 4, HALF])
        cols = sb("cols", [P, 4, KD])
        condT = sb("condT", [P, KD, B])
        gates = sb("gates", [P, 2, KD, D])
        ident = sb("ident", [P, P])
        tmp = sb("tmp", [P, 2, KD, B])
        gam = sb("gam", [P, KD, B])
        bet = sb("bet", [P, KD, B])
        groups = B + (context is not None)
        stats = sb("stats", [P, groups, TT, 6])
        mv = sb("mv", [P, groups, TT, 2])
        var = sb("var", [P, groups, TT])
        root = sb("root", [P, groups, TT])
        rstd = sb("rstd", [P, groups, TT])
        newton = sb("newton", [P, groups, TT])
        shift = sb("shift", [P, B, TT])
        ps_gate = ctx.enter_context(nc.psum_tensor(f"{tag}_gate", [P, 2, KD, B], F32))
        ps_t = [ctx.enter_context(nc.psum_tensor(f"{tag}_t{i}", [P, HALF], F32)) for i in range(4)]

        s_ident = sem("s_ident")
        s_par = sem("s_par")
        s_w = sem("s_w")
        s_x = [sem(f"s_x{b}") for b in range(B)]
        s_gate = sem("s_gate")
        s_tab = sem("s_tab")
        s_whi = sem("s_whi")
        s_wlo = sem("s_wlo")
        s_stat = sem("s_stat")
        s_root = sem("s_root")
        s_xc = sem("s_xc")
        s_tr = sem("s_tr")
        s_xn = sem("s_xn")
        s_hi = sem("s_hi")
        s_lo = sem("s_lo")
        VARIANCE, STEPS = 3, 8
        first_w = [0, 0] + [len(weights) * n // (B - 1) for n in range(1, B)]
        if context is not None:
            c_src, c_w, c_b, cT_hi, cT_lo = context
            cs = sb("cs", [M, B, DC])
            crow = sb("crow", [M, 2, DC])
            s_c = sem("s_c")
            s_cn = sem("s_cn")
            s_ct = sem("s_ct")
            s_chi = sem("s_chi")
            s_clo = sem("s_clo")
            ps_c = [ctx.enter_context(nc.psum_tensor(f"{tag}_c{k}", [P, HALF], F32)) for k in range(2)]
            c_parts = [(k, rows, ps_c[k][0:rows, 0:B * M]) for k, rows in enumerate((P, DC - P))]
        block = ctx.enter_context(nc.Block())

        @block.sync
        def _(sp):
            x_v = x_src.rearrange("b (t p) d -> b p t d", p=P)
            sp.dma_start(xs[:, 0], x_v[0]).then_inc(s_x[0], 16)
            sp.dma_start(ident[:], consts["identity"]).then_inc(s_ident, 16)
            for k in range(KD):
                sp.dma_start(condT[:, k, :], cond[:, k * P:(k + 1) * P].rearrange("b p -> p b"),
                             allow_slow_non_contiguous=True).then_inc(s_par, 16)
            for i, w in enumerate((gw, bw)):
                sp.dma_start(gates[:, i], w.rearrange("(k p) n -> p k n", p=P)).then_inc(s_par, 16)
            for i, v in enumerate((lnw, lnb, gb, bb)):
                sp.dma_start(cols[:, i, :], v.rearrange("(k p) -> p k", p=P),
                             allow_slow_non_contiguous=True).then_inc(s_par, 16)
            for b in range(1, B):
                sp.dma_start(xs[:, b], x_v[b]).then_inc(s_x[b], 16)
            if context is not None:
                sp.dma_start(cs[:], c_src.rearrange("b m d -> m b d")).then_inc(s_c, 16)
                sp.dma_start(crow[:, 0, :], c_w.partition_broadcast(M)).then_inc(s_c, 16)
                sp.dma_start(crow[:, 1, :], c_b.partition_broadcast(M)).then_inc(s_c, 16)
            for n, (src, _, _) in enumerate(weights):
                dst = staged[0:src.shape[0], n, :]
                if len(src.shape) == 3:
                    dst = dst.rearrange("p (a b) -> p a b", b=src.shape[2])
                sp.dma_start(dst, src).then_inc(s_w, 16)

        @block.gpsimd
        def _(pool):
            for b in range(B):
                for n in range(4):
                    k, h = n // 2, n % 2
                    pool.wait_ge(s_hi, 4 * b + n + 1)
                    pool.tensor_tensor(xT_lo[:, b, k, h * HALF:(h + 1) * HALF], xn[:, n, :],
                                       xT_hi[:, b, k, h * HALF:(h + 1) * HALF], ALU.subtract).then_inc(s_lo, 1)

        @block.scalar
        def _(act):
            def deviations(i):
                rows, tiles = (P, TT) if i < B else (M, B)
                at = (slice(0, rows), i, slice(0, tiles))
                act.wait_ge(s_stat, STEPS * i + VARIANCE)
                act.activation(root[at], var[at], ACT.Sqrt).then_inc(s_root, 1)

            def normalise(b):
                act.wait_ge(s_stat, STEPS * (b + 1))
                for t in range(TT):
                    ins = act.activation(xs[:, b, t, :], xs[:, b, t, :], ACT.Identity, bias=shift[:, b, t:t + 1],
                                         scale=rstd[:, b, t:t + 1])
                ins.then_inc(s_xc, 1)

            for b in range(2):
                deviations(b)
                normalise(b)
            for b in range(B):
                if b + 2 < B:
                    deviations(b + 2)
                for n in range(4):
                    k, h = n // 2, n % 2
                    act.wait_ge(s_xn, 4 * b + n + 1)
                    act.activation(xT_hi[:, b, k, h * HALF:(h + 1) * HALF], xn[:, n, :], ACT.Copy).then_inc(s_hi, 1)
                if b + 2 < B:
                    normalise(b + 2)
                if context is not None and b == 2:
                    deviations(B)
                if context is not None and b == 3:
                    for k, rows, src in c_parts:
                        act.wait_ge(s_ct, k + 1)
                        act.activation(cT_hi[0:rows, :, k, :], src.rearrange("p (b m) -> p b m", m=M),
                                       ACT.Copy).then_inc(s_chi, 1)
                if b == 1:
                    act.wait_ge(s_w, 16 * len(weights))
                for src, w_hi, _, n in ((*w, n) for n, w in enumerate(weights) if first_w[b] <= n < first_w[b + 1]):
                    rows = min(P, src.shape[0])
                    act.activation(w_hi[0:rows], staged[0:rows, n, :], ACT.Copy, scale=WS).then_inc(s_whi, 1)

        @block.tensor
        def _(pe):
            pe.wait_ge(s_par, 16 * 8)
            for i in range(2):
                for m in range(KD):
                    for k in range(KD):
                        ins = pe.matmul(ps_gate[:, i, m, :], gates[:, i, k, m * P:(m + 1) * P], condT[:, k, :],
                                        start=(k == 0), stop=(k == KD - 1))
            ins.then_inc(s_gate, 1)
            pe.wait_ge(s_ident, 16)
            for b in range(B):
                pe.wait_ge(s_xc, b + 1)
                for n in range(4):
                    k, h = n // 2, n % 2
                    if b >= 1:
                        pe.wait_ge(s_xn, 4 * (b - 1) + n + 1)
                    for q in range(4):
                        ins = pe.transpose(ps_t[n][:, q * P:(q + 1) * P], xs[:, b, 4 * h + q, k * P:(k + 1) * P],
                                           ident[:, :])
                    ins.then_inc(s_tr, 1)
            if context is not None:
                pe.wait_ge(s_cn, 3)
                for k, rows, dst in c_parts:
                    for b in range(B):
                        ins = pe.transpose(dst[:, b * M:(b + 1) * M], cs[:, b, k * P:k * P + rows], ident[0:M, 0:M])
                    ins.then_inc(s_ct, 1)

        @block.vector
        def _(dve):
            def variances(i, source, tiles, rows):
                for t in range(tiles):
                    ins = dve.bn_stats(stats[0:rows, i, t, :], source[:, t, :])
                ins.then_inc(s_stat, 1)
                dve.wait_ge(s_stat, STEPS * i + 1)
                for t in range(tiles):
                    ins = dve.bn_aggr(mv[0:rows, i, t, :], stats[0:rows, i, t, :])
                ins.then_inc(s_stat, 1)
                dve.wait_ge(s_stat, STEPS * i + 2)
                dve.tensor_scalar(var[0:rows, i, 0:tiles], mv[0:rows, i, 0:tiles, 1], EPS, None,
                                  ALU.add).then_inc(s_stat, 1)

            def reciprocals(i, tiles, rows):
                at = (slice(0, rows), i, slice(0, tiles))
                dve.wait_ge(s_root, i + 1)
                dve.reciprocal(rstd[at], root[at]).then_inc(s_stat, 1)
                dve.wait_ge(s_stat, STEPS * i + 4)
                dve.tensor_tensor(newton[at], rstd[at], rstd[at], ALU.mult).then_inc(s_stat, 1)
                dve.wait_ge(s_stat, STEPS * i + 5)
                dve.scalar_tensor_tensor(out=newton[at], in0=newton[at], scalar=-0.5, in1=var[at], op0=ALU.mult,
                                         op1=ALU.mult).then_inc(s_stat, 1)
                dve.wait_ge(s_stat, STEPS * i + 6)
                ins = dve.scalar_tensor_tensor(out=rstd[at], in0=newton[at], scalar=1.5, in1=rstd[at], op0=ALU.add,
                                               op1=ALU.mult)
                if i == B:
                    ins.then_inc(s_stat, 2)
                    return
                ins.then_inc(s_stat, 1)
                dve.wait_ge(s_stat, STEPS * i + 7)
                dve.scalar_tensor_tensor(out=shift[:, i, :], in0=mv[:, i, :, 0], scalar=-1.0, in1=rstd[at],
                                         op0=ALU.mult, op1=ALU.mult).then_inc(s_stat, 1)

            def tables():
                def wide(i, n):
                    return cols[:, i:i + n, :].rearrange("p i (k a) -> p (i k) a", a=1).broadcast_to([P, n * KD, B])
                dve.wait_ge(s_gate, 1)
                dve.tensor_tensor(tmp.rearrange("p i k b -> p (i k) b"), ps_gate.rearrange("p i k b -> p (i k) b"),
                                  wide(2, 2), ALU.add).then_inc(s_tab, 1)
                dve.wait_ge(s_tab, 1)
                for i, dst in enumerate((gam, bet)):
                    dve.scalar_tensor_tensor(out=dst[:], in0=tmp[:, 0], scalar=1.0, in1=wide(i, 1), op0=ALU.add,
                                             op1=ALU.mult).then_inc(s_tab, 1)
                dve.wait_ge(s_tab, 3)
                dve.tensor_tensor(bet[:], bet[:], tmp[:, 1], ALU.add).then_inc(s_tab, 1)
                dve.wait_ge(s_tab, 4)

            def context_norm():
                dve.wait_ge(s_c, 48)
                variances(B, cs, B, M)
                reciprocals(B, B, M)
                dve.wait_ge(s_stat, STEPS * (B + 1))
                for b in range(B):
                    ins = dve.tensor_scalar(cs[:, b, :], cs[:, b, :], mv[0:M, B, b, 0:1], rstd[0:M, B, b:b + 1],
                                            ALU.subtract, ALU.mult)
                ins.then_inc(s_cn, 1)
                for i, op in enumerate((ALU.mult, ALU.add)):
                    dve.wait_ge(s_cn, i + 1)
                    dve.tensor_tensor(cs[:], cs[:], crow[:, i:i + 1, :].broadcast_to([M, B, DC]), op).then_inc(s_cn, 1)

            def weights_low(b):
                for n in range(first_w[b], first_w[b + 1]):
                    src, w_hi, w_lo = weights[n]
                    rows = min(P, src.shape[0])
                    dve.wait_ge(s_whi, n + 1)
                    dve.scalar_tensor_tensor(out=w_lo[0:rows], in0=staged[0:rows, n, :], scalar=WS,
                                             in1=w_hi[0:rows], op0=ALU.mult, op1=ALU.subtract).then_inc(s_wlo, 1)

            if context is not None:
                dve.memset(cT_hi[DC - P:P, :, 1, :], 0.0)
                dve.memset(cT_lo[DC - P:P, :, 1, :], 0.0)
            for n, (src, w_hi, w_lo) in enumerate(weights):
                if src.shape[0] < P:
                    dve.memset(w_hi[src.shape[0]:P], 0.0)
                    dve.memset(w_lo[src.shape[0]:P], 0.0)
            for b in range(2):
                dve.wait_ge(s_x[b], 16)
                variances(b, xs[:, b], TT, P)
                reciprocals(b, TT, P)
            tables()
            for b in range(B):
                if b + 2 < B:
                    dve.wait_ge(s_x[b + 2], 16)
                    variances(b + 2, xs[:, b + 2], TT, P)
                for n in range(4):
                    dve.wait_ge(s_tr, 4 * b + n + 1)
                    if b >= 1:
                        dve.wait_ge(s_lo, 4 * (b - 1) + n + 1)
                    dve.tensor_scalar(xn[:, n, :], ps_t[n][:, :], gam[:, n // 2, b:b + 1], bet[:, n // 2, b:b + 1],
                                      ALU.mult, ALU.add).then_inc(s_xn, 1)
                if b + 2 < B:
                    reciprocals(b + 2, TT, P)
                if context is not None and b == 2:
                    context_norm()
                if b >= 1:
                    weights_low(b - 1)
            weights_low(B - 1)
            if context is not None:
                for k, rows, src in c_parts:
                    dve.wait_ge(s_chi, k + 1)
                    dve.tensor_tensor(cT_lo[0:rows, :, k, :], src.rearrange("p (b m) -> p b m", m=M),
                                      cT_hi[0:rows, :, k, :], ALU.subtract).then_inc(s_clo, 1)


def pair_at(j):
    if isinstance(j, int):
        return j // PAIRS % B, bass.ds(j % PAIRS * P, P)
    return (j >> 3) & (B - 1), bass.ds((j & (PAIRS - 1)) * P, P)


def split_product(pe, out, k_tiles, lhs, rhs, lhs_at, rhs_at, start=True, stop=True):
    terms = [(k, a, b) for k in k_tiles for a, b in ((0, 0), (1, 0), (0, 1))]
    for i, (k, a, b) in enumerate(terms):
        ins = pe.matmul(out, lhs[a][lhs_at(k)], rhs[b][rhs_at(k)], start=(start and i == 0),
                        stop=(stop and i == len(terms) - 1))
    return ins


def output_projection(pe, o_hi, o_lo, wo, ps_y, s_y, s_yr, b, s_ot, parts):
    o, last = (o_hi, o_lo), KM - 1

    def product(t, ks, start, stop):
        ts = slice(t * P, (t + 1) * P)
        return split_product(pe, ps_y[t % 4], ks, o, wo, lambda k: (slice(None), k, ts),
                             lambda k: (slice(None), k, slice(None)), start, stop)

    pe.wait_ge(s_ot, 1 + parts * (KM * b + last))
    for t in range(4):
        product(t, range(last), True, False)
    for t in range(4):
        if t == 0:
            pe.wait_ge(s_ot, 1 + parts * (KM * b + last) + 1)
        product(t, (last,), False, True).then_inc(s_y, 1)
    pe.wait_ge(s_ot, 1 + parts * KM * (b + 1))
    for t in range(4, TT):
        pe.wait_ge(s_yr, 1 + TT * b + t - 3)
        product(t, range(KM), True, True).then_inc(s_y, 1)


def self_attention(nc, consts, x_src, x_dst, bo, xT, wq, wk, wv, wo):
    NK = N // P
    MAXB = 4 * TT
    STEP_MAX = {1: range(0, 6), 2: range(6, 11), 3: range(11, 15), 4: range(15, 20), 5: range(20, 25),
                6: range(25, 30), 7: range(30, 32)}
    ident16, ropeC, ropeS, ones32 = consts["ident16"], consts["ropeC"], consts["ropeS"], consts["ones32"]
    with ExitStack() as ctx:
        def sb(name, shape, dt=F32):
            return ctx.enter_context(nc.sbuf_tensor(f"sa_{name}", shape, dt))

        def ps(name, shape):
            return ctx.enter_context(nc.psum_tensor(f"sa_{name}", shape, F32))

        def sem(name):
            return ctx.enter_context(nc.semaphore(f"sa_{name}"))

        q_hh = sb("q_hh", [P, 2, 2, N], F16)
        q_lm = sb("q_lm", [P, 2, 2, N], F16)
        k_hl = sb("k_hl", [P, 2, 2, N], F16)
        k_h1 = sb("k_h1", [P, 2, 2, N], F16)
        raw = sb("raw", [P, 2, N])
        swp = sb("swp", [P, 2, N])
        hi = sb("hi", [P, 2, N], F16)
        lo = sb("lo", [P, 2, N], F16)
        v_pair = sb("v_pair", [P, 2, NK, P])
        probs = sb("probs", [P, 2, 2, N])
        acc = sb("acc", [P, 2, N])
        inv = acc[:, 1, :]
        o_pair = sb("o_pair", [P, N])
        o_hi = sb("o_hi", [P, PAIRS, N], F16)
        o_lo = sb("o_lo", [P, PAIRS, N], F16)
        xr = sb("xr", [P, TT, D])
        bo_row = sb("bo_row", [P, 1, D])
        mx = sb("mx", [P, 2, 2, TT])
        mc = sb("mc", [P, 2, TT])
        zcol = sb("zcol", [P, 2, TT, DH + 1], F16)
        ps_s = [ps(f"ps_s{i}", [P, N]) for i in range(2)]
        ps_o = ps("ps_o", [P, N])
        ps_turn = [ps(f"ps_turn{i}", [P, HALF]) for i in range(2)]
        ps_y = [ps_s[i // 2][:, i % 2 * HALF:i % 2 * HALF + D] for i in range(4)]

        s_init = sem("s_init")
        s_bo = sem("s_bo")
        s_x = sem("s_x")
        s_xb = sem("s_xb")
        s_swap = [sem("s_swapk"), sem("s_swapq")]
        s_stack = [sem("s_stackk"), sem("s_stackq")]
        s_cos = sem("s_cos")
        s_sin = sem("s_sin")
        s_rot = sem("s_rot")
        s_hi = sem("s_hi")
        s_lo = sem("s_lo")
        s_kq_w = sem("s_kq_w")
        s_kq_r = sem("s_kq_r")
        s_v_w = sem("s_v_w")
        s_v_r = sem("s_v_r")
        s_max_w = sem("s_max_w")
        s_max_r = sem("s_max_r")
        s_mc = sem("s_mc")
        s_z = sem("s_z")
        s_row_w = sem("s_row_w")
        s_row_r = sem("s_row_r")
        s_sum_w = sem("s_sum_w")
        s_sum_r = sem("s_sum_r")
        s_st = sem("s_st")
        s_p = sem("s_p")
        s_acc0 = sem("s_acc0")
        s_acc1 = sem("s_acc1")
        s_pv = sem("s_pv")
        s_oev = sem("s_oev")
        s_inv = sem("s_inv")
        s_div = sem("s_div")
        s_ohi = sem("s_ohi")
        s_ot = sem("s_ot")
        s_y = sem("s_y")
        s_yr = sem("s_yr")
        s_out = sem("s_out")
        block = ctx.enter_context(nc.Block())
        x_v = x_src.rearrange("b (t p) d -> b p t d", p=P)
        y_v = x_dst.rearrange("b (t p) d -> b p t d", p=P)

        @block.sync
        def _(sp):
            def swap(j):
                for i in range(2):
                    sp.wait_ge(s_kq_r, 4 * j + 2 * i + 2)
                    sp.dma_start(swp[0:P:2, i, :], raw[1:P:2, i, :]).then_inc(s_swap[i], 16)
                    sp.dma_start(swp[1:P:2, i, :], raw[0:P:2, i, :]).then_inc(s_swap[i], 16)

            def stack(j, par):
                for i in range(2):
                    sp.wait_ge(s_hi, 2 * j + i + 1)
                    for x in range(2):
                        mine = hi[DH * x:DH * x + DH, i, :]
                        first, second = ((k_hl[0:DH], k_h1[0:DH]), (q_hh[0:DH], q_hh[DH:P]))[i]
                        sp.dma_start(first[:, par, x, :], mine).then_inc(s_stack[i], 16)
                        sp.dma_start(second[:, par, x, :], mine).then_inc(s_stack[i], 16)
                    sp.wait_ge(s_lo, 2 * j + i + 1)
                    for x in range(2):
                        dst = (k_hl[DH:P], q_lm[0:DH])[i]
                        sp.dma_start(dst[:, par, x, :], lo[DH * x:DH * x + DH, i, :]).then_inc(s_stack[i], 16)

            sp.dma_start(bo_row[:, 0, :], bo.partition_broadcast(P)).then_inc(s_bo, 16)
            swap(0)
            sp.wait_ge(s_init, 4)
            stack(0, 0)
            swap(1)
            for b in range(B):
                with sp.Fori(0, PAIRS // 2) as pp:
                    for par in range(2):
                        g = b * PAIRS + pp * 2 + par
                        sp.wait_ge(s_st, 1 + 2 * NK * g)
                        stack(g + 1, 1 - par)
                        swap(g + 2)
                if b >= 1:
                    sp.wait_ge(s_out, 16 * b)
                sp.dma_start(xr[:], x_v[b]).then_inc(s_x, 16)
                sp.wait_ge(s_yr, 1 + TT * b + TT)
                sp.dma_start(y_v[b], xr[:]).then_inc(s_out, 16)
            sp.wait_ge(s_out, 16 * B)
            for i in range(2):
                sp.wait_ge(s_swap[i], 32 * (B * PAIRS + 2))
                sp.wait_ge(s_stack[i], 96 * (B * PAIRS + 1))

        @block.gpsimd
        def _(pool):
            def rotate(j, i, table):
                pool.wait_ge(s_swap[i], 32 * j + 32)
                if table == 0:
                    pool.tensor_tensor(raw[:, i, :], raw[:, i, :], ropeC[:, :], ALU.mult).then_inc(s_cos, 1)
                else:
                    pool.tensor_tensor(swp[:, i, :], swp[:, i, :], ropeS[:, :], ALU.mult).then_inc(s_sin, 1)

            def low(j, i):
                pool.wait_ge(s_hi, 2 * j + i + 1)
                pool.wait_ge(s_stack[i], 96 * j)
                pool.tensor_tensor(lo[:, i, :], raw[:, i, :], hi[:, i, :], ALU.subtract).then_inc(s_lo, 1)

            def add_probs(g, kt):
                pool.wait_ge(s_p, 1 + 2 * NK * g + 2 * kt + 1)
                if kt == 1:
                    before = probs[:, 0, 0, :]
                else:
                    before = acc[:, 0, :]
                    pool.wait_ge(s_acc0, (NK - 1) * g + kt - 1)
                pool.tensor_tensor(acc[:, 0, :], before, probs[:, kt % 2, 0, :], ALU.add).then_inc(s_acc0, 1)

            for i in range(2):
                rotate(1, i, 0)
                rotate(1, i, 1)
            for i in range(2):
                low(1, i)
            pool.wait_ge(s_bo, 16)
            with pool.Fori(0, B) as b:
                with pool.Fori(0, PAIRS) as p:
                    g = b * PAIRS + p
                    for kt in range(1, NK):
                        add_probs(g, kt)
                        if kt <= 4:
                            rotate(g + 2, (kt - 1) // 2, (kt - 1) % 2)
                        elif kt == 5:
                            low(g + 2, 0)
                        elif kt == 7:
                            low(g + 2, 1)
                pool.wait_ge(s_x, 16 * b + 16)
                pool.tensor_tensor(xr[:], xr[:], bo_row[:].broadcast_to([P, TT, D]), ALU.add).then_inc(s_xb, 1)

        @block.tensor
        def _(pe):
            def project(j, first):
                b, cols = pair_at(j)
                for i, w in enumerate((wk, wq)):
                    for c in range(2):
                        if i == 0:
                            for s, v in first(c):
                                pe.wait_ge(s, v)
                        else:
                            pe.wait_ge(s_kq_r, 4 * j + c + 1)
                        split_product(pe, ps_turn[c][:, :], range(KD), w, xT, lambda k: (slice(None), k, cols),
                                      lambda k, c=c: (slice(None), b, k, slice(c * HALF, (c + 1) * HALF)))\
                            .then_inc(s_kq_w, 1)

            def project_v(j):
                b, cols = pair_at(j)
                for c in range(2):
                    for q in range(4):
                        ks = slice((4 * c + q) * P, (4 * c + q + 1) * P)
                        ins = split_product(pe, ps_turn[c][:, q * P:(q + 1) * P], range(KD), xT, wv,
                                            lambda k, ks=ks: (slice(None), b, k, ks),
                                            lambda k: (slice(None), k, cols))
                    ins.then_inc(s_v_w, 1)

            def max_block(j, par, n):
                if n >= 2:
                    pe.wait_ge(s_max_r, MAXB * j + n - 1)
                x, t, c = n // (2 * TT), n // 2 % TT, n % 2
                pe.matmul(ps_turn[c][:, :], q_hh[:, par, x, t * P:(t + 1) * P],
                          k_hl[:, par, x, c * HALF:(c + 1) * HALF], start=True, stop=True).then_inc(s_max_w, 1)

            def max_rows(j, x):
                pe.wait_ge(s_z, 2 * j + x + 1)
                for c in range(2):
                    if x == 0:
                        pe.wait_ge(s_max_r, MAXB * (j + 1) - 1 + c)
                    else:
                        pe.wait_ge(s_row_r, 4 * j + c + 1)
                    for q in range(4):
                        ins = pe.matmul(ps_turn[c][0:DH + 1, q * P:(q + 1) * P], zcol[:, x, 4 * c + q, :],
                                        ident16[:, :], start=True, stop=True)
                    ins.then_inc(s_row_w, 1)

            def scores(par, x, kt, c):
                cs, ks = slice(c * HALF, (c + 1) * HALF), slice(kt * P, (kt + 1) * P)
                pe.matmul(ps_s[x][:, cs], k_hl[:, par, x, ks], q_hh[:, par, x, cs], start=True, stop=False)
                return pe.matmul(ps_s[x][:, cs], k_h1[:, par, x, ks], q_lm[:, par, x, cs], start=False, stop=True)

            def values(par, kt, c):
                cs = slice(c * HALF, (c + 1) * HALF)
                for x in range(2):
                    ins = pe.matmul(ps_o[DH * x:DH * x + DH, cs], v_pair[:, par, kt, DH * x:DH * x + DH],
                                    probs[:, kt % 2, x, cs], start=(kt == 0), stop=(kt == NK - 1))
                return ins

            project(0, lambda c: ())
            for c in range(2):
                pe.wait_ge(s_kq_r, 3 + c)
            project_v(0)
            project(1, lambda c: ((s_v_r, c + 1),))
            for i in range(2):
                pe.wait_ge(s_stack[i], 96)
            pe.wait_ge(s_kq_r, 8)
            for n in range(MAXB):
                max_block(0, 0, n)
            max_rows(0, 0)
            max_rows(0, 1)
            pe.sem_inc(s_st, 1)
            with pe.Fori(0, B) as b:
                with pe.Fori(0, PAIRS // 2) as pp:
                    for par in range(2):
                        g = b * PAIRS + pp * 2 + par
                        pe.wait_ge(s_yr, 1 + TT * b)
                        pe.wait_ge(s_row_r, 4 * (g + 1))
                        for kt in range(NK):
                            blocks = STEP_MAX.get(kt, ())
                            for x in range(2):
                                if kt == 0:
                                    pe.wait_ge(s_p, 1 + 2 * NK * g)
                                else:
                                    pe.wait_ge(s_p, 1 + 2 * NK * g + 2 * (kt - 1) + x + 1)
                                for c in range(2):
                                    ins = scores(par, x, kt, c)
                                    if c == 1:
                                        ins.then_inc(s_st, 1)
                                    if kt == 1 and x == 0 and c == 0:
                                        for i in range(2):
                                            pe.wait_ge(s_stack[i], 96 * (g + 2))
                                        pe.wait_ge(s_kq_r, 4 * (g + 3))
                                    if 2 * x + c < len(blocks):
                                        max_block(g + 1, 1 - par, blocks[2 * x + c])
                            if kt == NK - 1:
                                max_rows(g + 1, 0)
                            if kt == 0:
                                pe.wait_ge(s_sum_r, 1 + 2 * g)
                                project_v(g + 1)
                                project(g + 2, lambda c: ((s_v_r, 2 * (g + 1) + c + 1),))
                            else:
                                pe.wait_ge(s_p, 1 + 2 * NK * g + 2 * kt)
                                if kt == 1:
                                    pe.wait_ge(s_oev, 1 + g)
                                    pe.wait_ge(s_v_r, 2 * (g + 1))
                                for c in range(2):
                                    ins = values(par, kt - 1, c)
                                    if c == 1:
                                        ins.then_inc(s_pv, 1)
                                    if 4 + c < len(blocks):
                                        max_block(g + 1, 1 - par, blocks[4 + c])
                        max_rows(g + 1, 1)
                        pe.wait_ge(s_p, 1 + 2 * NK * (g + 1))
                        for c in range(2):
                            ins = values(par, NK - 1, c)
                        ins.then_inc(s_pv, 1)
                        pe.wait_ge(s_acc0, (NK - 1) * (g + 1))
                        pe.wait_ge(s_acc1, (NK - 1) * (g + 1))
                        for c in range(2):
                            pe.wait_ge(s_row_r, 4 * (g + 1) + 3 + c)
                            for x in range(2):
                                ins = pe.matmul(ps_turn[c][DH * x:DH * x + DH, :], ones32[:, :],
                                                acc[:, x, c * HALF:(c + 1) * HALF], start=True, stop=True)
                            ins.then_inc(s_sum_w, 1)
                output_projection(pe, o_hi, o_lo, wo, ps_y, s_y, s_yr, b, s_ot, 2)

        @block.scalar
        def _(act):
            def evacuate_kq(j, i, c):
                act.wait_ge(s_kq_w, 4 * j + 2 * i + c + 1)
                act.activation(raw[:, i, c * HALF:(c + 1) * HALF], ps_turn[c][:, :], ACT.Copy,
                               scale=1.0 / WS).then_inc(s_kq_r, 1)

            def evacuate_v(j, par):
                for c in range(2):
                    act.wait_ge(s_v_w, 2 * j + c + 1)
                    act.activation(v_pair[:, par, 4 * c:4 * c + 4, :],
                                   ps_turn[c].rearrange("p (a b) -> p a b", b=P), ACT.Copy,
                                   scale=1.0 / WS).then_inc(s_v_r, 1)

            def high(j, i):
                act.wait_ge(s_rot, 2 * j + i + 1)
                act.activation(hi[:, i, :], raw[:, i, :], ACT.Copy).then_inc(s_hi, 1)

            def row(j, par, x):
                for c in range(2):
                    act.wait_ge(s_row_w, 4 * j + 2 * x + c + 1)
                    act.activation(q_lm[DH:DH + 1, par, x, c * HALF:(c + 1) * HALF], ps_turn[c][DH:DH + 1, :],
                                   ACT.Copy).then_inc(s_row_r, 1)

            def exponentials(g, kt, x):
                act.wait_ge(s_st, 1 + 2 * NK * g + 2 * kt + x + 1)
                if kt >= 2:
                    act.wait_ge(s_pv, NK * g + kt - 1)
                    act.wait_ge((s_acc0, s_acc1)[x], (NK - 1) * g + max(1, kt - 2))
                act.activation(probs[:, kt % 2, x, :], ps_s[x][:, :], ACT.Exp, scale=float(DH) ** -0.5).then_inc(s_p, 1)

            act.sem_inc(s_p, 1)
            act.sem_inc(s_oev, 1)
            act.sem_inc(s_sum_r, 1)
            for i in range(2):
                for c in range(2):
                    evacuate_kq(0, i, c)
            evacuate_v(0, 0)
            high(0, 0)
            high(0, 1)
            for i in range(2):
                act.wait_ge(s_lo, i + 1)
                for c in range(2):
                    evacuate_kq(1, i, c)
            act.wait_ge(s_init, 4)
            row(0, 0, 0)
            for i in range(2):
                act.wait_ge(s_stack[i], 96)
                high(1, i)
            row(0, 0, 1)
            with act.Fori(0, B) as b:
                with act.Fori(0, PAIRS // 2) as pp:
                    for par in range(2):
                        g = b * PAIRS + pp * 2 + par
                        p = pp * 2 + par
                        for kt in range(NK):
                            exponentials(g, kt, 0)
                            exponentials(g, kt, 1)
                            if kt == 0:
                                evacuate_v(g + 1, 1 - par)
                                for i in range(2):
                                    act.wait_ge(s_lo, 2 * (g + 1) + i + 1)
                                    for c in range(2):
                                        evacuate_kq(g + 2, i, c)
                            if kt == 3:
                                act.wait_ge(s_stack[0], 96 * (g + 2))
                                high(g + 2, 0)
                        row(g + 1, 1 - par, 0)
                        row(g + 1, 1 - par, 1)
                        act.wait_ge(s_stack[1], 96 * (g + 2))
                        high(g + 2, 1)
                        act.wait_ge(s_pv, NK * (g + 1))
                        act.wait_ge(s_ot, 1 + 2 * g)
                        act.activation(o_pair[:], ps_o[:], ACT.Copy).then_inc(s_oev, 1)
                        for c in range(2):
                            act.wait_ge(s_sum_w, 2 * g + c + 1)
                            act.activation(inv[:, c * HALF:(c + 1) * HALF], ps_turn[c][:, :], ACT.Copy).then_inc(s_sum_r, 1)

        @block.vector
        def _(dve):
            def rotated(j, i):
                dve.wait_ge(s_sin, 2 * j + i + 1)
                dve.wait_ge(s_cos, 2 * j + i + 1)
                dve.tensor_tensor(raw[:, i, :], raw[:, i, :], swp[:, i, :], ALU.add).then_inc(s_rot, 1)

            def maximum(j, n):
                x, t, c = n // (2 * TT), n // 2 % TT, n % 2
                dve.wait_ge(s_max_w, MAXB * j + n + 1)
                dve.reduce_max(mx[:, x, c, t:t + 1], ps_turn[c][:, :], AX_X).then_inc(s_max_r, 1)
                if n % (2 * TT) == 2 * TT - 1:
                    dve.wait_ge(s_max_r, MAXB * j + n + 1)
                    dve.tensor_tensor(mc[:, x, :], mx[:, x, 0, :], mx[:, x, 1, :], ALU.max).then_inc(s_mc, 1)
                    dve.wait_ge(s_mc, 2 * j + x + 1)
                    dve.tensor_scalar(zcol[:, x, :, DH], mc[:, x, :], -1.0 / MS, None, ALU.mult).then_inc(s_z, 1)

            def add_probs(g, kt):
                dve.wait_ge(s_p, 1 + 2 * NK * g + 2 * kt + 2)
                if kt == 1:
                    before = probs[:, 0, 1, :]
                else:
                    before = acc[:, 1, :]
                    dve.wait_ge(s_acc1, (NK - 1) * g + kt - 1)
                dve.tensor_tensor(acc[:, 1, :], before, probs[:, kt % 2, 1, :], ALU.add).then_inc(s_acc1, 1)

            dve.sem_inc(s_ot, 1)
            dve.sem_inc(s_yr, 1)
            dve.memset(zcol[:], 0.0).then_inc(s_init, 1)
            dve.memset(q_lm[DH:P], 0.0).then_inc(s_init, 1)
            dve.memset(k_h1[DH:P], 0.0).then_inc(s_init, 1)
            dve.wait_ge(s_init, 3)
            dve.memset(k_h1[DH:DH + 1], MS).then_inc(s_init, 1)
            for i in range(2):
                dve.wait_ge(s_swap[i], 32)
                dve.tensor_tensor(raw[:, i, :], raw[:, i, :], ropeC[:, :], ALU.mult).then_inc(s_cos, 1)
                dve.tensor_tensor(swp[:, i, :], swp[:, i, :], ropeS[:, :], ALU.mult).then_inc(s_sin, 1)
                rotated(0, i)
            for i in range(2):
                dve.wait_ge(s_hi, i + 1)
                dve.tensor_tensor(lo[:, i, :], raw[:, i, :], hi[:, i, :], ALU.subtract).then_inc(s_lo, 1)
            for n in range(MAXB // 2):
                maximum(0, n)
            rotated(1, 0)
            rotated(1, 1)
            for n in range(MAXB // 2, MAXB):
                maximum(0, n)
            with dve.Fori(0, B) as b:
                with dve.Fori(0, PAIRS) as p:
                    g = b * PAIRS + p
                    for kt in range(1, NK):
                        blocks = STEP_MAX.get(kt, ())
                        for n in blocks[:4]:
                            maximum(g + 1, n)
                        if kt >= 2:
                            add_probs(g, kt - 1)
                        for n in blocks[4:]:
                            maximum(g + 1, n)
                        if kt in (3, 7):
                            rotated(g + 2, (kt - 3) // 4)
                    add_probs(g, NK - 1)
                    for c in range(2):
                        n, cs = 2 * g + c + 1, slice(c * HALF, (c + 1) * HALF)
                        dve.wait_ge(s_sum_r, 1 + n)
                        dve.reciprocal(inv[:, cs], inv[:, cs]).then_inc(s_inv, 1)
                        dve.wait_ge(s_inv, n)
                        dve.wait_ge(s_oev, 1 + g + 1)
                        dve.tensor_tensor(o_pair[:, cs], o_pair[:, cs], inv[:, cs], ALU.mult).then_inc(s_div, 1)
                        dve.wait_ge(s_div, n)
                        dve.tensor_copy(o_hi[:, p, cs], o_pair[:, cs]).then_inc(s_ohi, 1)
                        dve.wait_ge(s_ohi, n)
                        dve.tensor_tensor(o_lo[:, p, cs], o_pair[:, cs], o_hi[:, p, cs], ALU.subtract).then_inc(s_ot, 1)
                dve.wait_ge(s_xb, b + 1)
                for t in range(TT):
                    dve.wait_ge(s_y, TT * b + t + 1)
                    dve.scalar_tensor_tensor(out=xr[:, t, :], in0=ps_y[t % 4], scalar=1.0 / WS, in1=xr[:, t, :],
                                             op0=ALU.mult, op1=ALU.add).then_inc(s_yr, 1)


def project_context(nc, consts, cT, wk, wv, k_hh, k_lo, v_all):
    ropeC, ropeS = consts["ropeC"], consts["ropeS"]
    PH = PAIRS // 2
    with ExitStack() as ctx:
        def sb(name, shape, dt=F32):
            return ctx.enter_context(nc.sbuf_tensor(f"cv_{name}", shape, dt))

        sems = []
        ctx.callback(clear_semaphores, nc, sems)

        def sem(name):
            sems.append(nc.alloc_semaphore(f"cv_{name}"))
            return sems[-1]

        raw = sb("raw", [P, PAIRS, B, M])
        swp = sb("swp", [P, PAIRS, B, M])
        rot = sb("rot", [P, PAIRS, B, M])
        hi = sb("hi", [P, PAIRS, B, M], F16)
        lo = sb("lo", [P, PAIRS, B, M], F16)
        banks = [ctx.enter_context(nc.psum_tensor(f"cv_bank{i}", [P, HALF], F32)) for i in range(8)]
        s_k_w = sem("s_k_w")
        s_k_r = sem("s_k_r")
        s_v_w = sem("s_v_w")
        s_v_r = sem("s_v_r")
        s_swap = [sem(f"s_swap{n}") for n in range(2)]
        s_cos = sem("s_cos")
        s_sin = sem("s_sin")
        s_rot = sem("s_rot")
        s_hi = sem("s_hi")
        s_lo = sem("s_lo")
        s_stack = sem("s_stack")
        block = ctx.enter_context(nc.Block())

        def half(n):
            return slice(n * PH, (n + 1) * PH)

        @block.sync
        def _(sp):
            for n in range(2):
                sp.wait_ge(s_k_r, PH * (n + 1))
                sp.dma_start(swp[0:P:2, half(n)], raw[1:P:2, half(n)]).then_inc(s_swap[n], 16)
                sp.dma_start(swp[1:P:2, half(n)], raw[0:P:2, half(n)]).then_inc(s_swap[n], 16)
            for n in range(2):
                sp.wait_ge(s_hi, n + 1)
                for x in range(2):
                    for dst in (k_hh[0:DH], k_hh[DH:P]):
                        sp.dma_start(dst[:, half(n), x], hi[DH * x:DH * x + DH, half(n)]).then_inc(s_stack, 16)
                sp.wait_ge(s_lo, n + 1)
                for x in range(2):
                    sp.dma_start(k_lo[:, half(n), x], lo[DH * x:DH * x + DH, half(n)]).then_inc(s_stack, 16)
            sp.wait_ge(s_stack, 16 * 12)

        @block.tensor
        def _(pe):
            for pair in range(PAIRS):
                split_product(pe, banks[pair][:, 0:B * M].rearrange("p (b m) -> p b m", m=M), range(KD), wk, cT,
                              lambda k: (slice(None), k, slice(pair * P, (pair + 1) * P)),
                              lambda k: (slice(None), slice(None), k, slice(0, M))).then_inc(s_k_w, 1)
            for n in range(2 * B):
                b, cs = n // 2, slice(n % 2 * HALF, (n % 2 + 1) * HALF)
                pe.wait_ge(s_k_r, n + 1)
                split_product(pe, banks[n][0:M, :], range(KD), cT, wv, lambda k: (slice(None), b, k, slice(0, M)),
                              lambda k: (slice(None), k, cs)).then_inc(s_v_w, 1)

        @block.scalar
        def _(act):
            for pair in range(PAIRS):
                act.wait_ge(s_k_w, pair + 1)
                act.activation(raw[:, pair], banks[pair][:, 0:B * M].rearrange("p (b m) -> p b m", m=M), ACT.Copy,
                               scale=1.0 / WS).then_inc(s_k_r, 1)
            for n in range(2 * B):
                act.wait_ge(s_v_w, n + 1)
                act.activation(v_all[:, n // 2, n % 2 * HALF:(n % 2 + 1) * HALF], banks[n][0:M, :], ACT.Copy,
                               scale=1.0 / WS).then_inc(s_v_r, 1)
                if n in (1, 5):
                    i = n // 4
                    act.wait_ge(s_rot, i + 1)
                    act.activation(hi[:, half(i)], rot[:, half(i)], ACT.Copy).then_inc(s_hi, 1)

        @block.vector
        def _(dve):
            def rows(buffer, n):
                return buffer[:, half(n)].rearrange("p a b m -> p (a b) m")

            def table(rope):
                return rope[:, 0:M].rearrange("p (a m) -> p a m", a=1).broadcast_to([P, PH * B, M])

            for n in range(2):
                dve.wait_ge(s_k_r, PH * (n + 1))
                dve.tensor_tensor(rows(rot, n), rows(raw, n), table(ropeC), ALU.mult).then_inc(s_cos, 1)
            for n in range(2):
                dve.wait_ge(s_swap[n], 32)
                dve.tensor_tensor(rows(swp, n), rows(swp, n), table(ropeS), ALU.mult).then_inc(s_sin, 1)
                dve.wait_ge(s_cos, n + 1)
                dve.wait_ge(s_sin, n + 1)
                dve.tensor_tensor(rows(rot, n), rows(rot, n), rows(swp, n), ALU.add).then_inc(s_rot, 1)
            for n in range(2):
                dve.wait_ge(s_hi, n + 1)
                dve.tensor_tensor(rows(lo, n), rows(rot, n), rows(hi, n), ALU.subtract).then_inc(s_lo, 1)


def cross_attention(nc, consts, x_src, x_dst, bo, xT, k_hh, k_lo, v_all, wq, wo):
    ropeC, ropeS = consts["ropeC"], consts["ropeS"]
    with ExitStack() as ctx:
        def sb(name, shape, dt=F32):
            return ctx.enter_context(nc.sbuf_tensor(f"ca_{name}", shape, dt))

        def ps(name, shape):
            return ctx.enter_context(nc.psum_tensor(f"ca_{name}", shape, F32))

        def sem(name):
            return ctx.enter_context(nc.semaphore(f"ca_{name}"))

        q_hl = sb("q_hl", [P, 2, 2, N], F16)
        raw = sb("raw", [P, 2, N])
        swp = sb("swp", [P, 2, N])
        rot = sb("rot", [P, 2, N])
        hi = sb("hi", [P, N], F16)
        lo = sb("lo", [P, N], F16)
        v_pair = sb("v_pair", [M, 2, P])
        ident = sb("ident", [P, P])
        e = sb("e", [P, 2, 2, TT, M])
        mx = sb("mx", [P, 2, TT])
        total = sb("total", [P, 2, TT])
        inv = sb("inv", [P, 2, 2, TT])
        pT = sb("pT", [M, 2, N])
        o_hi = sb("o_hi", [P, PAIRS, N], F16)
        o_lo = sb("o_lo", [P, PAIRS, N], F16)
        xr = sb("xr", [P, TT, D])
        bo_row = sb("bo_row", [P, 1, D])
        ps_sc = ps("ps_sc", [P, TT, P])
        ps_pt = ps("ps_pt", [P, N])
        ps_o = ps("ps_o", [P, N])
        ps_turn = [ps(f"ps_turn{i}", [P, HALF]) for i in range(2)]
        ps_y = [ps_pt[:, i * HALF:i * HALF + D] for i in range(2)] + [t[:, 0:D] for t in ps_turn]

        s_ident = sem("s_ident")
        s_bo = sem("s_bo")
        s_x = sem("s_x")
        s_xb = sem("s_xb")
        s_swap = [sem(f"s_swap{par}") for par in range(2)]
        s_stack = [sem(f"s_stack{par}") for par in range(2)]
        s_cos = sem("s_cos")
        s_sin = sem("s_sin")
        s_rot = sem("s_rot")
        s_hi = sem("s_hi")
        s_lo = sem("s_lo")
        s_q_w = sem("s_q_w")
        s_q_r = sem("s_q_r")
        s_sc_w = sem("s_sc_w")
        s_sc_r = sem("s_sc_r")
        s_mx = sem("s_mx")
        s_e = sem("s_e")
        s_v = sem("s_v")
        s_total = sem("s_total")
        s_inv = sem("s_inv")
        s_prob0 = sem("s_prob0")
        s_prob1 = sem("s_prob1")
        s_pt_w = sem("s_pt_w")
        s_pt_r = sem("s_pt_r")
        s_pv = sem("s_pv")
        s_ohi = sem("s_ohi")
        s_ot = sem("s_ot")
        s_y = sem("s_y")
        s_yr = sem("s_yr")
        s_out = sem("s_out")
        block = ctx.enter_context(nc.Block())
        x_v = x_src.rearrange("b (t p) d -> b p t d", p=P)
        y_v = x_dst.rearrange("b (t p) d -> b p t d", p=P)

        @block.sync
        def _(sp):
            def swap(j, par):
                sp.wait_ge(s_q_r, 2 * j + 2)
                sp.dma_start(swp[0:P:2, par, :], raw[1:P:2, par, :]).then_inc(s_swap[par], 16)
                sp.dma_start(swp[1:P:2, par, :], raw[0:P:2, par, :]).then_inc(s_swap[par], 16)

            def stack(j, par):
                sp.wait_ge(s_hi, j + 1)
                for x in range(2):
                    sp.dma_start(q_hl[0:DH, par, x, :], hi[DH * x:DH * x + DH, :]).then_inc(s_stack[par], 16)
                sp.wait_ge(s_lo, j + 1)
                for x in range(2):
                    sp.dma_start(q_hl[DH:P, par, x, :], lo[DH * x:DH * x + DH, :]).then_inc(s_stack[par], 16)

            sp.dma_start(bo_row[:, 0, :], bo.partition_broadcast(P)).then_inc(s_bo, 16)
            sp.dma_start(ident[:], consts["identity"]).then_inc(s_ident, 16)
            swap(0, 0)
            swap(1, 1)
            stack(0, 0)
            stack(1, 1)
            swap(2, 0)
            for b in range(B):
                with sp.Fori(0, PAIRS // 2) as pp:
                    for par in range(2):
                        g = b * PAIRS + pp * 2 + par
                        stack(g + 2, par)
                        swap(g + 3, 1 - par)
                if b >= 1:
                    sp.wait_ge(s_out, 16 * b)
                sp.dma_start(xr[:], x_v[b]).then_inc(s_x, 16)
                sp.wait_ge(s_yr, 1 + TT * b + TT)
                sp.dma_start(y_v[b], xr[:]).then_inc(s_out, 16)
            sp.wait_ge(s_out, 16 * B)
            for par in range(2):
                sp.wait_ge(s_swap[par], 32 * (B * PAIRS // 2 + 2 - par))
                sp.wait_ge(s_stack[par], 64 * (B * PAIRS // 2 + 1))

        @block.gpsimd
        def _(pool):
            def rotate(j, par, used=None):
                if used is not None:
                    pool.wait_ge(s_lo, used)
                pool.wait_ge(s_q_r, 2 * j + 2)
                pool.tensor_tensor(rot[:, par, :], raw[:, par, :], ropeC[:, :], ALU.mult).then_inc(s_cos, 1)
                pool.wait_ge(s_swap[par], 32 * (j >> 1) + 32)
                pool.tensor_tensor(swp[:, par, :], swp[:, par, :], ropeS[:, :], ALU.mult).then_inc(s_sin, 1)

            def normalise(j, par):
                pool.wait_ge(s_inv, 2 * j + 2)
                pool.tensor_tensor(e[:, par, 1], e[:, par, 1],
                                   inv[:, par, 1, :].rearrange("p (t a) -> p t a", a=1).broadcast_to([P, TT, M]),
                                   ALU.mult).then_inc(s_prob1, 1)

            def pick_values(j, par):
                b, cols = pair_at(j)
                pool.tensor_copy(v_pair[:, par, :], v_all[:, b, cols]).then_inc(s_v, 1)

            rotate(0, 0)
            rotate(1, 1)
            rotate(2, 0, 1)
            pick_values(0, 0)
            pool.wait_ge(s_bo, 16)
            with pool.Fori(0, B) as b:
                with pool.Fori(0, PAIRS // 2) as pp:
                    for par in range(2):
                        g = b * PAIRS + pp * 2 + par
                        normalise(g, par)
                        pool.wait_ge(s_pv, 1 + g)
                        pick_values(g + 1, 1 - par)
                        rotate(g + 3, 1 - par, g + 2)
                pool.wait_ge(s_x, 16 * b + 16)
                pool.tensor_tensor(xr[:], xr[:], bo_row[:].broadcast_to([P, TT, D]), ALU.add).then_inc(s_xb, 1)

        @block.tensor
        def _(pe):
            def project(j, c):
                b, cols = pair_at(j)
                split_product(pe, ps_turn[c][:, :], range(KD), wq, xT, lambda k: (slice(None), k, cols),
                              lambda k: (slice(None), b, k, slice(c * HALF, (c + 1) * HALF))).then_inc(s_q_w, 1)

            def scores(j, par, x):
                b, pair = (j >> 3) & (B - 1), j & (PAIRS - 1)
                for t in range(TT):
                    ts = slice(t * P, (t + 1) * P)
                    pe.matmul(ps_sc[:, t, 0:M], q_hl[:, par, x, ts], k_hh[:, pair, x, b, :], start=True, stop=False)
                    ins = pe.matmul(ps_sc[:, t, 0:M], q_hl[0:DH, par, x, ts], k_lo[:, pair, x, b, :],
                                    start=False, stop=True)
                ins.then_inc(s_sc_w, 1)

            def transposes(par, x):
                for t in range(TT):
                    ins = pe.transpose(ps_pt[0:M, t * P:(t + 1) * P], e[:, par, x, t, :], ident[:, :])
                ins.then_inc(s_pt_w, 1)

            for j in range(3):
                for c in range(2):
                    if j >= 1:
                        pe.wait_ge(s_q_r, 2 * (j - 1) + c + 1)
                    project(j, c)
            pe.wait_ge(s_stack[0], 64)
            scores(0, 0, 0)
            pe.wait_ge(s_sc_r, 1)
            scores(0, 0, 1)
            pe.wait_ge(s_ident, 16)
            pe.sem_inc(s_pv, 1)

            def values(g, par):
                pe.wait_ge(s_v, g + 1)
                pe.wait_ge(s_ot, 1 + g)
                pe.wait_ge(s_pt_r, 1 + 2 * g + 2)
                for c in range(2):
                    for x in range(2):
                        cs = slice(c * HALF, (c + 1) * HALF)
                        ins = pe.matmul(ps_o[DH * x:DH * x + DH, cs], v_pair[:, par, DH * x:DH * x + DH],
                                        pT[:, x, cs], start=True, stop=True)
                ins.then_inc(s_pv, 1)

            def iteration(b, p, par, first=False):
                g = b * PAIRS + p
                if not first:
                    values(g - 1, 1 - par)
                pe.wait_ge(s_yr, 1 + TT * b)
                pe.wait_ge(s_pt_r, 1 + 2 * g)
                pe.wait_ge(s_prob0, g + 1)
                transposes(par, 0)
                pe.wait_ge(s_q_r, 2 * (g + 2) + 1)
                project(g + 3, 0)
                pe.wait_ge(s_stack[1 - par], 64 * (((g + 1) >> 1) + 1))
                pe.wait_ge(s_sc_r, 2 * (g + 1))
                scores(g + 1, 1 - par, 0)
                pe.wait_ge(s_q_r, 2 * (g + 2) + 2)
                project(g + 3, 1)
                pe.wait_ge(s_pt_r, 1 + 2 * g + 1)
                pe.wait_ge(s_prob1, g + 1)
                transposes(par, 1)
                pe.wait_ge(s_sc_r, 2 * (g + 1) + 1)
                scores(g + 1, 1 - par, 1)

            with pe.Fori(0, B) as b:
                iteration(b, 0, 0, first=True)
                with pe.Fori(0, PAIRS // 2 - 1) as pp:
                    iteration(b, pp * 2 + 1, 1)
                    iteration(b, pp * 2 + 2, 0)
                iteration(b, PAIRS - 1, 1)
                values(b * PAIRS + PAIRS - 1, 1)
                pe.wait_ge(s_q_r, 2 * (b * PAIRS + PAIRS + 2) + 2)
                output_projection(pe, o_hi, o_lo, wo, ps_y, s_y, s_yr, b, s_ot, 1)

        @block.scalar
        def _(act):
            def evacuate(j, par, c):
                act.wait_ge(s_q_w, 2 * j + c + 1)
                act.activation(raw[:, par, c * HALF:(c + 1) * HALF], ps_turn[c][:, :], ACT.Copy,
                               scale=1.0 / WS).then_inc(s_q_r, 1)

            def high(j, par):
                act.wait_ge(s_rot, j + 1)
                act.activation(hi[:], rot[:, par, :], ACT.Copy).then_inc(s_hi, 1)

            def exponentials(j, par, x):
                act.wait_ge(s_sc_r, 2 * j + x + 1)
                act.activation(e[:, par, x], e[:, par, x], ACT.Exp, scale=float(DH) ** -0.5).then_inc(s_e, 1)

            def untranspose(g, x):
                act.wait_ge(s_pt_w, 2 * g + x + 1)
                act.activation(pT[:, x, :], ps_pt[0:M, :], ACT.Copy).then_inc(s_pt_r, 1)

            act.sem_inc(s_pt_r, 1)
            for j in range(2):
                for c in range(2):
                    evacuate(j, j, c)
            high(0, 0)
            act.wait_ge(s_lo, 1)
            for c in range(2):
                evacuate(2, 0, c)
            act.wait_ge(s_stack[0], 64)
            high(1, 1)
            exponentials(0, 0, 0)

            def split_output(g, p):
                act.wait_ge(s_pv, 1 + g + 1)
                act.activation(o_hi[:, p, :], ps_o[:], ACT.Copy).then_inc(s_ohi, 1)

            def iteration(g, p, par, first=False):
                exponentials(g, par, 1)
                if not first:
                    split_output(g - 1, p - 1)
                act.wait_ge(s_stack[1 - par], 64 * (((g + 1) >> 1) + 1))
                high(g + 2, par)
                act.wait_ge(s_pv, 1 + g)
                untranspose(g, 0)
                act.wait_ge(s_lo, g + 2)
                evacuate(g + 3, 1 - par, 0)
                evacuate(g + 3, 1 - par, 1)
                exponentials(g + 1, 1 - par, 0)
                untranspose(g, 1)

            with act.Fori(0, B) as b:
                iteration(b * PAIRS, 0, 0, first=True)
                with act.Fori(0, PAIRS // 2 - 1) as pp:
                    iteration(b * PAIRS + pp * 2 + 1, pp * 2 + 1, 1)
                    iteration(b * PAIRS + pp * 2 + 2, pp * 2 + 2, 0)
                iteration(b * PAIRS + PAIRS - 1, PAIRS - 1, 1)
                split_output(b * PAIRS + PAIRS - 1, PAIRS - 1)

        @block.vector
        def _(dve):
            def rotated(j, par):
                dve.wait_ge(s_sin, j + 1)
                dve.wait_ge(s_cos, j + 1)
                dve.tensor_tensor(rot[:, par, :], rot[:, par, :], swp[:, par, :], ALU.add).then_inc(s_rot, 1)

            def low(j, par):
                dve.wait_ge(s_hi, j + 1)
                dve.tensor_tensor(lo[:], rot[:, par, :], hi[:], ALU.subtract).then_inc(s_lo, 1)

            def shift(j, par, x):
                dve.wait_ge(s_sc_w, 2 * j + x + 1)
                dve.reduce_max(mx[:, x, :], ps_sc[:, :, 0:M], AX_X).then_inc(s_mx, 1)
                dve.wait_ge(s_mx, 2 * j + x + 1)
                dve.tensor_tensor(e[:, par, x], ps_sc[:, :, 0:M],
                                  mx[:, x, :].rearrange("p (t a) -> p t a", a=1).broadcast_to([P, TT, M]),
                                  ALU.subtract).then_inc(s_sc_r, 1)

            def totals(j, par, x):
                dve.wait_ge(s_e, 2 * j + x + 1)
                dve.reduce_sum(total[:, x, :], e[:, par, x], AX_X).then_inc(s_total, 1)
                dve.wait_ge(s_total, 2 * j + x + 1)
                dve.reciprocal(inv[:, par, x, :], total[:, x, :]).then_inc(s_inv, 1)
                if x == 0:
                    dve.wait_ge(s_inv, 2 * j + 1)
                    dve.tensor_tensor(e[:, par, 0], e[:, par, 0],
                                      inv[:, par, 0, :].rearrange("p (t a) -> p t a", a=1).broadcast_to([P, TT, M]),
                                      ALU.mult).then_inc(s_prob0, 1)

            dve.sem_inc(s_ot, 1)
            dve.sem_inc(s_yr, 1)
            for j in range(2):
                rotated(j, j)
                if j == 1:
                    dve.wait_ge(s_stack[0], 64)
                low(j, j)
            shift(0, 0, 0)
            totals(0, 0, 0)

            def split_output(g, p):
                dve.wait_ge(s_ohi, g + 1)
                dve.tensor_tensor(o_lo[:, p, :], ps_o[:], o_hi[:, p, :], ALU.subtract).then_inc(s_ot, 1)

            def iteration(g, p, par, first=False):
                shift(g, par, 1)
                totals(g, par, 1)
                rotated(g + 2, par)
                if not first:
                    split_output(g - 1, p - 1)
                dve.wait_ge(s_stack[1 - par], 64 * (((g + 1) >> 1) + 1))
                low(g + 2, par)
                shift(g + 1, 1 - par, 0)
                totals(g + 1, 1 - par, 0)

            with dve.Fori(0, B) as b:
                iteration(b * PAIRS, 0, 0, first=True)
                with dve.Fori(0, PAIRS // 2 - 1) as pp:
                    iteration(b * PAIRS + pp * 2 + 1, pp * 2 + 1, 1)
                    iteration(b * PAIRS + pp * 2 + 2, pp * 2 + 2, 0)
                iteration(b * PAIRS + PAIRS - 1, PAIRS - 1, 1)
                split_output(b * PAIRS + PAIRS - 1, PAIRS - 1)
                dve.wait_ge(s_xb, b + 1)
                for t in range(TT):
                    dve.wait_ge(s_y, TT * b + t + 1)
                    dve.scalar_tensor_tensor(out=xr[:, t, :], in0=ps_y[t % 4], scalar=1.0 / WS, in1=xr[:, t, :],
                                             op0=ALU.mult, op1=ALU.add).then_inc(s_yr, 1)


def feed_forward(nc, tag, x_src, x_dst, b1, b2, xT, w1, w2):
    with ExitStack() as ctx:
        def sb(name, shape, dt=F32):
            return ctx.enter_context(nc.sbuf_tensor(f"{tag}_{name}", shape, dt))

        def sem(name):
            return ctx.enter_context(nc.semaphore(f"{tag}_{name}"))

        hid = sb("hid", [P, 2, N])
        h_hi = sb("h_hi", [P, KM, N], F16)
        h_lo = sb("h_lo", [P, KM, N], F16)
        xr = sb("xr", [P, 2, TT, D])
        b1_col = sb("b1_col", [P, KM])
        b2_row = sb("b2_row", [P, 1, D])
        ps_h = [ctx.enter_context(nc.psum_tensor(f"{tag}_ps_h{i}", [P, N], F32)) for i in range(2)]
        ps_y = [ctx.enter_context(nc.psum_tensor(f"{tag}_ps_y{i}", [P, HALF], F32)) for i in range(4)]
        s_b = sem("s_b")
        s_x = [sem("s_x0"), sem("s_x1")]
        s_xb = sem("s_xb")
        s_h = sem("s_h")
        s_g = sem("s_g")
        s_hi = sem("s_hi")
        s_lo = sem("s_lo")
        s_y = sem("s_y")
        s_yr = sem("s_yr")
        s_out = sem("s_out")
        block = ctx.enter_context(nc.Block())
        x_v = x_src.rearrange("b (t p) d -> b p t d", p=P)
        y_v = x_dst.rearrange("b (t p) d -> b p t d", p=P)

        @block.sync
        def _(sp):
            sp.dma_start(b1_col[:], b1.rearrange("(k p) -> p k", p=P),
                         allow_slow_non_contiguous=True).then_inc(s_b, 16)
            sp.dma_start(b2_row[:, 0, :], b2.partition_broadcast(P)).then_inc(s_b, 16)
            sp.dma_start(xr[:, 0], x_v[0]).then_inc(s_x[0], 16)
            for b in range(B):
                if b + 1 < B:
                    if b >= 1:
                        sp.wait_ge(s_out, 16 * b)
                    sp.dma_start(xr[:, 1 - b % 2], x_v[b + 1]).then_inc(s_x[1 - b % 2], 16)
                sp.wait_ge(s_yr, 1 + TT * b + TT)
                sp.dma_start(y_v[b], xr[:, b % 2]).then_inc(s_out, 16)
            sp.wait_ge(s_out, 16 * B)

        @block.tensor
        def _(pe):
            with pe.Fori(0, B) as b:
                for m in range(KM):
                    n = KM * b + m
                    if m >= 2:
                        pe.wait_ge(s_g, 1 + n - 1)
                    else:
                        pe.wait_ge(s_g, 1 + KM * b)
                    for c in range(2):
                        cs, ms = slice(c * HALF, (c + 1) * HALF), slice(m * P, (m + 1) * P)
                        ins = split_product(pe, ps_h[m % 2][:, cs], range(KD), w1, xT, lambda k, ms=ms: (slice(None), k, ms),
                                            lambda k, cs=cs: (slice(None), b, k, cs))
                    ins.then_inc(s_h, 1)
                pe.wait_ge(s_yr, 1 + TT * b)
                output_projection(pe, h_hi, h_lo, w2, [t[:, 0:D] for t in ps_y], s_y, s_yr, b, s_lo, 1)

        @block.scalar
        def _(act):
            act.sem_inc(s_g, 1)
            act.wait_ge(s_b, 32)
            with act.Fori(0, B) as b:
                for m in range(KM):
                    act.wait_ge(s_h, KM * b + m + 1)
                    if m >= 2:
                        act.wait_ge(s_lo, 1 + KM * b + m - 1)
                    act.activation(hid[:, m % 2, :], ps_h[m % 2][:, :], ACT.Gelu, bias=b1_col[:, m:m + 1],
                                   scale=1.0 / WS).then_inc(s_g, 1)

        @block.vector
        def _(dve):
            dve.sem_inc(s_yr, 1)
            dve.sem_inc(s_lo, 1)
            dve.wait_ge(s_b, 32)
            with dve.Fori(0, B // 2) as bb:
                for par in range(2):
                    b = bb * 2 + par
                    dve.wait_ge(s_x[par], 16 * bb + 16)
                    dve.tensor_tensor(xr[:, par], xr[:, par], b2_row[:].broadcast_to([P, TT, D]),
                                      ALU.add).then_inc(s_xb, 1)
                    for m in range(KM):
                        n = KM * b + m + 1
                        dve.wait_ge(s_g, 1 + n)
                        dve.tensor_copy(h_hi[:, m, :], hid[:, m % 2, :]).then_inc(s_hi, 1)
                        dve.wait_ge(s_hi, n)
                        dve.tensor_tensor(h_lo[:, m, :], hid[:, m % 2, :], h_hi[:, m, :],
                                          ALU.subtract).then_inc(s_lo, 1)
                    dve.wait_ge(s_xb, b + 1)
                    for t in range(TT):
                        dve.wait_ge(s_y, TT * b + t + 1)
                        dve.scalar_tensor_tensor(out=xr[:, par, t, :], in0=ps_y[t % 4][:, 0:D], scalar=1.0 / WS,
                                                 in1=xr[:, par, t, :], op0=ALU.mult, op1=ALU.add).then_inc(s_yr, 1)


def load_constants(nc, consts, cosines, sines):
    with ExitStack() as ctx:
        ident = ctx.enter_context(nc.sbuf_tensor("const_ident", [P, P], F32))
        s_load = ctx.enter_context(nc.semaphore("const_load"))
        s_made = ctx.enter_context(nc.semaphore("const_made"))
        block = ctx.enter_context(nc.Block())

        @block.sync
        def _(sp):
            sp.dma_start(ident[:], consts["identity"]).then_inc(s_load, 16)
            sp.dma_start(consts["ropeC"][:], cosines).then_inc(s_load, 16)
            sp.dma_start(consts["ropeS"][:], sines).then_inc(s_load, 16)
            sp.wait_ge(s_load, 48)

        @block.vector
        def _(dve):
            dve.memset(consts["ones32"][:], 1.0).then_inc(s_made, 1)
            dve.wait_ge(s_load, 48)
            dve.tensor_copy(consts["ident16"][:], ident[:]).then_inc(s_made, 1)


def program(nc, a, identity, cosines, sines, out):
    with ExitStack() as top:
        def keep(name, shape, dt=F32):
            return top.enter_context(nc.sbuf_tensor(name, shape, dt))

        consts = {"identity": identity, "ident16": keep("ident16", [P, P], F16),
                  "ropeC": keep("ropeC", [P, N]), "ropeS": keep("ropeS", [P, N]), "ones32": keep("ones32", [P, DH])}
        x1 = nc.dram_tensor("x_after_self", (B, N, D), F32, kind="Internal").ap()
        x2 = nc.dram_tensor("x_after_cross", (B, N, D), F32, kind="Internal").ap()
        xT = (keep("xT_hi", [P, B, KD, N], F16), keep("xT_lo", [P, B, KD, N], F16))
        load_constants(nc, consts, cosines, sines)

        def units(src, pair, width):
            hi, lo = pair
            rows = src.shape[0]
            if width == N:
                return [(src[k * P:min(rows, (k + 1) * P), :], hi[:, k, :], lo[:, k, :]) for k in range(-(-rows // P))]
            n = N // width
            return [(src[k * P:(k + n) * P, :].rearrange("(k p) n -> p k n", p=P),
                     hi[:, k:k + n, :].rearrange("p k n -> p (k n)"), lo[:, k:k + n, :].rearrange("p k n -> p (k n)"))
                    for k in range(0, rows // P, n)]

        def split_pair(ctx, name, k, width):
            return tuple(ctx.enter_context(nc.sbuf_tensor(f"{name}_{part}", [P, k, width], F16)) for part in ("hi", "lo"))

        norm1 = [a[n] for n in ("ln1_w", "ln1_b", "g1_w", "g1_b", "b1_w", "b1_b")]
        norm2 = [a[n] for n in ("ln2_w", "ln2_b", "g2_w", "g2_b", "b2_w", "b2_b")]
        for tag, src in (("sa", a["x"]), ("ca", x1)):
            with ExitStack() as ctx:
                wq, wo = split_pair(ctx, f"{tag}_wq", KD, MID), split_pair(ctx, f"{tag}_wo", KM, D)
                wk, wv = (split_pair(ctx, f"{tag}_{n}", KD, MID) for n in ("wk", "wv"))
                wkv = a[f"{tag}_wkv"]
                pieces = units(a[f"{tag}_wq"], wq, MID) + units(wkv[:, 0:MID], wk, MID)
                pieces += units(wkv[:, MID:2 * MID], wv, MID) + units(a[f"{tag}_wo"], wo, D)
                if tag == "sa":
                    prepare(nc, "sap", consts, src, a["cond_1024"], norm1, pieces, *xT)
                    self_attention(nc, consts, src, x1, a["sa_bo"], xT, wq, wk, wv, wo)
                else:
                    cT = tuple(ctx.enter_context(nc.sbuf_tensor(f"cT_{part}", [P, B, KD, M], F16))
                               for part in ("hi", "lo"))
                    prepare(nc, "cap", consts, src, a["cond_1024"], norm1, pieces, *xT,
                            context=(a["ctx_768"], a["ca_lnc_w"], a["ca_lnc_b"], *cT))
                    k_hh, k_lo = (ctx.enter_context(nc.sbuf_tensor(n, [rows, PAIRS, 2, B, M], F16))
                                  for n, rows in (("k_hh", P), ("k_lo", DH)))
                    v_all = ctx.enter_context(nc.sbuf_tensor("v_all", [M, B, MID], F32))
                    project_context(nc, consts, cT, wk, wv, k_hh, k_lo, v_all)
                    cross_attention(nc, consts, src, x2, a["ca_bo"], xT, k_hh, k_lo, v_all, wq, wo)
        with ExitStack() as ctx:
            w1 = split_pair(ctx, "w1", KD, HID)
            w2 = split_pair(ctx, "w2", KM, D)
            pieces = units(a["ff_w1"], w1, HID) + units(a["ff_w2"], w2, D)
            prepare(nc, "ffp", consts, x2, a["cond_1024"], norm2, pieces, *xT)
            feed_forward(nc, "ff", x2, out, a["ff_b1"], a["ff_b2"], xT, w1, w2)


def rope_tables():
    inv = (np.float32(1.0) / np.float32(10000.0) ** (np.arange(0, DH, 2, dtype=np.float32) / np.float32(DH)))
    ang = inv.astype(np.float32)[:, None] * np.arange(N, dtype=np.float32)[None, :]
    rows = np.arange(P) % DH // 2
    sign = np.where(np.arange(P) % 2 == 0, -1.0, 1.0).astype(np.float32)[:, None]
    return np.cos(ang)[rows].astype(np.float32), (np.sin(ang)[rows] * sign).astype(np.float32)


def kernel(**inputs):
    from concourse import bacc
    from concourse.bass_utils import run_bass_kernel_spmd

    nc = bacc.Bacc("TRN2", target_bir_lowering=False, num_devices=1)
    cosines, sines = rope_tables()
    arrays = {name: np.ascontiguousarray(v) for name, v in inputs.items()}
    arrays |= {"identity": np.eye(P, dtype=np.float32), "rope_cos": cosines, "rope_sin": sines}
    aps = {name: nc.dram_tensor(f"in_{name}", v.shape, mybir.dt.from_np(v.dtype), kind="ExternalInput").ap()
           for name, v in arrays.items()}
    out = nc.dram_tensor("out_x", (B, N, D), F32, kind="ExternalOutput").ap()
    a = {name.removeprefix("L0_xcond_"): ap for name, ap in aps.items()}
    program(nc, a, aps["identity"], aps["rope_cos"], aps["rope_sin"], out)
    r = run_bass_kernel_spmd(nc, [{f"in_{name}": v for name, v in arrays.items()}], core_ids=[0])
    return r.results[0]["out_x"]
```
